# Optimizing a Trainium2 kernel written in Bass

```python
import numpy as np
import jax
import jax.numpy as jnp

def _softmax(x, axis=-1):
    return jax.nn.softmax(x, axis=axis)

def _gelu(x):
    return jax.nn.gelu(x, approximate=True)

def _silu(x):
    return jax.nn.silu(x)

def _sigmoid(x):
    return jax.nn.sigmoid(x)

def _layernorm(x, axis=-1, eps=1e-05):
    m = jnp.mean(x, axis=axis, keepdims=True)
    v = jnp.var(x, axis=axis, keepdims=True)
    return (x - m) / jnp.sqrt(v + eps)

def _scatter_add(tgt, idx, src, axis=0):
    return tgt.at[idx].add(src)

def _segment_sum(src, seg, n):
    return jax.ops.segment_sum(src, seg, n)
kernel_name = 'mk_gnn_preln_d4_gnn_r8_ae4283'

def setup_inputs(seed: int=0):
    np.random.seed(seed)
    _w = jnp.asarray

    def _rec_inputs():
        import jax
        import jax.numpy as jnp
        _gk = jax.random.key(seed)
        x = -0.0003713 + 1 * jax.random.normal(jax.random.fold_in(_gk, 1), (6250, 128), jnp.float32)
        src = jax.random.randint(jax.random.fold_in(_gk, 2), (100000,), 0, 6250, jnp.int32)
        dst = jnp.minimum((6250 * jax.random.uniform(jax.random.fold_in(_gk, 3), (100000,)) ** 2.0).astype(jnp.int32), 49999)
        _o = jnp.argsort(dst, stable=True)
        src = src[_o]
        dst = dst[_o]
        edge_type_4 = jax.random.randint(jax.random.fold_in(_gk, 13), (100000,), 0, 4, jnp.int32)
        return (x, src, dst, edge_type_4)
    x, src, dst, edge_type_4 = _rec_inputs()

    def _L0_gnn_setup():
        import jax, jax.numpy as jnp
        import numpy as np
        N_NODES = 12500
        IN_DIM = 128
        HIDDEN = 128

        def _sage_conv(x, src, dst, Wl, b, Wr, n_nodes):
            msgs = x[src]
            agg = jax.ops.segment_sum(msgs, dst, num_segments=n_nodes)
            cnt = jax.ops.segment_sum(jnp.ones((src.shape[0], 1), x.dtype), dst, num_segments=n_nodes)
            agg = agg / jnp.maximum(cnt, 1.0)
            return agg @ Wl.T + b + x @ Wr.T
        key = jax.random.key(seed)
        ks = jax.random.split(key, 8)
        x = jax.random.normal(ks[0], (N_NODES, IN_DIM), dtype=jnp.float32)
        edge_index = jax.random.randint(ks[1], (2, 75000), 0, N_NODES, dtype=jnp.int64)
        s = 1.0 / np.sqrt(IN_DIM)
        sh = 1.0 / np.sqrt(HIDDEN)
        return {'x': x, 'edge_index': edge_index, 'W1l': jax.random.uniform(ks[2], (HIDDEN, IN_DIM), jnp.float32, -s, s), 'b1': jnp.zeros((HIDDEN,), jnp.float32), 'W1r': jax.random.uniform(ks[3], (HIDDEN, IN_DIM), jnp.float32, -s, s), 'W2l': jax.random.uniform(ks[4], (HIDDEN, HIDDEN), jnp.float32, -sh, sh), 'b2': jnp.zeros((HIDDEN,), jnp.float32), 'W2r': jax.random.uniform(ks[5], (HIDDEN, HIDDEN), jnp.float32, -sh, sh)}
    _L0_gnn_all = _L0_gnn_setup()
    _L0_gnn_in = {k: v for k, v in _L0_gnn_all.items() if k in ('W1l', 'b1', 'W1r', 'W2l', 'b2', 'W2r')}
    del _L0_gnn_all

    def _L1_gnn_setup():
        import jax, jax.numpy as jnp
        import numpy as np
        N, E, D, H, C, FF = (1250, 40000, 128, 4, 128, 512)
        EPS_BN = 1e-05

        def _batchnorm(v, w, b):
            mu = v.mean(0)
            var = v.var(0)
            return (v - mu) * jax.lax.rsqrt(var + EPS_BN) * w + b

        def _gat(h, edge_index, W, att_src, att_dst, bias):
            n = h.shape[0]
            loops = jnp.arange(n, dtype=edge_index.dtype)
            src = jnp.concatenate([edge_index[0], loops])
            dst = jnp.concatenate([edge_index[1], loops])
            x = (h @ W).reshape(n, H, C)
            a_src = (x * att_src).sum(-1)
            a_dst = (x * att_dst).sum(-1)
            e = jax.nn.leaky_relu(a_src[src] + a_dst[dst], 0.2)
            m = jax.ops.segment_max(e, dst, num_segments=n)
            e = jnp.exp(e - m[dst])
            denom = jax.ops.segment_sum(e, dst, num_segments=n)
            alpha = e / denom[dst]
            msg = x[src] * alpha[..., None]
            out = jax.ops.segment_sum(msg, dst, num_segments=n)
            return out.mean(1) + bias
        key = jax.random.key(seed)
        ks = jax.random.split(key, 16)
        sd = 1.0 / np.sqrt(D)
        sf = 1.0 / np.sqrt(FF)
        return {'h': jax.random.normal(ks[0], (N, D), dtype=jnp.float32), 'edge_index': jax.random.randint(ks[1], (2, E), 0, N, dtype=jnp.int32), 'W': jax.random.uniform(ks[2], (D, H * C), jnp.float32, -sd, sd), 'att_src': jax.random.uniform(ks[3], (H, C), jnp.float32, -sd, sd), 'att_dst': jax.random.uniform(ks[4], (H, C), jnp.float32, -sd, sd), 'bias': jnp.zeros((C,), jnp.float32), 'bn1_w': jnp.ones((D,), jnp.float32), 'bn1_b': jnp.zeros((D,), jnp.float32), 'W1': jax.random.uniform(ks[5], (D, FF), jnp.float32, -sd, sd), 'b1': jax.random.uniform(ks[6], (FF,), jnp.float32, -sf, sf), 'W2': jax.random.uniform(ks[7], (FF, D), jnp.float32, -sf, sf), 'b2': jax.random.uniform(ks[8], (D,), jnp.float32, -sd, sd), 'bn2_w': jnp.ones((D,), jnp.float32), 'bn2_b': jnp.zeros((D,), jnp.float32)}
    _L1_gnn_all = _L1_gnn_setup()
    _L1_gnn_in = {k: v for k, v in _L1_gnn_all.items() if k in ('W', 'att_src', 'att_dst', 'bias', 'bn1_w', 'bn1_b', 'W1', 'b1', 'W2', 'b2', 'bn2_w', 'bn2_b')}
    del _L1_gnn_all

    def _L2_gnn_setup():
        import jax, jax.numpy as jnp
        import numpy as np
        N_NODES = 6250
        N_EDGES = 100000
        HEADS = 2
        HID = 64
        NEG_SLOPE = 0.2

        def gat_prelu(x, W_src, W_dst, att_src, att_dst, bias, prelu_w, edge_index):
            N = x.shape[0]
            src, dst = (edge_index[0], edge_index[1])
            xs = (x @ W_src).reshape(N, HEADS, HID)
            xd = (x @ W_dst).reshape(N, HEADS, HID)
            a_src = jnp.einsum('nhc,hc->nh', xs, att_src)
            a_dst = jnp.einsum('nhc,hc->nh', xd, att_dst)
            e = jax.nn.leaky_relu(a_src[src] + a_dst[dst], NEG_SLOPE)
            m = jax.ops.segment_max(e, dst, num_segments=N)
            ee = jnp.exp(e - m[dst])
            denom = jax.ops.segment_sum(ee, dst, num_segments=N)
            alpha = ee / (denom[dst] + 1e-16)
            msg = xs[src] * alpha[:, :, None]
            out = jax.ops.segment_sum(msg, dst, num_segments=N)
            out = out.reshape(N, HEADS * HID) + bias
            return jnp.where(out >= 0, out, prelu_w * out)
        key = jax.random.key(seed)
        ks = jax.random.split(key, 8)
        x = jax.random.normal(ks[0], (N_NODES, 128), dtype=jnp.float32)
        W_src = jax.random.normal(ks[1], (128, HEADS * HID), dtype=jnp.float32) * (1.0 / np.sqrt(128))
        W_dst = jax.random.normal(ks[2], (128, HEADS * HID), dtype=jnp.float32) * (1.0 / np.sqrt(128))
        att_src = jax.random.normal(ks[3], (HEADS, HID), dtype=jnp.float32) * 0.1
        att_dst = jax.random.normal(ks[4], (HEADS, HID), dtype=jnp.float32) * 0.1
        bias = jax.random.normal(ks[5], (HEADS * HID,), dtype=jnp.float32) * 0.01
        prelu_w = jnp.full((HEADS * HID,), 0.25, dtype=jnp.float32)
        edge_index = jax.random.randint(ks[6], (2, N_EDGES), 0, N_NODES, dtype=jnp.int64)
        return {'x': x, 'W_src': W_src, 'W_dst': W_dst, 'att_src': att_src, 'att_dst': att_dst, 'bias': bias, 'prelu_w': prelu_w, 'edge_index': edge_index}
    _L2_gnn_all = _L2_gnn_setup()
    _L2_gnn_in = {k: v for k, v in _L2_gnn_all.items() if k in ('W_src', 'W_dst', 'att_src', 'att_dst', 'bias', 'prelu_w')}
    del _L2_gnn_all

    def _L3_gnn_setup():
        import jax, jax.numpy as jnp
        import numpy as np
        N, E, IN, OUT = (6250, 100000, 128, 128)
        R = 5
        key = jax.random.key(seed)
        k = jax.random.split(key, 6)
        x = jax.random.normal(k[0], (N, IN), jnp.float32)
        src = jax.random.randint(k[1], (E,), 0, N)
        dst = jax.random.randint(k[2], (E,), 0, N)
        rel = jax.random.randint(k[3], (E,), 0, R - 1)
        xavier = np.sqrt(2.0) * np.sqrt(6.0 / (IN + OUT))
        weight = jax.random.uniform(k[4], (R, IN, OUT), jnp.float32, -xavier, xavier)
        bias = jax.random.uniform(k[5], (R, OUT), jnp.float32, -xavier, xavier)
        return dict(x=x, weight=weight, bias=bias, src=src, dst=dst, rel=rel)
    _L3_gnn_all = _L3_gnn_setup()
    _L3_gnn_in = {k: v for k, v in _L3_gnn_all.items() if k in ('weight', 'bias')}
    del _L3_gnn_all
    return {'x': x, 'src': src, 'dst': dst, 'edge_type_4': edge_type_4, 'L0_gnn_W1l': _L0_gnn_in['W1l'], 'L0_gnn_b1': _L0_gnn_in['b1'], 'L0_gnn_W1r': _L0_gnn_in['W1r'], 'L0_gnn_W2l': _L0_gnn_in['W2l'], 'L0_gnn_b2': _L0_gnn_in['b2'], 'L0_gnn_W2r': _L0_gnn_in['W2r'], 'L1_gnn_W': _L1_gnn_in['W'], 'L1_gnn_att_src': _L1_gnn_in['att_src'], 'L1_gnn_att_dst': _L1_gnn_in['att_dst'], 'L1_gnn_bias': _L1_gnn_in['bias'], 'L1_gnn_bn1_w': _L1_gnn_in['bn1_w'], 'L1_gnn_bn1_b': _L1_gnn_in['bn1_b'], 'L1_gnn_W1': _L1_gnn_in['W1'], 'L1_gnn_b1': _L1_gnn_in['b1'], 'L1_gnn_W2': _L1_gnn_in['W2'], 'L1_gnn_b2': _L1_gnn_in['b2'], 'L1_gnn_bn2_w': _L1_gnn_in['bn2_w'], 'L1_gnn_bn2_b': _L1_gnn_in['bn2_b'], 'L2_gnn_W_src': _L2_gnn_in['W_src'], 'L2_gnn_W_dst': _L2_gnn_in['W_dst'], 'L2_gnn_att_src': _L2_gnn_in['att_src'], 'L2_gnn_att_dst': _L2_gnn_in['att_dst'], 'L2_gnn_bias': _L2_gnn_in['bias'], 'L2_gnn_prelu_w': _L2_gnn_in['prelu_w'], 'L3_gnn_weight': _L3_gnn_in['weight'], 'L3_gnn_bias': _L3_gnn_in['bias']}

def reference(x, src, dst, edge_type_4, L0_gnn_W1l, L0_gnn_b1, L0_gnn_W1r, L0_gnn_W2l, L0_gnn_b2, L0_gnn_W2r, L1_gnn_W, L1_gnn_att_src, L1_gnn_att_dst, L1_gnn_bias, L1_gnn_bn1_w, L1_gnn_bn1_b, L1_gnn_W1, L1_gnn_b1, L1_gnn_W2, L1_gnn_b2, L1_gnn_bn2_w, L1_gnn_bn2_b, L2_gnn_W_src, L2_gnn_W_dst, L2_gnn_att_src, L2_gnn_att_dst, L2_gnn_bias, L2_gnn_prelu_w, L3_gnn_weight, L3_gnn_bias):
    import jax
    import jax.numpy as jnp

    def _L0_gnn_ref(x, edge_index, W1l, b1, W1r, W2l, b2, W2r):
        import jax, jax.numpy as jnp
        import numpy as np
        N_NODES = 12500
        IN_DIM = 128
        HIDDEN = 128

        def _sage_conv(x, src, dst, Wl, b, Wr, n_nodes):
            msgs = x[src]
            agg = jax.ops.segment_sum(msgs, dst, num_segments=n_nodes)
            cnt = jax.ops.segment_sum(jnp.ones((src.shape[0], 1), x.dtype), dst, num_segments=n_nodes)
            agg = agg / jnp.maximum(cnt, 1.0)
            return agg @ Wl.T + b + x @ Wr.T
        n = x.shape[0]
        src, dst = (edge_index[0], edge_index[1])
        h = _sage_conv(x, src, dst, W1l, b1, W1r, n)
        h = jax.nn.elu(h)
        h = _sage_conv(h, src, dst, W2l, b2, W2r, n)
        h = jax.nn.elu(h)
        return jax.nn.log_softmax(h, axis=-1)

    def _L1_gnn_ref(h, edge_index, W, att_src, att_dst, bias, bn1_w, bn1_b, W1, b1, W2, b2, bn2_w, bn2_b):
        import jax, jax.numpy as jnp
        import numpy as np
        N, E, D, H, C, FF = (1250, 40000, 128, 4, 128, 512)
        EPS_BN = 1e-05

        def _batchnorm(v, w, b):
            mu = v.mean(0)
            var = v.var(0)
            return (v - mu) * jax.lax.rsqrt(var + EPS_BN) * w + b

        def _gat(h, edge_index, W, att_src, att_dst, bias):
            n = h.shape[0]
            loops = jnp.arange(n, dtype=edge_index.dtype)
            src = jnp.concatenate([edge_index[0], loops])
            dst = jnp.concatenate([edge_index[1], loops])
            x = (h @ W).reshape(n, H, C)
            a_src = (x * att_src).sum(-1)
            a_dst = (x * att_dst).sum(-1)
            e = jax.nn.leaky_relu(a_src[src] + a_dst[dst], 0.2)
            m = jax.ops.segment_max(e, dst, num_segments=n)
            e = jnp.exp(e - m[dst])
            denom = jax.ops.segment_sum(e, dst, num_segments=n)
            alpha = e / denom[dst]
            msg = x[src] * alpha[..., None]
            out = jax.ops.segment_sum(msg, dst, num_segments=n)
            return out.mean(1) + bias
        h1 = h + _gat(h, edge_index, W, att_src, att_dst, bias)
        h1 = _batchnorm(h1, bn1_w, bn1_b)
        ff = jax.nn.relu(h1 @ W1 + b1) @ W2 + b2
        h2 = _batchnorm(h1 + ff, bn2_w, bn2_b)
        return h2

    def _L2_gnn_ref(x, W_src, W_dst, att_src, att_dst, bias, prelu_w, edge_index):
        import jax, jax.numpy as jnp
        import numpy as np
        N_NODES = 6250
        N_EDGES = 100000
        HEADS = 2
        HID = 64
        NEG_SLOPE = 0.2

        def gat_prelu(x, W_src, W_dst, att_src, att_dst, bias, prelu_w, edge_index):
            N = x.shape[0]
            src, dst = (edge_index[0], edge_index[1])
            xs = (x @ W_src).reshape(N, HEADS, HID)
            xd = (x @ W_dst).reshape(N, HEADS, HID)
            a_src = jnp.einsum('nhc,hc->nh', xs, att_src)
            a_dst = jnp.einsum('nhc,hc->nh', xd, att_dst)
            e = jax.nn.leaky_relu(a_src[src] + a_dst[dst], NEG_SLOPE)
            m = jax.ops.segment_max(e, dst, num_segments=N)
            ee = jnp.exp(e - m[dst])
            denom = jax.ops.segment_sum(ee, dst, num_segments=N)
            alpha = ee / (denom[dst] + 1e-16)
            msg = xs[src] * alpha[:, :, None]
            out = jax.ops.segment_sum(msg, dst, num_segments=N)
            out = out.reshape(N, HEADS * HID) + bias
            return jnp.where(out >= 0, out, prelu_w * out)
        return gat_prelu(x, W_src, W_dst, att_src, att_dst, bias, prelu_w, edge_index)

    def _L3_gnn_ref(x, weight, bias, src, dst, rel):
        import jax, jax.numpy as jnp
        import numpy as np
        N, E, IN, OUT = (6250, 100000, 128, 128)
        R = 5
        num_nodes = x.shape[0]
        num_edge_rels = weight.shape[0] - 1
        x_src = x[src]
        msg = jnp.zeros((src.shape[0], weight.shape[2]), x.dtype)
        for r in range(num_edge_rels):
            hr = x_src @ weight[r] + bias[r]
            msg = jnp.where((rel == r)[:, None], hr, msg)
        agg = jax.ops.segment_max(msg, dst, num_segments=num_nodes)
        deg = jax.ops.segment_sum(jnp.ones_like(dst, jnp.float32), dst, num_segments=num_nodes)
        agg = jnp.where((deg > 0)[:, None], agg, jnp.zeros((), x.dtype))
        h = x @ weight[-1] + bias[-1] + agg
        return h
    edge_index = jnp.stack([src, dst])
    h = jnp.maximum(_layernorm(x, axis=-1), 0.0)
    x = x + _L0_gnn_ref(h, edge_index, L0_gnn_W1l, L0_gnn_b1, L0_gnn_W1r, L0_gnn_W2l, L0_gnn_b2, L0_gnn_W2r)
    h = jnp.maximum(_layernorm(x, axis=-1), 0.0)
    x = x + _L1_gnn_ref(h, edge_index, L1_gnn_W, L1_gnn_att_src, L1_gnn_att_dst, L1_gnn_bias, L1_gnn_bn1_w, L1_gnn_bn1_b, L1_gnn_W1, L1_gnn_b1, L1_gnn_W2, L1_gnn_b2, L1_gnn_bn2_w, L1_gnn_bn2_b)
    h = jnp.maximum(_layernorm(x, axis=-1), 0.0)
    x = x + _L2_gnn_ref(h, L2_gnn_W_src, L2_gnn_W_dst, L2_gnn_att_src, L2_gnn_att_dst, L2_gnn_bias, L2_gnn_prelu_w, edge_index)
    h = jnp.maximum(_layernorm(x, axis=-1), 0.0)
    x = x + _L3_gnn_ref(h, L3_gnn_weight, L3_gnn_bias, src, dst, edge_type_4)
    return x

_drawn_inputs = setup_inputs


def setup_inputs(seed=0):
    import zlib

    import numpy as np

    out = dict(_drawn_inputs(seed))
    spreads = {'L0_gnn_b1': (0.0, 0.288),
     'L0_gnn_b2': (0.0, 0.1),
     'L1_gnn_bias': (0.0, 2.0),
     'L1_gnn_bn1_w': (1.0, 0.6),
     'L1_gnn_bn1_b': (0.0, 0.8),
     'L1_gnn_bn2_w': (1.0, 0.2),
     'L1_gnn_bn2_b': (0.0, 0.268),
     'L2_gnn_prelu_w': (0.25, 0.6)}
    factors = {'L1_gnn_att_src': 8.0,
     'L1_gnn_att_dst': 45.864,
     'L1_gnn_b1': 22.883,
     'L1_gnn_b2': 64.0,
     'L2_gnn_W_dst': 7.518,
     'L2_gnn_att_src': 2.753,
     'L2_gnn_att_dst': 7.325,
     'L2_gnn_bias': 8.0}
    for name, (base, spread) in spreads.items():
        noise = np.random.default_rng([zlib.crc32(name.encode()), seed]).standard_normal(out[name].shape)
        drawn = base * np.exp(spread * noise) if base else spread * noise
        out[name] = jnp.asarray(drawn.astype(out[name].dtype))
    for name, factor in factors.items():
        out[name] = (out[name] * factor).astype(out[name].dtype)
    return out
```

```python
import numpy as np
import concourse.bass as bass
from concourse import mybir
from contextlib import ExitStack

F32 = mybir.dt.float32
BF16 = mybir.dt.bfloat16
I32 = mybir.dt.int32
ALU = mybir.AluOpType
ACT = mybir.ActivationFunctionType
AX = mybir.AxisListType

P = 128
N, D, E = 6250, 128, 100000
NT = -(-N // P)
NP = NT * P
NG = 7
NL = N - (NT - 1) * P
TQ = 7
EC = TQ * P
ER = -(-E // EC)
EP = ER * EC
ET = EP // P
CT = 4
CE = CT * P
NB = 4
CHUNKS = ET // CT
ITERS = CHUNKS // NB
H1, H2, R = 4, 2, 4
FF = 512
HI = -(-NT // 2)
BIG = 3.0e38
LN_EPS = 1e-5
SKIP = EP + 1024


class Chain:

    def __init__(self, sem):
        self.sem, self.n = sem, 0

    def __call__(self, engine, ins):
        self.n += 1
        ins.then_inc(self.sem, 1)
        engine.wait_ge(self.sem, self.n)


class Count:

    def __init__(self, sem, ahead=0):
        self.sem, self.base, self.ahead = sem, 0, ahead

    def past(self, n):
        return n + (self.base + self.ahead)

    def by_last_lap(self, n):
        return n + self.base


def build(nc, a, out):
    assert NT % NG == 0 and ET % CT == 0 and CHUNKS % NB == 0
    groups = NT // NG
    with ExitStack() as ctx:
        def sb(name, shape, dt=F32):
            return ctx.enter_context(nc.sbuf_tensor(name, shape, dt))

        def count(name, ahead=0):
            return Count(ctx.enter_context(nc.semaphore(name)), ahead)

        def dram(name, shape, dt=F32):
            return nc.dram_tensor(name, shape, dt).ap()

        h_tab = dram("h_tab", [NP, D])
        x1_tab = dram("x1_tab", [NP, H1 * D])
        y_tab = dram("y_tab", [R * NP, D])
        scan_rows = dram("scan_rows", [EP + P, D])
        start1_rows = dram("start1_rows", [EP, 2 * H1])
        start2_rows = dram("start2_rows", [EP, H2])
        self_rows = dram("self_rows", [EP + P, H1])
        keep_row = dram("keep_row", [1, EP], BF16)
        cut_row = dram("cut_row", [1, EP], BF16)
        lo_row = dram("lo_row", [1, EP], BF16)

        x = sb("x", [P, NT, D])
        h = sb("h", [P, NT, D])
        arena = sb("arena", [P, 14336])
        g = arena[:, 0:NT * D].rearrange("p (j d) -> p j d", d=D)
        g2 = arena[:, NT * D:2 * NT * D].rearrange("p (j d) -> p j d", d=D)
        weighted = sb("weighted", [P, 2, CT, H1 * P])
        weighted_flat = weighted[:, :, :, :].rearrange("p b t n -> p (b t n)")
        alpha = sb("alpha", [P, ET, H1])
        alpha_flat = alpha[:, :, :].rearrange("p t h -> p (t h)")
        hi_t = alpha_flat[:, 0:ET]
        lo_t = alpha_flat[:, ET:2 * ET]
        src_idx = sb("src_idx", [P, ET + NB * CT], I32)
        y_idx = sb("y_idx", [P, ET + NB * CT], I32)
        last_idx = sb("last_idx", [P, NT], I32)
        start_idx = sb("start_idx", [P, NT], I32)
        rcount = sb("rcount", [P, NT])
        slot = sb("slot", [P, NB, CT], I32)
        keep = sb("keep", [ER, EC])
        cut = sb("cut", [ER, EC])
        last = sb("last", [ER, EC])
        notlast = sb("notlast", [ER, EC])
        whole = sb("whole", [P, 3, P])
        ends = sb("ends", [ER, 2, P])
        ends_row = sb("ends_row", [P, P])
        carry = sb("carry", [ER, P])
        mask = sb("mask", [P, NB, CE], BF16)
        scan_t = sb("scan_t", [P, 2, CE])
        out_rows = sb("out_rows", [P, 2, CE])
        nodeval = sb("nodeval", [P, NT, 2 * H1])
        startval = sb("startval", [P, NT, 2 * H1])
        selfw = sb("selfw", [P, NT, H1])
        stat = sb("stat", [P, 2, NT])
        ident = sb("ident", [P, P])
        ones = sb("ones", [P, P])
        ones_tail = sb("ones_tail", [P, P])
        before = sb("before", [NT, NT])
        counts = sb("counts", [64, P])
        number = sb("number", [P, 2])
        his = sb("his", [P, HI])
        parts = sb("parts", [P, 3, H1, 64], BF16)
        w0 = sb("w0", [P, 4, D])
        w1 = sb("w1", [P, H1 * D])
        sc1 = sb("sc1", [P, 2 * H1])
        ff1 = sb("ff1", [P, FF])
        ff2 = sb("ff2", [P, FF // P, D])
        ff1_b = sb("ff1_b", [P, FF // P])
        w2 = sb("w2", [P, D])
        sc2 = sb("sc2", [P, 2 * H2])
        w3 = sb("w3", [P, (R + 1) * D])
        b0 = sb("b0", [1, 2, D])
        b3 = sb("b3", [1, (R + 1) * D])
        VECS = ["L1_gnn_bias", "L1_gnn_bn1_w", "L1_gnn_bn1_b", "L1_gnn_b2", "L1_gnn_bn2_w", "L1_gnn_bn2_b",
                "L2_gnn_bias", "L2_gnn_prelu_w"]
        vec = {n: sb(n + "_all", [P, D]) for n in VECS}
        mean = sb("mean", [P, D])
        gain = sb("gain", [P, D])

        pa, pb, pc, pd = [ctx.enter_context(nc.psum_tensor(n, [P, 2 * CE], F32)) for n in ("pa", "pb", "pc", "pd")]

        step = Chain(ctx.enter_context(nc.semaphore("vector_step")))
        act_step = Chain(ctx.enter_context(nc.semaphore("scalar_step")))
        pool_step = Chain(ctx.enter_context(nc.semaphore("pool_step")))
        passed = ctx.enter_context(nc.semaphore("passed"))
        cleared = count("cleared")
        loaded = count("loaded")
        stored = count("stored")
        rows_moved = count("rows_moved")
        turned = count("turned")
        ends_ready = count("ends_ready")
        sums_ready = count("sums_ready")
        gathered = [count(f"gathered{c}") for c in range(NB)]
        idx_staged = count("idx_staged")
        hot_made = count("hot_made", NB)
        picked = count("picked", 2)
        masked = count("masked", NB)
        hi_made = count("hi_made")
        summed = count("summed", 2)
        chunk_weighted = count("chunk_weighted")
        counted = count("counted", 1)
        chunk_turned = count("chunk_turned", NB)
        chunk_scanned = count("chunk_scanned", NB)
        chunk_back = count("chunk_back", 2)
        chunk_copied = count("chunk_copied", 2)
        written = [count(f"written{b}", 16) for b in range(2)]
        mask_loaded = [count(f"mask_loaded{c}") for c in range(NB)]
        group_staged = count("group_staged")
        group_turned = count("group_turned", 1)
        group_lhs = count("group_lhs")
        tile_product = count("tile_product", 1)
        tile_out = [count(f"tile_out{o}", 2) for o in range(2)]
        tile_stored = [count(f"tile_stored{b}", 16) for b in range(2)]
        ff_up = count("ff_up", 1)
        ff_hidden = count("ff_hidden", 2)
        ff_down = count("ff_down", 1)
        ff_kept = count("ff_kept", 1)

        def wait_apart(engine, sem, value):
            engine.wait_ge(sem, value)
            engine.sem_inc(passed, 1)

        def move_rows(pool, to, rows, table, idx, width):
            for j in range(NT):
                nc.gpsimd.indirect_dma_start(out=to[:, j, 0:width], out_offset=None, in_=table[:, :],
                                             in_offset=bass.IndirectOffsetOnAxis(ap=idx[:, j:j + 1], axis=0)
                                             ).then_inc(rows.sem, 16)

        dst_i = arena[0:ER, 0:EC].bitcast(I32)
        src_i = arena[0:ER, EC:2 * EC].bitcast(I32)
        rel_i = arena[0:ER, 2 * EC:3 * EC].bitcast(I32)
        dst_f = arena[0:ER, 3 * EC:4 * EC]
        src_f = arena[0:ER, 4 * EC:5 * EC]
        tmp_f = arena[0:ER, 5 * EC:6 * EC]
        tmp_i = arena[0:ER, 6 * EC:7 * EC].bitcast(I32)
        prev_i = arena[0:ER, 7 * EC:7 * EC + 1].bitcast(I32)
        next_i = arena[0:ER, 7 * EC + 1:7 * EC + 2].bitcast(I32)
        prev_f = arena[0:ER, 7 * EC + 2:7 * EC + 3]
        next_f = arena[0:ER, 7 * EC + 3:7 * EC + 4]
        at = 7 * EC + 8

        def take(n):
            nonlocal at
            at += n
            return arena[:, at - n:at]

        raw_w = take(4 * D).rearrange("p (k d) -> p k d", d=D)
        att = take(4 * H1 * D).rearrange("p (k d) -> p k d", d=H1 * D)
        wdst = take(D)
        prod = take(H1 * D)
        iota_i = take(P).bitcast(I32)
        number_i = take(1).bitcast(I32)
        lo16 = take(EC // 2).bitcast(BF16)
        keep16 = take(EC // 2).bitcast(BF16)
        cut16 = take(EC // 2).bitcast(BF16)

        ERF, TAIL = E // EC, E % EC
        with nc.Block() as block:
            @block.vector
            def _(dve):
                v = nc.vector
                v.memset(dst_i, N)
                v.memset(src_i, 0)
                v.memset(rel_i, 0)
                v.memset(prev_i, -1)
                v.memset(next_i, -1)
                v.memset(x[:, NT - 1, :], 0.0)
                v.memset(ends[:, :, :], 0.0)
                v.memset(ends_row[:, :], 0.0)
                v.memset(counts[:, :], 0.0)
                v.memset(src_idx[:, ET:], 0)
                v.memset(y_idx[:, ET:], 0)
                v.memset(scan_t[:, 1, :], 0.0)
                v.memset(ones[:, :], 1.0)
                v.memset(out_rows[:, 0, :], 0.0).then_inc(cleared.sem, 1)

            @block.gpsimd
            def _(pool):
                p = nc.gpsimd
                pool_step(pool, p.memset(ident[:, :], 0.0))
                p.affine_select(out=ident[:, :], in_=ident[:, :], compare_op=ALU.not_equal, fill=1.0,
                                base=0, pattern=[[-1, P]], channel_multiplier=1)
                pool_step(pool, p.memset(ones_tail[:, :], 1.0))
                p.affine_select(out=ones_tail[:, :], in_=ones_tail[:, :], compare_op=ALU.is_ge, fill=0.0,
                                base=NL - 1, pattern=[[0, P]], channel_multiplier=-1)
                pool_step(pool, p.memset(before[:, :], 1.0))
                p.affine_select(out=before[:, :], in_=before[:, :], compare_op=ALU.is_gt, fill=0.0,
                                base=0, pattern=[[1, NT]], channel_multiplier=-1)
                p.iota(iota_i, [[1, P]], base=0, channel_multiplier=0)
                p.iota(number_i, [[0, 1]], base=0, channel_multiplier=1)

            @block.tensor
            def _(pe):
                for c in (counted, ff_up, picked, masked, summed, chunk_turned, chunk_back, group_turned, tile_product, ff_down):
                    pe.sem_inc(c.sem, c.ahead)

            @block.scalar
            def _(act):
                for c in (hot_made, chunk_scanned, chunk_copied, *written, *tile_out, *tile_stored, ff_hidden, ff_kept):
                    act.sem_inc(c.sem, c.ahead)

            @block.sync
            def _(sp):
                loads = 0

                def load(to, of, **single):
                    nonlocal loads
                    loads += 1
                    sp.dma_start(to, of, **single).then_inc(loaded.sem, 16)

                few = {"allow_slow_non_contiguous": True}
                sp.wait_ge(cleared.sem, 1)
                for to, name in ((dst_i, "dst"), (src_i, "src"), (rel_i, "edge_type_4")):
                    load(to[0:ERF, :], a[name][0:ERF * EC].rearrange("(q f) -> q f", f=EC))
                    load(to[ERF:ERF + 1, 0:TAIL], a[name][ERF * EC:E].rearrange("(q f) -> q f", q=1))
                load(prev_i[1:ER, :], a["dst"][0:ERF * EC].rearrange("(q f) -> q f", f=EC)[:, EC - 1:EC], **few)
                load(next_i[0:ER - 2, :], a["dst"][EC:ERF * EC].rearrange("(q f) -> q f", f=EC)[:, 0:1], **few)
                load(next_i[ER - 2:ER - 1, :], a["dst"][ERF * EC:ERF * EC + 1].rearrange("(q f) -> q f", q=1), **few)
                load(x[:, 0:NT - 1, :], a["x"][0:(NT - 1) * P, :].rearrange("(j p) d -> p j d", p=P))
                load(x[0:NL, NT - 1, :], a["x"][(NT - 1) * P:N, :])
                for k, name in enumerate(("L0_gnn_W1l", "L0_gnn_W1r", "L0_gnn_W2l", "L0_gnn_W2r")):
                    load(raw_w[:, k, :], a[name][:, :])
                for k, name in enumerate(("L0_gnn_b1", "L0_gnn_b2")):
                    load(b0[0:1, k, :], a[name].rearrange("(o d) -> o d", o=1))
                load(w1[:, :], a["L1_gnn_W"][:, :])
                load(ff1[:, :], a["L1_gnn_W1"][:, :])
                load(ff2[:, :, :], a["L1_gnn_W2"].rearrange("(k p) d -> p k d", p=P))
                load(ff1_b[:, :], a["L1_gnn_b1"].rearrange("(k p) -> p k", p=P), **few)
                load(w2[:, :], a["L2_gnn_W_src"][:, :])
                load(wdst, a["L2_gnn_W_dst"][:, :])
                load(w3[:, :].rearrange("p (r d) -> p r d", d=D), a["L3_gnn_weight"].rearrange("r p d -> p r d"))
                load(b3[0:1, :], a["L3_gnn_bias"].rearrange("(o r) d -> o (r d)", o=1))
                for name in VECS:
                    load(vec[name][:, :], a[name].rearrange("(o d) -> o d", o=1).broadcast_to([P, D]))
                for k, (name, n) in enumerate((("L1_gnn_att_src", H1 * D), ("L1_gnn_att_dst", H1 * D),
                                               ("L2_gnn_att_src", D), ("L2_gnn_att_dst", D))):
                    load(att[:, k, 0:n], a[name].rearrange("(o h) c -> o (h c)", o=1).broadcast_to([P, n]))
                load(scan_rows[EP:EP + P, :], out_rows[:, 0, 0:D])
                load(self_rows[EP:EP + P, :], ones[:, 0:H1])
                sp.wait_ge(loaded.sem, 16 * loads)
                loaded.base = 16 * loads
        cleared.base += 1

        def turn_edges(row, tiles):
            with nc.Block() as block:
                @block.tensor
                def _(pe):
                    for f in range(TQ):
                        ins = nc.tensor.transpose(pa[:, f * P:f * P + ER], row[:, f * P:(f + 1) * P], ident[0:ER, 0:ER])
                    ins.then_inc(turned.sem, 1)

                @block.vector
                def _(dve):
                    dve.wait_ge(turned.sem, turned.past(1))
                    nc.vector.tensor_copy(tiles.rearrange("p (q f) -> p f q", f=TQ),
                                          pa[:, 0:TQ * P].rearrange("p (f q) -> p f q", q=P)[:, :, 0:ER])
            turned.base += 1

        with nc.Block() as block:
            @block.vector
            def _(dve):
                v = nc.vector
                v.tensor_copy(dst_f, dst_i)
                v.tensor_copy(src_f, src_i)
                v.tensor_copy(pd[:, 0:P], iota_i)
                v.tensor_copy(his[:, :], iota_i[:, 0:HI])
                step(dve, v.tensor_copy(number[:, 0:1], number_i))
                v.tensor_scalar(number[:, 1:2], number[:, 0:1], float(P), None, ALU.add)
                v.memset(parts[:, :, :, :], 0.0)
                step(dve, v.tensor_single_scalar(tmp_i, src_i, 2 * P - 1, ALU.bitwise_and))
                v.tensor_copy(lo16[0:ER, :], tmp_i)
                v.tensor_copy(prev_f, prev_i)
                step(dve, v.tensor_copy(next_f, next_i))
                v.tensor_tensor(keep[:, 1:EC], dst_f[:, 1:EC], dst_f[:, 0:EC - 1], ALU.is_equal)
                v.tensor_tensor(keep[:, 0:1], dst_f[:, 0:1], prev_f, ALU.is_equal)
                v.tensor_tensor(notlast[:, 0:EC - 1], dst_f[:, 0:EC - 1], dst_f[:, 1:EC], ALU.is_equal)
                step(dve, v.tensor_tensor(notlast[:, EC - 1:EC], dst_f[:, EC - 1:EC], next_f, ALU.is_equal))
                v.tensor_scalar(cut[:, :], keep[:, :], -1.0, BIG, ALU.add, ALU.mult)
                v.tensor_scalar(last[:, :], notlast[:, :], -1.0, 1.0, ALU.mult, ALU.add)
                v.tensor_copy(keep16[0:ER, :], keep[:, :])
                v.tensor_scalar(cut16[0:ER, :], keep[:, :], -1.0, BIG, ALU.add, ALU.mult)
                v.scalar_tensor_tensor(out=tmp_f, in0=rel_i, scalar=float(NP), in1=src_f, op0=ALU.mult, op1=ALU.add)
                v.tensor_reduce(carry[:, 0:1], keep[:, :], AX.X, ALU.min)
                step(dve, v.tensor_reduce(carry[:, 1:2], notlast[:, :], AX.X, ALU.min))
                for k in range(2):
                    v.tensor_copy(ends[:, k, 0:2 * H1], carry[:, k:k + 1].broadcast_to([ER, 2 * H1]))
                for k, (w, to, heads, c) in enumerate(((w1[:, :], sc1[:, 0:H1], H1, D), (w1[:, :], sc1[:, H1:2 * H1], H1, D),
                                                       (w2[:, :], sc2[:, 0:H2], H2, D // H2),
                                                       (wdst, sc2[:, H2:2 * H2], H2, D // H2))):
                    step(dve, v.tensor_tensor(prod[:, 0:heads * c], w[:, 0:heads * c], att[:, k, 0:heads * c], ALU.mult))
                    step(dve, v.tensor_reduce(to, prod[:, 0:heads * c].rearrange("p (h c) -> p h c", c=c), AX.X, ALU.add))

            @block.tensor
            def _(pe):
                for k in range(4):
                    ins = nc.tensor.transpose(pb[:, k * D:(k + 1) * D], raw_w[:, k, :], ident[:, :])
                ins.then_inc(turned.sem, 1)

            @block.scalar
            def _(act):
                act.wait_ge(turned.sem, turned.past(1))
                nc.scalar.copy(w0[:, :, :], pb[:, 0:4 * D].rearrange("p (k d) -> p k d", d=D))
        turned.base += 1

        with nc.Block() as block:
            @block.tensor
            def _(pe):
                nc.tensor.transpose(pa[:, 0:ER], ends[:, 0, :], ident[0:ER, 0:ER])
                nc.tensor.transpose(pa[:, P:P + ER], ends[:, 1, :], ident[0:ER, 0:ER]).then_inc(turned.sem, 1)

            @block.vector
            def _(dve):
                dve.wait_ge(turned.sem, turned.past(1))
                nc.vector.tensor_copy(whole[:, 0, 0:ER], pa[:, 0:ER])
                nc.vector.tensor_scalar(whole[:, 1, 0:ER], pa[:, 0:ER], -1.0, BIG, ALU.add, ALU.mult)
                nc.vector.tensor_copy(whole[:, 2, 0:ER], pa[:, P:P + ER])

            @block.sync
            def _(sp):
                sp.dma_start(keep_row.rearrange("o (q f) -> (o q) f", f=EC), keep16[0:ER, :]).then_inc(stored.sem, 16)
                sp.dma_start(cut_row.rearrange("o (q f) -> (o q) f", f=EC), cut16[0:ER, :]).then_inc(stored.sem, 16)
                sp.dma_start(lo_row.rearrange("o (q f) -> (o q) f", f=EC), lo16[0:ER, :]).then_inc(stored.sem, 16)
                sp.wait_ge(stored.sem, stored.past(48))
        turned.base += 1
        stored.base += 48
        turn_edges(src_f, src_idx[:, 0:ET])
        turn_edges(tmp_f, y_idx[:, 0:ET])
        for op, by, tiles in ((ALU.arith_shift_right, 7, hi_t), (ALU.bitwise_and, P - 1, lo_t)):
            with nc.Block() as block:
                @block.vector
                def _(dve):
                    step(dve, nc.vector.tensor_single_scalar(tmp_i, dst_i, by, op))
                    nc.vector.tensor_copy(tmp_f, tmp_i)
            turn_edges(tmp_f, tiles)

        def laps(engine, first, body):
            first()
            with engine.Fori(0, ITERS - 1) as i:
                for c in range(NB):
                    body(i, c, True)
            for c in range(NB):
                body(ITERS - 1, c, c < NB - 1)

        def edge_pass(table, width, idx, mask_row, op0, op1, mode="plain"):
            def rows(c, t):
                n = (c * CT + t) * width
                return arena[:, n:n + width]

            def hot(b):
                both = weighted_flat[:, b * CT * H1 * P:b * CT * H1 * P + CT * (64 + P) // 2].bitcast(BF16)
                return (both[:, 0:CT * 64].rearrange("p (t k) -> p t k", k=64),
                        both[:, CT * 64:CT * (64 + P)].rearrange("p (t k) -> p t k", k=P))

            with nc.Block() as block:
                @block.gpsimd
                def _(pool):
                    with pool.Fori(0, ITERS) as i:
                        for c in range(NB):
                            wait_apart(pool, idx_staged.sem, idx_staged.past(i * NB + c + 1))
                            for t in range(CT):
                                nc.gpsimd.indirect_dma_start(
                                    out=rows(c, t), out_offset=None, in_=table[:, :],
                                    in_offset=bass.IndirectOffsetOnAxis(ap=slot[:, c, t:t + 1], axis=0)
                                ).then_inc(gathered[c].sem, 16)

                @block.sync
                def _(sp):
                    with sp.Fori(0, ITERS) as i:
                        for c in range(NB):
                            k = i * NB + c
                            sp.wait_ge(chunk_scanned.sem, chunk_scanned.by_last_lap(k + 1))
                            sp.dma_start(mask[:, c, :], mask_row[0:1, bass.ds(k * CE, CE)].broadcast_to([P, CE])
                                         ).then_inc(mask_loaded[c].sem, 16)

                @block.vector
                def _(dve):
                    v = nc.vector

                    def weigh(i, c):
                        k, b = i * NB + c, c % 2
                        if mode == "plain":
                            return
                        dve.wait_ge(chunk_turned.sem, chunk_turned.by_last_lap(k + NB - 1))
                        if mode == "count":
                            hot_hi, hot_lo = hot(b)
                            v.tensor_tensor(hot_hi, pd[:, 0:64].unsqueeze(1).broadcast_to([P, CT, 64]),
                                            hi_t[:, bass.ds(k * CT, CT)].unsqueeze(2).broadcast_to([P, CT, 64]), ALU.is_equal)
                            v.tensor_tensor(hot_lo, pd[:, 0:P].unsqueeze(1).broadcast_to([P, CT, P]),
                                            lo_t[:, bass.ds(k * CT, CT)].unsqueeze(2).broadcast_to([P, CT, P]), ALU.is_equal
                                            ).then_inc(chunk_weighted.sem, 1)
                        elif mode == "heads":
                            for t in range(CT):
                                ins = v.tensor_tensor(
                                    weighted[:, b, t, :].rearrange("p (h n) -> p h n", n=P),
                                    pd[:, 0:P].unsqueeze(1).broadcast_to([P, H1, P]),
                                    alpha_flat[:, bass.ds((k * CT + t) * H1, H1)].unsqueeze(2).broadcast_to([P, H1, P]), ALU.mult)
                            ins.then_inc(chunk_weighted.sem, 1)
                        else:
                            dve.wait_ge(gathered[c % NB].sem, gathered[c % NB].past((i + c // NB + 1) * 16 * CT))
                            half = D // H2
                            n = (c % NB) * CT * width
                            v.tensor_tensor(
                                weighted[:, b, :, 0:D].rearrange("p t (h n) -> p t h n", n=half),
                                arena[:, n:n + CT * width].rearrange("p (t h n) -> p t h n", h=H2, n=half),
                                alpha[:, bass.ds(k * CT, CT), 0:H2].unsqueeze(3).broadcast_to([P, CT, H2, half]), ALU.mult
                            ).then_inc(chunk_weighted.sem, 1)

                    def scan(i, c, more):
                        if more:
                            weigh(i, c + 1)
                        k, b = i * NB + c, c % 2
                        dve.wait_ge(chunk_turned.sem, chunk_turned.past(k + 1))
                        if mode == "count":
                            dve.wait_ge(counted.sem, counted.past(k))
                            v.tensor_tensor(counts[:, :], counts[:, :], pc[0:64, b * CE:b * CE + P], ALU.add
                                            ).then_inc(counted.sem, 1)
                        dve.wait_ge(mask_loaded[c].sem, mask_loaded[c].past((i + 1) * 16))
                        dve.wait_ge(chunk_back.sem, chunk_back.by_last_lap(k + 1))
                        dve.wait_ge(chunk_scanned.sem, chunk_scanned.past(k))
                        v.tensor_tensor_scan(scan_t[:, b, :], mask[:, c, :], pa[:, b * CE:(b + 1) * CE],
                                             scan_t[:, 1 - b, CE - 1:CE], op0, op1).then_inc(chunk_scanned.sem, 1)

                    laps(dve, lambda: weigh(0, 0), scan)

                @block.tensor
                def _(pe):
                    def turn(i, c):
                        k, b, s = i * NB + c, c % 2, c % NB
                        if mode != "plain":
                            pe.wait_ge(chunk_weighted.sem, chunk_weighted.past(k + 1))
                        if mode != "halves":
                            pe.wait_ge(gathered[s].sem, gathered[s].past((i + c // NB + 1) * 16 * CT))
                        pe.wait_ge(chunk_scanned.sem, chunk_scanned.past(k - 1))
                        if mode == "count":
                            hot_hi, hot_lo = hot(b)
                            for t in range(CT):
                                nc.tensor.matmul(pc[0:64, b * CE:b * CE + P], hot_hi[:, t, :], hot_lo[:, t, :],
                                                 start=(t == 0), stop=(t == CT - 1))
                        for t in range(CT):
                            to = pa[:, b * CE + t * P:b * CE + (t + 1) * P]
                            if mode == "heads":
                                for hd in range(H1):
                                    ins = nc.tensor.matmul(to, rows(s, t)[:, hd * D:(hd + 1) * D],
                                                           weighted[:, b, t, hd * P:(hd + 1) * P],
                                                           start=(hd == 0), stop=(hd == H1 - 1))
                            elif mode == "halves":
                                ins = nc.tensor.transpose(to, weighted[:, b, t, 0:D], ident[:, :])
                            else:
                                ins = nc.tensor.transpose(to, rows(s, t), ident[:, :])
                        ins.then_inc(chunk_turned.sem, 1)

                    def back(i, c, more):
                        if more:
                            turn(i, c + 1)
                        k, b = i * NB + c, c % 2
                        pe.wait_ge(chunk_scanned.sem, chunk_scanned.past(k + 1))
                        pe.wait_ge(chunk_copied.sem, chunk_copied.by_last_lap(k + 1))
                        for t in range(CT):
                            ins = nc.tensor.transpose(pb[:, b * CE + t * P:b * CE + (t + 1) * P],
                                                      scan_t[:, b, t * P:(t + 1) * P], ident[:, :])
                        ins.then_inc(chunk_back.sem, 1)

                    laps(pe, lambda: turn(0, 0), back)

                @block.scalar
                def _(act):
                    def stage_numbers(k, c):
                        nc.scalar.copy(slot[:, c, :], idx[:, bass.ds(k * CT, CT)]).then_inc(idx_staged.sem, 1)

                    for c in range(NB):
                        stage_numbers(c, c)
                    with act.Fori(0, ITERS) as i:
                        for c in range(NB):
                            k, b = i * NB + c, c % 2
                            act.wait_ge(chunk_back.sem, chunk_back.past(k + 1))
                            act.wait_ge(written[b].sem, written[b].by_last_lap((i * 2 + c // 2 + 1) * 16))
                            nc.scalar.copy(out_rows[:, b, :], pb[:, b * CE:(b + 1) * CE]).then_inc(chunk_copied.sem, 1)
                            act.wait_ge(chunk_copied.sem, chunk_copied.past(k + 1))
                            act.dma_start(scan_rows[bass.ds(k * CE, CE), :].rearrange("(t p) d -> p t d", p=P),
                                          out_rows[:, b, :].rearrange("p (t d) -> p t d", d=D)).then_inc(written[b].sem, 16)
                            stage_numbers(k + NB, c)
                    for b in range(2):
                        act.wait_ge(written[b].sem, written[b].past(16 * CHUNKS // 2))
            idx_staged.base += CHUNKS + NB
            for c in gathered:
                c.base += 16 * CT * ITERS
            for c in (chunk_turned, chunk_scanned, chunk_back, chunk_copied):
                c.base += CHUNKS
            if mode != "plain":
                chunk_weighted.base += CHUNKS
            for w in written:
                w.base += 16 * CHUNKS // 2
            for m in mask_loaded:
                m.base += 16 * ITERS

        def gather_results(to, table, width):
            with nc.Block() as block:
                @block.gpsimd
                def _(pool):
                    move_rows(pool, to, rows_moved, table, last_idx, width)
                    pool.wait_ge(rows_moved.sem, rows_moved.past(16 * NT))
            rows_moved.base += 16 * NT

        def wide(t):
            return t.unsqueeze(2).broadcast_to([P, NT, D])

        def across(t):
            return t.unsqueeze(1).broadcast_to([P, NT, D])

        def layernorm_relu(tmp):
            with nc.Block() as block:
                @block.vector
                def _(dve):
                    v = nc.vector
                    step(dve, v.tensor_reduce(stat[:, 0, :], x[:, :, :], AX.X, ALU.add))
                    step(dve, v.tensor_scalar(stat[:, 0, :], stat[:, 0, :], 1.0 / D, None, ALU.mult))
                    step(dve, v.tensor_tensor(h[:, :, :], x[:, :, :], wide(stat[:, 0, :]), ALU.subtract))
                    step(dve, v.tensor_tensor(tmp, h[:, :, :], h[:, :, :], ALU.mult))
                    step(dve, v.tensor_reduce(stat[:, 1, :], tmp, AX.X, ALU.add))
                    v.tensor_scalar(stat[:, 1, :], stat[:, 1, :], 1.0 / D, LN_EPS, ALU.mult, ALU.add).then_inc(sums_ready.sem, 1)
                    dve.wait_ge(sums_ready.sem, sums_ready.past(2))
                    step(dve, v.reciprocal(stat[:, 0, :], stat[:, 1, :]))
                    v.scalar_tensor_tensor(out=h[:, :, :], in0=h[:, :, :], scalar=0.0, in1=wide(stat[:, 0, :]),
                                           op0=ALU.max, op1=ALU.mult)

                @block.scalar
                def _(act):
                    act.wait_ge(sums_ready.sem, sums_ready.past(1))
                    nc.scalar.activation(stat[:, 1, :], stat[:, 1, :], ACT.Sqrt).then_inc(sums_ready.sem, 1)
            sums_ready.base += 2

        def store_rows(table, rows):
            with nc.Block() as block:
                @block.sync
                def _(sp):
                    sp.dma_start(table.rearrange("(j p) d -> p j d", p=P), rows).then_inc(stored.sem, 16)
                    sp.wait_ge(stored.sem, stored.past(16))
            stored.base += 16

        def stage(s):
            return weighted_flat[:, s * NG * P:(s + 1) * NG * P]

        def lhs(s):
            return weighted_flat[:, (2 + s) * NG * P:(3 + s) * NG * P]

        def project(srcs, outs):
            ns = len(srcs)
            turns, results = (pa, pd), (pb, pc)

            with nc.Block() as block:
                @block.gpsimd
                def _(pool):
                    with pool.Fori(0, groups) as i:
                        for s in range(ns):
                            wait_apart(pool, group_turned.sem, group_turned.by_last_lap(i * ns + 1))
                            nc.gpsimd.tensor_copy(stage(s).rearrange("p (t d) -> p t d", d=D), srcs[s][:, bass.ds(i * NG, NG), :]
                                                  ).then_inc(group_staged.sem, 1)

                @block.tensor
                def _(pe):
                    with pe.Fori(0, groups) as i:
                        for s in range(ns):
                            pe.wait_ge(group_staged.sem, group_staged.past(i * ns + s + 1))
                            for t in range(NG):
                                ins = nc.tensor.transpose(turns[s][:, t * P:(t + 1) * P], stage(s)[:, t * P:(t + 1) * P], ident[:, :])
                            ins.then_inc(group_turned.sem, 1)
                        for t in range(NG):
                            b = t % 2
                            if t == 0:
                                pe.wait_ge(group_lhs.sem, group_lhs.past((i + 1) * ns))
                            for o in range(len(outs)):
                                pe.wait_ge(tile_out[o].sem, tile_out[o].by_last_lap(i * NG + (t + 1 if t > 1 else 2 - t)))
                            for o, (ws, bias, n, _) in enumerate(outs):
                                to = results[o][:, b * CE:b * CE + n]
                                for s in range(ns):
                                    ins = nc.tensor.matmul(to, lhs(s)[:, t * P:(t + 1) * P], ws[s],
                                                           start=(s == 0), stop=(bias is None and s == ns - 1))
                                if bias is not None:
                                    ins = nc.tensor.matmul(to, ones[0:1, :], bias, start=False, stop=True)
                            ins.then_inc(tile_product.sem, 1)

                def keep_products(engine, copy, o, i, t):
                    ws, bias, n, where = outs[o]
                    b = t % 2
                    wait_apart(engine, tile_product.sem, tile_product.past(i * NG + t + 1))
                    if callable(where):
                        use = i * (4 - b) + t // 2
                        engine.wait_ge(tile_stored[b].sem, tile_stored[b].by_last_lap(use * 16 + 16))
                        to = out_rows[:, b, 0:n]
                    else:
                        to = where[:, bass.ds(i * NG + t, 1), 0:n].rearrange("p j d -> p (j d)")
                    copy(to, results[o][:, b * CE:b * CE + n]).then_inc(tile_out[o].sem, 1)

                @block.vector
                def _(dve):
                    with dve.Fori(0, groups) as i:
                        for s in range(ns):
                            dve.wait_ge(tile_product.sem, tile_product.by_last_lap(i * NG + 1))
                            dve.wait_ge(group_turned.sem, group_turned.past(i * ns + s + 1))
                            nc.vector.tensor_copy(lhs(s), turns[s][:, 0:NG * P]).then_inc(group_lhs.sem, 1)
                        if len(outs) > 1:
                            for t in range(NG):
                                keep_products(dve, nc.vector.tensor_copy, 1, i, t)

                @block.scalar
                def _(act):
                    with act.Fori(0, groups) as i:
                        for t in range(NG):
                            keep_products(act, nc.scalar.copy, 0, i, t)

                if callable(outs[0][3]):
                    @block.sync
                    def _(sp):
                        with sp.Fori(0, groups) as i:
                            for t in range(NG):
                                b = t % 2
                                sp.wait_ge(tile_out[0].sem, tile_out[0].past(i * NG + t + 1))
                                to = outs[0][3](i * NG + t)
                                sp.dma_start(to, out_rows[:, b, 0:outs[0][2]] if len(to.shape) == 2 else
                                             out_rows[:, b, 0:outs[0][2]].rearrange("p (r d) -> p r d", d=D)
                                             ).then_inc(tile_stored[b].sem, 16)
                        for b in range(2):
                            sp.wait_ge(tile_stored[b].sem, tile_stored[b].past(16 * (4 - b) * groups))
            group_staged.base += ns * groups
            group_turned.base += ns * groups
            group_lhs.base += ns * groups
            tile_product.base += NT
            for o in range(len(outs)):
                tile_out[o].base += NT
            if callable(outs[0][3]):
                for b in range(2):
                    tile_stored[b].base += 16 * (4 - b) * groups

        def feed_forward():
            hidden = [arena[:, NT * D + k * NG * P:NT * D + (k + 1) * NG * P] for k in range(FF // P)]
            nk = FF // P
            ups = (pb, pd)

            with nc.Block() as block:
                @block.gpsimd
                def _(pool):
                    with pool.Fori(0, groups) as i:
                        wait_apart(pool, group_turned.sem, group_turned.by_last_lap(i + 1))
                        nc.gpsimd.tensor_copy(stage(0).rearrange("p (t d) -> p t d", d=D), h[:, bass.ds(i * NG, NG), :]
                                              ).then_inc(group_staged.sem, 1)

                @block.tensor
                def _(pe):
                    with pe.Fori(0, groups) as i:
                        pe.wait_ge(group_staged.sem, group_staged.past(i + 1))
                        for t in range(NG):
                            ins = nc.tensor.transpose(pa[:, t * P:(t + 1) * P], stage(0)[:, t * P:(t + 1) * P], ident[:, :])
                        ins.then_inc(group_turned.sem, 1)
                        pe.wait_ge(group_lhs.sem, group_lhs.past(i + 1))
                        for k in range(nk):
                            pe.wait_ge(ff_hidden.sem, ff_hidden.by_last_lap(i * nk + k + 1))
                            for lo, hi in ((0, CE), (CE, NG * P)):
                                ins = nc.tensor.matmul(ups[k % 2][:, lo:hi], ff1[:, k * P:(k + 1) * P], lhs(0)[:, lo:hi],
                                                       start=True, stop=True)
                            ins.then_inc(ff_up.sem, 1)
                        pe.wait_ge(ff_hidden.sem, ff_hidden.past((i + 1) * nk))
                        pe.wait_ge(ff_kept.sem, ff_kept.by_last_lap(i + 1))
                        for t in range(NG):
                            for k in range(nk):
                                ins = nc.tensor.matmul(pc[:, t * P:(t + 1) * P], hidden[k][:, t * P:(t + 1) * P], ff2[:, k, :],
                                                       start=(k == 0), stop=(k == nk - 1))
                        ins.then_inc(ff_down.sem, 1)

                @block.scalar
                def _(act):
                    with act.Fori(0, groups) as i:
                        for k in range(nk):
                            act.wait_ge(ff_down.sem, ff_down.by_last_lap(i + 1))
                            act.wait_ge(ff_up.sem, ff_up.past(i * nk + k + 1))
                            nc.scalar.activation(hidden[k], ups[k % 2][:, 0:NG * P], ACT.Relu, bias=ff1_b[:, k:k + 1]
                                                 ).then_inc(ff_hidden.sem, 1)

                @block.vector
                def _(dve):
                    with dve.Fori(0, groups) as i:
                        dve.wait_ge(ff_up.sem, ff_up.past(i * nk))
                        dve.wait_ge(group_turned.sem, group_turned.past(i + 1))
                        nc.vector.tensor_copy(lhs(0), pa[:, 0:NG * P]).then_inc(group_lhs.sem, 1)
                        dve.wait_ge(ff_down.sem, ff_down.past(i + 1))
                        nc.vector.tensor_copy(g[:, bass.ds(i * NG, NG), :], pc[:, 0:NG * P].rearrange("p (t d) -> p t d", d=D)
                                              ).then_inc(ff_kept.sem, 1)
            group_staged.base += groups
            group_turned.base += groups
            group_lhs.base += groups
            ff_up.base += nk * groups
            ff_hidden.base += nk * groups
            ff_down.base += groups
            ff_kept.base += groups

        def column_sums(rows):
            with nc.Block() as block:
                @block.tensor
                def _(pe):
                    nc.tensor.matmul(pa[:, 0:D], ones[:, :], rows[:, 0, :], start=True, stop=False)
                    with pe.Fori(1, NT - 1) as j:
                        nc.tensor.matmul(pa[:, 0:D], ones[:, :], rows[:, bass.ds(j, 1), :].rearrange("p j d -> p (j d)"),
                                         start=False, stop=False)
                    nc.tensor.matmul(pa[:, 0:D], ones_tail[:, :], rows[:, NT - 1, :], start=False, stop=True)

        def batchnorm(w, b, to):
            column_sums(g)
            with nc.Block() as block:
                @block.vector
                def _(dve):
                    v = nc.vector
                    step(dve, v.tensor_scalar(mean[:, :], pa[:, 0:D], 1.0 / N, None, ALU.mult))
                    step(dve, v.tensor_tensor(g2, g, across(mean[:, :]), ALU.subtract))
                    v.tensor_tensor(g, g2, g2, ALU.mult)
            column_sums(g)
            with nc.Block() as block:
                @block.vector
                def _(dve):
                    v = nc.vector
                    v.tensor_scalar(gain[:, :], pa[:, 0:D], 1.0 / N, LN_EPS, ALU.mult, ALU.add).then_inc(sums_ready.sem, 1)
                    dve.wait_ge(sums_ready.sem, sums_ready.past(2))
                    step(dve, v.reciprocal(mean[:, :], gain[:, :]))
                    step(dve, v.tensor_tensor(mean[:, :], mean[:, :], w, ALU.mult))
                    step(dve, v.tensor_tensor(g2, g2, across(mean[:, :]), ALU.mult))
                    v.tensor_tensor(to, g2, across(b), ALU.add)

                @block.scalar
                def _(act):
                    act.wait_ge(sums_ready.sem, sums_ready.past(1))
                    nc.scalar.activation(gain[:, :], gain[:, :], ACT.Sqrt).then_inc(sums_ready.sem, 1)
            sums_ready.base += 2

        def elu(to):
            with nc.Block() as block:
                @block.vector
                def _(dve):
                    v = nc.vector
                    v.tensor_scalar(g2, g, 0.0, None, ALU.min).then_inc(sums_ready.sem, 1)
                    dve.wait_ge(sums_ready.sem, sums_ready.past(2))
                    step(dve, v.tensor_scalar(g2, g2, -1.0, None, ALU.add))
                    v.scalar_tensor_tensor(out=to, in0=g, scalar=0.0, in1=g2, op0=ALU.max, op1=ALU.add)

                @block.scalar
                def _(act):
                    act.wait_ge(sums_ready.sem, sums_ready.past(1))
                    nc.scalar.activation(g2, g2, ACT.Exp).then_inc(sums_ready.sem, 1)
            sums_ready.base += 2

        EA = weighted_flat[0:ER, 0:H1 * EC].rearrange("q (h f) -> q h f", f=EC)
        FROM_DST = arena[0:ER, 0:2 * H1 * EC].rearrange("q (h f) -> q h f", f=EC)
        START = arena[0:ER, 2 * H1 * EC:4 * H1 * EC]
        M = arena[0:ER, 2 * H1 * EC:3 * H1 * EC].rearrange("q (h f) -> q h f", f=EC)
        DEN = arena[0:ER, 3 * H1 * EC:4 * H1 * EC].rearrange("q (h f) -> q h f", f=EC)

        def segment_scan(n, to, of, kind):
            with_, flag, op0, op1, start = {"sum": (keep, 0, ALU.mult, ALU.add, 0.0),
                                            "max": (cut, 1, ALU.add, ALU.max, -BIG),
                                            "spread": (notlast, 2, ALU.mult, ALU.add, 0.0)}[kind]
            way = slice(None, None, -1) if kind == "spread" else slice(None)
            end = 0 if kind == "spread" else EC - 1
            into = (0, ER) if kind == "spread" else (1, ER + 1)
            out_of = (1, ER + 1) if kind == "spread" else (0, ER)

            with nc.Block() as block:
                @block.vector
                def _(dve):
                    v = nc.vector
                    for k in range(n):
                        step(dve, v.tensor_tensor_scan(to(k)[:, way], with_[:, way], of(k)[:, way], start, op0, op1))
                        v.tensor_copy(ends[:, 0, k:k + 1], to(k)[:, end:end + 1])
                    v.memset(ends_row[:, 0:1], start)
                    v.memset(ends_row[:, ER:ER + 1], start).then_inc(ends_ready.sem, 1)
                    dve.wait_ge(turned.sem, turned.past(1))
                    v.tensor_tensor_scan(ends_row[0:n, into[0]:into[1]][:, way], whole[0:n, flag, 0:ER][:, way],
                                         pa[0:n, 0:ER][:, way], start, op0, op1).then_inc(ends_ready.sem, 1)
                    dve.wait_ge(turned.sem, turned.past(2))
                    step(dve, v.tensor_copy(carry[:, 0:n], pb[0:ER, 0:n]))
                    for k in range(n):
                        v.tensor_tensor_scan(to(k)[:, way], with_[:, way], of(k)[:, way], carry[:, k:k + 1], op0, op1)

                @block.tensor
                def _(pe):
                    pe.wait_ge(ends_ready.sem, ends_ready.past(1))
                    nc.tensor.transpose(pa[:, 0:ER], ends[:, 0, :], ident[0:ER, 0:ER]).then_inc(turned.sem, 1)
                    pe.wait_ge(ends_ready.sem, ends_ready.past(2))
                    nc.tensor.transpose(pb[0:ER, 0:P], ends_row[:, out_of[0]:out_of[1]], ident[:, :]).then_inc(turned.sem, 1)
            ends_ready.base += 2
            turned.base += 2

        def look_up_scores(heads, start_rows, width):
            hots = weighted_flat[:, 0:2 * CE].bitcast(BF16).rearrange("p (b a n) -> p b a n", b=2, a=2)
            hot_hi = weighted_flat[:, 2 * CE:2 * CE + 2 * CT * HI].rearrange("p (b t j) -> p b t j", b=2, t=CT)
            left = weighted_flat[:, 3 * CE:5 * CE].rearrange("p (b n) -> p b n", b=2)
            hi_i = weighted_flat[:, 5 * CE:5 * CE + ET].bitcast(I32)
            hi = out_rows[:, :, :].rearrange("p b n -> p (b n)")[:, 0:ET]
            ways = heads * HI
            picks = [(pa, pb)[c // 2][:, c % 2 * CE:c % 2 * CE + CT * ways] for c in range(NB)]

            with nc.Block() as block:
                @block.vector
                def _(dve):
                    v = nc.vector
                    v.memset(arena[:, 0:EP * width // P], 0.0).then_inc(cleared.sem, 1)
                    rest = nodeval[:, :, 0:heads].rearrange("p j h -> p h j")
                    for k in range(3):
                        part = parts[:, k, 0:heads, 0:NT]
                        step(dve, v.tensor_copy(part, rest))
                        if k < 2:
                            step(dve, v.tensor_tensor(rest, rest, part, ALU.subtract))
                    step(dve, v.tensor_single_scalar(hi_i, src_idx[:, 0:ET], 8, ALU.arith_shift_right))
                    step(dve, v.tensor_copy(hi, hi_i))

                    def make_hot(i, c):
                        k, b, s = i * NB + c, c % 2, c % NB
                        dve.wait_ge(mask_loaded[s].sem, mask_loaded[s].past((i + c // NB + 1) * 16))
                        dve.wait_ge(picked.sem, picked.by_last_lap(k + 1))
                        for a in range(2):
                            ins = v.tensor_scalar(hots[:, b, a, :], mask[:, s, :], number[:, a:a + 1], None, ALU.is_equal)
                        ins.then_inc(hot_made.sem, 1)

                    def make_mask(i, c):
                        k, b = i * NB + c, c % 2
                        dve.wait_ge(masked.sem, masked.past(k - 1))
                        v.tensor_tensor(hot_hi[:, b, :, :], his[:, :].unsqueeze(1).broadcast_to([P, CT, HI]),
                                        hi[:, bass.ds(k * CT, CT)].unsqueeze(2).broadcast_to([P, CT, HI]), ALU.is_equal
                                        ).then_inc(hi_made.sem, 1)

                    def begin():
                        make_hot(0, 0)
                        make_mask(0, 0)

                    def leave_one(i, c, more):
                        if more:
                            make_hot(i, c + 1)
                        k, b, s = i * NB + c, c % 2, c % NB
                        dve.wait_ge(hi_made.sem, hi_made.past(k + 1))
                        dve.wait_ge(summed.sem, summed.by_last_lap(k + 1))
                        dve.wait_ge(picked.sem, picked.past(k + 1))
                        kept = left[:, b, 0:CT * ways]
                        v.tensor_tensor(kept.rearrange("p (t h j) -> p t h j", h=heads, j=HI),
                                        picks[s].rearrange("p (t h j) -> p t h j", h=heads, j=HI),
                                        hot_hi[:, b, :, :].unsqueeze(2).broadcast_to([P, CT, heads, HI]), ALU.mult
                                        ).then_inc(masked.sem, 1)
                        if more:
                            make_mask(i, c + 1)
                        dve.wait_ge(masked.sem, masked.past(k + 1))
                        v.tensor_reduce(alpha[:, bass.ds(k * CT, CT), 0:heads],
                                        kept.rearrange("p (t h j) -> p t h j", h=heads, j=HI), AX.X, ALU.add
                                        ).then_inc(summed.sem, 1)

                    laps(dve, begin, leave_one)

                @block.tensor
                def _(pe):
                    with pe.Fori(0, ITERS) as i:
                        for c in range(NB):
                            k, b = i * NB + c, c % 2
                            pe.wait_ge(hot_made.sem, hot_made.past(k + 1))
                            pe.wait_ge(masked.sem, masked.by_last_lap(k + 1))
                            for t in range(CT):
                                for a in range(2):
                                    for n in range(3):
                                        ins = nc.tensor.matmul(
                                            picks[c][:, t * ways:(t + 1) * ways].rearrange("p (h j) -> p h j", j=HI),
                                            hots[:, b, a, t * P:(t + 1) * P], parts[:, n, 0:heads, a:a + 2 * HI - 1:2],
                                            start=(a == 0 and n == 0), stop=(a == 1 and n == 2))
                            ins.then_inc(picked.sem, 1)

                @block.gpsimd
                def _(pool):
                    pool.wait_ge(stored.sem, stored.past(16))
                    for j in range(NT):
                        nc.gpsimd.indirect_dma_start(out=start_rows[:, :],
                                                     out_offset=bass.IndirectOffsetOnAxis(ap=start_idx[:, j:j + 1], axis=0),
                                                     in_=startval[:, j, 0:width], in_offset=None, bounds_check=EP - 1,
                                                     oob_is_err=False).then_inc(rows_moved.sem, 16)
                    pool.wait_ge(rows_moved.sem, rows_moved.past(16 * NT))

                @block.sync
                def _(sp):
                    sp.wait_ge(cleared.sem, cleared.past(1))
                    sp.dma_start(start_rows.rearrange("(p e) w -> p (e w)", p=P), arena[:, 0:EP * width // P]).then_inc(stored.sem, 16)
                    with sp.Fori(0, ITERS) as i:
                        for c in range(NB):
                            k = i * NB + c
                            sp.wait_ge(hot_made.sem, hot_made.by_last_lap(k + 1))
                            sp.dma_start(mask[:, c, :], lo_row[0:1, bass.ds(k * CE, CE)].broadcast_to([P, CE])
                                         ).then_inc(mask_loaded[c].sem, 16)
                    sp.wait_ge(stored.sem, stored.past(16))
                    sp.wait_ge(rows_moved.sem, rows_moved.past(16 * NT))
                    sp.dma_start(START[:, 0:width * EC], start_rows.rearrange("(q f) w -> q (f w)", f=EC)).then_inc(loaded.sem, 16)
                    sp.wait_ge(loaded.sem, loaded.past(16))
            cleared.base += 1
            stored.base += 16
            loaded.base += 16
            rows_moved.base += 16 * NT
            for c in (hot_made, hi_made, picked, masked, summed):
                c.base += CHUNKS
            for m in mask_loaded:
                m.base += 16 * ITERS

        def attention(heads, start_rows, with_self):
            width = 2 * heads if with_self else heads
            look_up_scores(heads, start_rows, width)
            start = START[:, 0:width * EC].rearrange("q (f w) -> q w f", w=width)
            segment_scan(width, lambda k: FROM_DST[:, k, :], lambda k: start[:, k, :], "sum")
            scores_to_rows(heads)
            e, den, m = EA[:, 0:heads, :], DEN[:, 0:heads, :], M[:, 0:heads, :]
            with nc.Block() as block:
                @block.vector
                def _(dve):
                    v = nc.vector
                    step(dve, v.tensor_tensor(e, e, FROM_DST[:, 0:heads, :], ALU.add))
                    v.scalar_tensor_tensor(out=e, in0=e, scalar=0.2, in1=e, op0=ALU.mult, op1=ALU.max)
            segment_scan(heads, lambda k: M[:, k, :], lambda k: EA[:, k, :], "max")

            def by_last(t):
                return last[:, :].unsqueeze(1).broadcast_to([ER, heads, EC])

            with nc.Block() as block:
                @block.vector
                def _(dve):
                    nc.vector.tensor_tensor(den, m, by_last(m), ALU.mult)
            segment_scan(heads, lambda k: M[:, k, :], lambda k: DEN[:, k, :], "spread")
            with nc.Block() as block:
                @block.vector
                def _(dve):
                    v = nc.vector
                    if with_self:
                        own = FROM_DST[:, heads:2 * heads, :]
                        step(dve, v.tensor_tensor(m, m, own, ALU.max))
                        v.tensor_tensor(own, own, m, ALU.subtract)
                    v.tensor_tensor(e, e, m, ALU.subtract).then_inc(sums_ready.sem, 1)

                @block.scalar
                def _(act):
                    act.wait_ge(sums_ready.sem, sums_ready.past(1))
                    nc.scalar.activation(e, e, ACT.Exp)
                    if with_self:
                        nc.scalar.activation(FROM_DST[:, heads:2 * heads, :], FROM_DST[:, heads:2 * heads, :], ACT.Exp)
            sums_ready.base += 1
            segment_scan(heads, lambda k: M[:, k, :], lambda k: EA[:, k, :], "sum")
            with nc.Block() as block:
                @block.vector
                def _(dve):
                    step(dve, nc.vector.tensor_tensor(den, m, by_last(m), ALU.mult))
            segment_scan(heads, lambda k: M[:, k, :], lambda k: DEN[:, k, :], "spread")
            own_il = arena[0:ER, 3 * H1 * EC:4 * H1 * EC]
            with nc.Block() as block:
                @block.vector
                def _(dve):
                    v = nc.vector
                    if with_self:
                        step(dve, v.tensor_tensor(m, m, FROM_DST[:, heads:2 * heads, :], ALU.add))
                    else:
                        step(dve, v.tensor_scalar(m, m, 1e-16, None, ALU.add))
                    step(dve, v.reciprocal(m, m))
                    v.tensor_tensor(e, e, m, ALU.mult)
                    if with_self:
                        v.tensor_tensor(own_il.rearrange("q (f h) -> q h f", h=heads), FROM_DST[:, heads:2 * heads, :], m, ALU.mult
                                        ).then_inc(sums_ready.sem, 1)

                if with_self:
                    @block.sync
                    def _(sp):
                        sp.wait_ge(sums_ready.sem, sums_ready.past(1))
                        sp.dma_start(self_rows[0:EP, :].rearrange("(q f) h -> q (f h)", f=EC), own_il).then_inc(stored.sem, 16)
                        sp.wait_ge(stored.sem, stored.past(16))
            if with_self:
                sums_ready.base += 1
                stored.base += 16
            with nc.Block() as block:
                @block.tensor
                def _(pe):
                    for hd in range(heads):
                        if hd >= 2:
                            pe.wait_ge(ends_ready.sem, ends_ready.past(hd - 1))
                        for f in range(TQ):
                            ins = nc.tensor.transpose((pa, pb)[hd % 2][:, f * P:f * P + ER], EA[:, hd, f * P:(f + 1) * P],
                                                      ident[0:ER, 0:ER])
                        ins.then_inc(turned.sem, 1)

                @block.vector
                def _(dve):
                    for hd in range(heads):
                        dve.wait_ge(turned.sem, turned.past(hd + 1))
                        nc.vector.tensor_copy(alpha[:, :, hd].rearrange("p (q f) -> p f q", f=TQ),
                                              (pa, pb)[hd % 2][:, 0:TQ * P].rearrange("p (f q) -> p f q", q=P)[:, :, 0:ER]
                                              ).then_inc(ends_ready.sem, 1)
            turned.base += heads
            ends_ready.base += heads

        def scores_to_rows(heads):
            with nc.Block() as block:
                @block.tensor
                def _(pe):
                    for hd in range(heads):
                        if hd >= 2:
                            pe.wait_ge(ends_ready.sem, ends_ready.past(hd - 1))
                        tiles = alpha[:, :, hd].rearrange("p (q f) -> p f q", f=TQ)
                        for f in range(TQ):
                            ins = nc.tensor.transpose((pa, pb)[hd % 2][0:ER, f * P:(f + 1) * P], tiles[:, f, :], ident[:, :])
                        ins.then_inc(turned.sem, 1)

                @block.vector
                def _(dve):
                    for hd in range(heads):
                        dve.wait_ge(turned.sem, turned.past(hd + 1))
                        nc.vector.tensor_copy(EA[:, hd, :], (pa, pb)[hd % 2][0:ER, 0:EC]).then_inc(ends_ready.sem, 1)
            turned.base += heads
            ends_ready.base += heads

        layernorm_relu(g)
        store_rows(h_tab, h[:, :, :])
        edge_pass(h_tab, D, src_idx, keep_row, ALU.mult, ALU.add, "count")

        cum = arena[0:NT, 0:P]
        firsts = arena[0:NT, 2 * P:3 * P]
        has = arena[0:NT, 3 * P:4 * P]
        total = arena[0:NT, 4 * P:4 * P + 1]
        offset = arena[0:NT, 4 * P + 1:4 * P + 2]
        with nc.Block() as block:
            @block.vector
            def _(dve):
                v = nc.vector
                cnt = counts[0:NT, :]
                v.tensor_scalar(has, cnt, 1.0, None, ALU.min)
                step(dve, v.tensor_reduce(total, cnt, AX.X, ALU.add))
                v.tensor_tensor_scan(cum, ones[0:NT, :], cnt, 0.0, ALU.mult, ALU.add).then_inc(ends_ready.sem, 1)
                dve.wait_ge(turned.sem, turned.past(1))
                step(dve, v.tensor_copy(offset, pa[0:NT, 0:1]))
                step(dve, v.tensor_scalar(cum, cum, offset, None, ALU.add))
                step(dve, v.tensor_tensor(firsts, cum, cnt, ALU.subtract))
                v.tensor_scalar(cum, cum, -1.0 - EP, None, ALU.add)
                step(dve, v.tensor_scalar(firsts, firsts, -float(SKIP), None, ALU.add))
                v.tensor_tensor(cum, cum, has, ALU.mult)
                step(dve, v.tensor_tensor(firsts, firsts, has, ALU.mult))
                v.tensor_scalar(cum, cum, float(EP), None, ALU.add)
                step(dve, v.tensor_scalar(firsts, firsts, float(SKIP), None, ALU.add))
                v.tensor_scalar(has, cnt, 1.0, None, ALU.max).then_inc(ends_ready.sem, 1)
                dve.wait_ge(turned.sem, turned.past(2))
                v.tensor_copy(last_idx[:, :], pb[:, 0:NT])
                v.tensor_copy(start_idx[:, :], pb[:, P:P + NT])
                v.reciprocal(rcount[:, :], pb[:, 2 * P:2 * P + NT])

            @block.tensor
            def _(pe):
                pe.wait_ge(ends_ready.sem, ends_ready.past(1))
                nc.tensor.matmul(pa[0:NT, 0:1], before[:, :], total, start=True, stop=True).then_inc(turned.sem, 1)
                pe.wait_ge(ends_ready.sem, ends_ready.past(2))
                for k, t in enumerate((cum, firsts, has)):
                    ins = nc.tensor.transpose(pb[:, k * P:k * P + NT], t, ident[0:NT, 0:NT])
                ins.then_inc(turned.sem, 1)
        turned.base += 2
        ends_ready.base += 2

        for layer in range(2):
            gather_results(g, scan_rows, D)
            with nc.Block() as block:
                @block.vector
                def _(dve):
                    nc.vector.tensor_tensor(g, g, wide(rcount[:, :]), ALU.mult)
            project([g, h[:, :, :]], [([w0[:, 2 * layer, :], w0[:, 2 * layer + 1, :]], b0[0:1, layer, :], D, g)])
            elu(h[:, :, :])
            if layer == 0:
                store_rows(h_tab, h[:, :, :])
                edge_pass(h_tab, D, src_idx, keep_row, ALU.mult, ALU.add)
        with nc.Block() as block:
            @block.vector
            def _(dve):
                v = nc.vector
                step(dve, v.tensor_reduce(stat[:, 0, :], h[:, :, :], AX.X, ALU.max))
                v.tensor_tensor(h[:, :, :], h[:, :, :], wide(stat[:, 0, :]), ALU.subtract).then_inc(sums_ready.sem, 1)
                dve.wait_ge(sums_ready.sem, sums_ready.past(2))
                v.tensor_reduce(stat[:, 1, :], g, AX.X, ALU.add).then_inc(sums_ready.sem, 1)
                step(dve, v.tensor_tensor(x[:, :, :], x[:, :, :], h[:, :, :], ALU.add))
                dve.wait_ge(sums_ready.sem, sums_ready.past(4))
                v.tensor_tensor(x[:, :, :], x[:, :, :], wide(stat[:, 0, :]), ALU.subtract)

            @block.scalar
            def _(act):
                act.wait_ge(sums_ready.sem, sums_ready.past(1))
                nc.scalar.activation(g, h[:, :, :], ACT.Exp).then_inc(sums_ready.sem, 1)
                act.wait_ge(sums_ready.sem, sums_ready.past(3))
                nc.scalar.activation(stat[:, 0, :], stat[:, 1, :], ACT.Ln).then_inc(sums_ready.sem, 1)
        sums_ready.base += 4

        layernorm_relu(g)
        project([h[:, :, :]], [([w1[:, :]], None, H1 * D, lambda j: x1_tab[bass.ds(j * P, P), :]),
                               ([sc1[:, :]], None, 2 * H1, nodeval)])
        with nc.Block() as block:
            @block.vector
            def _(dve):
                v = nc.vector
                s_src, s_dst = nodeval[:, :, 0:H1], nodeval[:, :, H1:2 * H1]
                v.tensor_copy(startval[:, :, 0:H1], s_dst)
                step(dve, v.tensor_tensor(startval[:, :, H1:2 * H1], s_src, s_dst, ALU.add))
                own = startval[:, :, H1:2 * H1]
                v.scalar_tensor_tensor(out=own, in0=own, scalar=0.2, in1=own, op0=ALU.mult, op1=ALU.max)
        attention(H1, start1_rows, True)
        with nc.Block() as block:
            @block.vector
            def _(dve):
                nc.vector.tensor_copy(pd[:, 0:P], ident[:, :])
        edge_pass(x1_tab, H1 * D, src_idx, keep_row, ALU.mult, ALU.add, "heads")
        gather_results(g, scan_rows, D)
        gather_results(selfw, self_rows, H1)
        half = [weighted_flat[:, 0:2048], weighted_flat[:, 2048:4096]]
        own_rows = arena[:, NT * D:NT * D + NG * H1 * D].rearrange("p (t n) -> p t n", t=NG)
        own_part = arena[:, NT * D + NG * H1 * D:NT * D + NG * H1 * D + NG * D].rearrange("p (t d) -> p t d", d=D)
        with nc.Block() as block:
            @block.sync
            def _(sp):
                with sp.Fori(0, groups) as i:
                    sp.wait_ge(group_turned.sem, group_turned.by_last_lap(i + 1))
                    sp.dma_start(own_rows, x1_tab[bass.ds(i * NG * P, NG * P), :].rearrange("(t p) n -> p t n", p=P)
                                 ).then_inc(loaded.sem, 16)

            @block.vector
            def _(dve):
                v = nc.vector
                with dve.Fori(0, groups) as i:
                    part = g[:, bass.ds(i * NG, NG), :]
                    dve.wait_ge(loaded.sem, loaded.past((i + 1) * 16))
                    for hd in range(H1):
                        v.tensor_tensor(own_part, own_rows[:, :, hd * D:(hd + 1) * D],
                                        selfw[:, bass.ds(i * NG, NG), hd:hd + 1].broadcast_to([P, NG, D]), ALU.mult
                                        ).then_inc(ff_up.sem, 1)
                        dve.wait_ge(ff_up.sem, ff_up.past(i * 2 * H1 + 2 * hd + 1))
                        v.tensor_tensor(part, part, own_part, ALU.add).then_inc(ff_up.sem, 1)
                        dve.wait_ge(ff_up.sem, ff_up.past(i * 2 * H1 + 2 * hd + 2))
                    v.memset(stat[:, 0, 0:1], 0.0).then_inc(group_turned.sem, 1)
                step(dve, v.scalar_tensor_tensor(out=g, in0=g, scalar=1.0 / H1, in1=h[:, :, :], op0=ALU.mult, op1=ALU.add))
                v.tensor_tensor(g, g, across(vec["L1_gnn_bias"][:, :]), ALU.add)
        loaded.base += 16 * groups
        group_turned.base += groups
        ff_up.base += 2 * H1 * groups
        batchnorm(vec["L1_gnn_bn1_w"][:, :], vec["L1_gnn_bn1_b"][:, :], h[:, :, :])
        feed_forward()
        with nc.Block() as block:
            @block.vector
            def _(dve):
                step(dve, nc.vector.tensor_tensor(g, g, across(vec["L1_gnn_b2"][:, :]), ALU.add))
                nc.vector.tensor_tensor(g, g, h[:, :, :], ALU.add)
        batchnorm(vec["L1_gnn_bn2_w"][:, :], vec["L1_gnn_bn2_b"][:, :], g)
        with nc.Block() as block:
            @block.vector
            def _(dve):
                nc.vector.tensor_tensor(x[:, :, :], x[:, :, :], g, ALU.add)

        layernorm_relu(g)
        project([h[:, :, :]], [([w2[:, :]], None, D, lambda j: h_tab[bass.ds(j * P, P), :]),
                               ([sc2[:, :]], None, 2 * H2, nodeval)])
        with nc.Block() as block:
            @block.vector
            def _(dve):
                nc.vector.tensor_copy(startval[:, :, 0:H2], nodeval[:, :, H2:2 * H2])
        attention(H2, start2_rows, False)
        edge_pass(h_tab, D, src_idx, keep_row, ALU.mult, ALU.add, "halves")
        gather_results(g, scan_rows, D)
        with nc.Block() as block:
            @block.vector
            def _(dve):
                v = nc.vector
                step(dve, v.tensor_tensor(g, g, across(vec["L2_gnn_bias"][:, :]), ALU.add))
                step(dve, v.scalar_tensor_tensor(out=g2, in0=g, scalar=0.0, in1=across(vec["L2_gnn_prelu_w"][:, :]),
                                                 op0=ALU.min, op1=ALU.mult))
                step(dve, v.scalar_tensor_tensor(out=g, in0=g, scalar=0.0, in1=g2, op0=ALU.max, op1=ALU.add))
                v.tensor_tensor(x[:, :, :], x[:, :, :], g, ALU.add)

        layernorm_relu(g)
        y_rows = y_tab.rearrange("(r n) d -> n r d", r=R)
        project([h[:, :, :]], [([w3[:, 0:R * D]], b3[0:1, 0:R * D], R * D, lambda j: y_rows[bass.ds(j * P, P), :, :]),
                               ([w3[:, R * D:(R + 1) * D]], b3[0:1, R * D:(R + 1) * D], D, g2)])
        edge_pass(y_tab, D, y_idx, cut_row, ALU.add, ALU.max)
        with nc.Block() as block:
            @block.vector
            def _(dve):
                nc.vector.tensor_tensor(x[:, :, :], x[:, :, :], g2, ALU.add)
        gather_results(g, scan_rows, D)
        with nc.Block() as block:
            @block.vector
            def _(dve):
                nc.vector.tensor_tensor(x[:, :, :], x[:, :, :], g, ALU.add).then_inc(sums_ready.sem, 1)

            @block.sync
            def _(sp):
                sp.wait_ge(sums_ready.sem, sums_ready.past(1))
                sp.dma_start(out[0:(NT - 1) * P, :].rearrange("(j p) d -> p j d", p=P), x[:, 0:NT - 1, :]).then_inc(stored.sem, 16)
                sp.dma_start(out[(NT - 1) * P:N, :], x[0:NL, NT - 1, :]).then_inc(stored.sem, 16)
                sp.wait_ge(stored.sem, stored.past(32))


INPUTS = ["x", "src", "dst", "edge_type_4", "L0_gnn_W1l", "L0_gnn_b1", "L0_gnn_W1r", "L0_gnn_W2l", "L0_gnn_b2", "L0_gnn_W2r",
          "L1_gnn_W", "L1_gnn_att_src", "L1_gnn_att_dst", "L1_gnn_bias", "L1_gnn_bn1_w", "L1_gnn_bn1_b", "L1_gnn_W1",
          "L1_gnn_b1", "L1_gnn_W2", "L1_gnn_b2", "L1_gnn_bn2_w", "L1_gnn_bn2_b", "L2_gnn_W_src", "L2_gnn_W_dst",
          "L2_gnn_att_src", "L2_gnn_att_dst", "L2_gnn_bias", "L2_gnn_prelu_w", "L3_gnn_weight", "L3_gnn_bias"]


def kernel(**inputs):
    import concourse.bacc as bacc
    from concourse.bass_utils import run_bass_kernel_spmd

    nc = bacc.Bacc("TRN2", target_bir_lowering=False, num_devices=1)
    arrays, aps = {}, {}
    for name in INPUTS:
        arrays[f"in_{name}"] = np.ascontiguousarray(inputs[name])
        aps[name] = nc.dram_tensor(f"in_{name}", arrays[f"in_{name}"].shape, mybir.dt.from_np(arrays[f"in_{name}"].dtype),
                                   kind="ExternalInput").ap()
    out = nc.dram_tensor("out", [N, D], F32, kind="ExternalOutput").ap()
    build(nc, aps, out)
    return run_bass_kernel_spmd(nc, [arrays], core_ids=[0]).results[0]["out"]
```

```python
import numpy as np
import concourse.bass as bass
from concourse import mybir
from contextlib import ExitStack

F32 = mybir.dt.float32
BF16 = mybir.dt.bfloat16
I32 = mybir.dt.int32
ALU = mybir.AluOpType
ACT = mybir.ActivationFunctionType
AX = mybir.AxisListType

P = 128
N, D, E = 6250, 128, 100000
NT = -(-N // P)
NP = NT * P
NG = 7
NS = 4
NL = N - (NT - 1) * P
TQ = 7
EC = TQ * P
ER = -(-E // EC)
EP = ER * EC
ET = EP // P
CT = 4
CE = CT * P
NB = 4
CHUNKS = ET // CT
ITERS = CHUNKS // NB
H1, H2, R = 4, 2, 4
FF = 512
HI = -(-NT // 2)
BIG = 3.0e38
LN_EPS = 1e-5
SKIP = EP + 1024


class Chain:

    def __init__(self, sem):
        self.sem, self.n = sem, 0

    def __call__(self, engine, ins):
        self.n += 1
        ins.then_inc(self.sem, 1)
        engine.wait_ge(self.sem, self.n)


class Count:

    def __init__(self, sem, ahead=0):
        self.sem, self.base, self.ahead = sem, 0, ahead

    def past(self, n):
        return n + (self.base + self.ahead)

    def by_last_lap(self, n):
        return n + self.base


class GroupChain:

    def __init__(self, count, wait_apart):
        self.count, self.wait_apart, self.per = count, wait_apart, 0

    def of(self, engine, i, per):
        self.per, at = per, 0

        def step(ins, apart=False):
            nonlocal at
            at += 1
            assert at <= per
            ins.then_inc(self.count.sem, 1)
            if apart:
                self.wait_apart(engine, self.count.sem, self.count.past(i * per + at))
            else:
                engine.wait_ge(self.count.sem, self.count.past(i * per + at))

        return step

    def done(self, laps):
        self.count.base += laps * self.per


def build(nc, a, out):
    assert NT % NG == 0 and ET % CT == 0 and CHUNKS % NB == 0
    groups = NT // NG
    with ExitStack() as ctx:
        def sb(name, shape, dt=F32):
            return ctx.enter_context(nc.sbuf_tensor(name, shape, dt))

        def count(name, ahead=0):
            return Count(ctx.enter_context(nc.semaphore(name)), ahead)

        def dram(name, shape, dt=F32):
            return nc.dram_tensor(name, shape, dt).ap()

        h_tab = dram("h_tab", [NP, D])
        x1_tab = dram("x1_tab", [NP, H1 * D])
        y_tab = dram("y_tab", [R * NP, D])
        scan_rows = dram("scan_rows", [EP + P, D])
        start1_rows = dram("start1_rows", [EP, 2 * H1])
        start2_rows = dram("start2_rows", [EP, H2])
        scan1_rows = dram("scan1_rows", [EP + P, D + H1])
        keep_row = dram("keep_row", [1, EP], BF16)
        cut_row = dram("cut_row", [1, EP], BF16)
        lo_row = dram("lo_row", [1, EP], BF16)

        x = sb("x", [P, NT, D])
        h = sb("h", [P, NT, D])
        arena = sb("arena", [P, 14336])
        g = arena[:, 0:NT * D].rearrange("p (j d) -> p j d", d=D)
        g2 = arena[:, NT * D:2 * NT * D].rearrange("p (j d) -> p j d", d=D)
        weighted = sb("weighted", [P, 2, CT, H1 * P])
        weighted_flat = weighted[:, :, :, :].rearrange("p b t n -> p (b t n)")
        alpha = sb("alpha", [P, ET, H1])
        alpha_flat = alpha[:, :, :].rearrange("p t h -> p (t h)")
        hi_t = alpha_flat[:, 0:ET]
        lo_t = alpha_flat[:, ET:2 * ET]
        src_idx = sb("src_idx", [P, ET + (NB + 1) * CT], I32)
        y_idx = sb("y_idx", [P, ET + (NB + 1) * CT], I32)
        last_idx = sb("last_idx", [P, NT], I32)
        start_idx = sb("start_idx", [P, NT], I32)
        rcount = sb("rcount", [P, NT])
        slot = sb("slot", [P, NB, CT], I32)
        keep = sb("keep", [ER, EC])
        cut = sb("cut", [ER, EC])
        last = sb("last", [ER, EC])
        notlast = sb("notlast", [ER, EC])
        whole = sb("whole", [P, 3, P])
        ends = sb("ends", [ER, 2, P])
        ends_row = sb("ends_row", [P, P])
        carry = sb("carry", [ER, P])
        mask = sb("mask", [P, NB, CE], BF16)
        scan_t = sb("scan_t", [P, 2, CE])
        out_rows = sb("out_rows", [P, 2, CE + CT * H1])
        nodeval = sb("nodeval", [P, NT, 2 * H1])
        startval = sb("startval", [P, NT, 2 * H1])
        stat = sb("stat", [P, 2, NT])
        ln_stat = sb("ln_stat", [P, 2, NG])
        ident = sb("ident", [P, P])
        ones = sb("ones", [P, P])
        ones_tail = sb("ones_tail", [P, P])
        before = sb("before", [NT, NT])
        counts = sb("counts", [64, P])
        startval_slot = sb("startval_slot", [P, 2 * H1])
        number = sb("number", [P, 3])
        his = sb("his", [P, HI])
        parts = sb("parts", [P, 3, H1, 64], BF16)
        w0 = sb("w0", [P, 4, D])
        w1 = sb("w1", [P, H1 * D])
        sc1 = sb("sc1", [P, 2 * H1])
        ff1 = sb("ff1", [P, FF])
        ff2 = sb("ff2", [P, FF // P, D])
        ff1_b = sb("ff1_b", [P, FF // P])
        w2 = sb("w2", [P, D])
        sc2 = sb("sc2", [P, 2 * H2])
        w3 = sb("w3", [P, (R + 1) * D])
        bias_sum = sb("bias_sum", [65, (2 + R + 1) * D], BF16)
        one_rows = sb("one_rows", [65, P], BF16)
        VECS = ["L1_gnn_bias", "L1_gnn_bn1_w", "L1_gnn_bn1_b", "L1_gnn_b2", "L1_gnn_bn2_w", "L1_gnn_bn2_b",
                "L2_gnn_bias", "L2_gnn_prelu_w"]
        vec = {n: sb(n + "_all", [P, D]) for n in VECS}
        mean = sb("mean", [P, D])
        gain = sb("gain", [P, D])

        pa, pb, pc, pd = [ctx.enter_context(nc.psum_tensor(n, [P, 2 * CE], F32)) for n in ("pa", "pb", "pc", "pd")]

        step = Chain(ctx.enter_context(nc.semaphore("vector_step")))
        act_step = Chain(ctx.enter_context(nc.semaphore("scalar_step")))
        pool_step = Chain(ctx.enter_context(nc.semaphore("pool_step")))
        passed = ctx.enter_context(nc.semaphore("passed"))
        cleared = count("cleared")
        loaded = count("loaded")
        stored = count("stored")
        rows_moved = count("rows_moved")
        group_rows = [count(f"group_rows{b}") for b in range(2)]
        group_here = count("group_here")
        own_loaded = [count(f"own_loaded{b}") for b in range(2)]
        turned = count("turned")
        ends_ready = count("ends_ready")
        sums_ready = count("sums_ready")
        gathered = [count(f"gathered{c}") for c in range(NB)]
        idx_staged = count("idx_staged")
        hot_made = [count(f"hot_made{a}", NB) for a in range(2)]
        lo_apart = count("lo_apart")
        picked = count("picked", 2)
        masked = count("masked", NB)
        hi_made = count("hi_made")
        summed = count("summed", 2)
        chunk_weighted = count("chunk_weighted")
        counted = count("counted", 1)
        chunk_turned = count("chunk_turned", NB)
        chunk_scanned = count("chunk_scanned", NB)
        chunk_back = count("chunk_back", 2)
        chunk_copied = count("chunk_copied", 2)
        written = [count(f"written{b}", 16) for b in range(2)]
        mask_loaded = [count(f"mask_loaded{c}") for c in range(NB)]
        group_staged = count("group_staged")
        group_turned = count("group_turned", 1)
        group_lhs = count("group_lhs")
        group_product = count("group_product", 2)
        group_kept = count("group_kept", 2)
        to_scalar = count("to_scalar")
        to_vector = count("to_vector")
        tile_product = count("tile_product")
        tile_out = count("tile_out", 2)
        tile_stored = [count(f"tile_stored{b}", 16) for b in range(NS)]
        ff_up = count("ff_up", 1)
        ff_hidden = count("ff_hidden", 2)
        ff_down = count("ff_down", 1)
        ff_kept = count("ff_kept", 1)

        def wait_apart(engine, sem, value):
            engine.wait_ge(sem, value)
            engine.sem_inc(passed, 1)

        front_step = GroupChain(count("front_step"), wait_apart)
        post_step = GroupChain(count("post_step"), wait_apart)

        dst_i = arena[0:ER, 0:EC].bitcast(I32)
        src_i = arena[0:ER, EC:2 * EC].bitcast(I32)
        rel_i = arena[0:ER, 2 * EC:3 * EC].bitcast(I32)
        dst_f = arena[0:ER, 3 * EC:4 * EC]
        src_f = arena[0:ER, 4 * EC:5 * EC]
        tmp_f = arena[0:ER, 5 * EC:6 * EC]
        tmp_i = arena[0:ER, 6 * EC:7 * EC].bitcast(I32)
        prev_i = arena[0:ER, 7 * EC:7 * EC + 1].bitcast(I32)
        next_i = arena[0:ER, 7 * EC + 1:7 * EC + 2].bitcast(I32)
        prev_f = arena[0:ER, 7 * EC + 2:7 * EC + 3]
        next_f = arena[0:ER, 7 * EC + 3:7 * EC + 4]
        at = 7 * EC + 8

        def take(n):
            nonlocal at
            at += n
            return arena[:, at - n:at]

        raw_b = take((2 + R + 1) * D)[0:65, :]
        raw_w = take(4 * D).rearrange("p (k d) -> p k d", d=D)
        att = take(4 * H1 * D).rearrange("p (k d) -> p k d", d=H1 * D)
        wdst = take(D)
        prod = take(H1 * D)
        prod16 = take((2 + R + 1) * D // 2).bitcast(BF16)
        iota_i = take(P).bitcast(I32)
        number_i = take(1).bitcast(I32)
        lo16 = take(EC // 2).bitcast(BF16)
        keep16 = take(EC // 2).bitcast(BF16)
        cut16 = take(EC // 2).bitcast(BF16)

        ERF, TAIL = E // EC, E % EC
        with nc.Block() as block:
            @block.vector
            def _(dve):
                v = nc.vector
                v.memset(dst_i, N)
                v.memset(src_i, 0)
                v.memset(rel_i, 0)
                v.memset(prev_i, -1)
                v.memset(next_i, -1)
                v.memset(x[:, NT - 1, :], 0.0)
                v.memset(ends[:, :, :], 0.0)
                v.memset(ends_row[:, :], 0.0)
                v.memset(counts[:, :], 0.0)
                v.memset(src_idx[:, ET:], 0)
                v.memset(y_idx[:, ET:], 0)
                v.memset(scan_t[:, 1, :], 0.0)
                v.memset(ones[:, :], 1.0)
                v.memset(out_rows[:, 0, :], 0.0).then_inc(cleared.sem, 1)

            @block.gpsimd
            def _(pool):
                p = nc.gpsimd
                pool_step(pool, p.memset(ident[:, :], 0.0))
                p.affine_select(out=ident[:, :], in_=ident[:, :], compare_op=ALU.not_equal, fill=1.0,
                                base=0, pattern=[[-1, P]], channel_multiplier=1)
                pool_step(pool, p.memset(ones_tail[:, :], 1.0))
                p.affine_select(out=ones_tail[:, :], in_=ones_tail[:, :], compare_op=ALU.is_ge, fill=0.0,
                                base=NL - 1, pattern=[[0, P]], channel_multiplier=-1)
                pool_step(pool, p.memset(before[:, :], 1.0))
                p.affine_select(out=before[:, :], in_=before[:, :], compare_op=ALU.is_gt, fill=0.0,
                                base=0, pattern=[[1, NT]], channel_multiplier=-1)
                p.iota(iota_i, [[1, P]], base=0, channel_multiplier=0)
                p.iota(number_i, [[0, 1]], base=0, channel_multiplier=1)

            @block.tensor
            def _(pe):
                for c in (counted, ff_up, picked, masked, summed, chunk_turned, chunk_back, group_turned, group_product, ff_down):
                    pe.sem_inc(c.sem, c.ahead)

            @block.scalar
            def _(act):
                for c in (*hot_made, chunk_scanned, chunk_copied, *written, tile_out, group_kept, *tile_stored, ff_hidden, ff_kept):
                    act.sem_inc(c.sem, c.ahead)

            @block.sync
            def _(sp):
                loads = 0

                def load(to, of, **single):
                    nonlocal loads
                    loads += 1
                    sp.dma_start(to, of, **single).then_inc(loaded.sem, 16)

                few = {"allow_slow_non_contiguous": True}
                sp.wait_ge(cleared.sem, 1)
                for to, name in ((dst_i, "dst"), (src_i, "src"), (rel_i, "edge_type_4")):
                    load(to[0:ERF, :], a[name][0:ERF * EC].rearrange("(q f) -> q f", f=EC))
                    load(to[ERF:ERF + 1, 0:TAIL], a[name][ERF * EC:E].rearrange("(q f) -> q f", q=1))
                load(prev_i[1:ER, :], a["dst"][0:ERF * EC].rearrange("(q f) -> q f", f=EC)[:, EC - 1:EC], **few)
                load(next_i[0:ER - 2, :], a["dst"][EC:ERF * EC].rearrange("(q f) -> q f", f=EC)[:, 0:1], **few)
                load(next_i[ER - 2:ER - 1, :], a["dst"][ERF * EC:ERF * EC + 1].rearrange("(q f) -> q f", q=1), **few)
                load(x[:, 0:NT - 1, :], a["x"][0:(NT - 1) * P, :].rearrange("(j p) d -> p j d", p=P))
                load(x[0:NL, NT - 1, :], a["x"][(NT - 1) * P:N, :])
                for k, name in enumerate(("L0_gnn_W1l", "L0_gnn_W1r", "L0_gnn_W2l", "L0_gnn_W2r")):
                    load(raw_w[:, k, :], a[name][:, :])
                for k, name in enumerate(("L0_gnn_b1", "L0_gnn_b2")):
                    load(raw_b[:, k * D:(k + 1) * D], a[name].rearrange("(o d) -> o d", o=1).broadcast_to([65, D]))
                load(raw_b[:, 2 * D:], a["L3_gnn_bias"].rearrange("(o r) d -> o (r d)", o=1).broadcast_to([65, (R + 1) * D]))
                load(w1[:, :], a["L1_gnn_W"][:, :])
                load(ff1[:, :], a["L1_gnn_W1"][:, :])
                load(ff2[:, :, :], a["L1_gnn_W2"].rearrange("(k p) d -> p k d", p=P))
                load(ff1_b[:, :], a["L1_gnn_b1"].rearrange("(k p) -> p k", p=P), **few)
                load(w2[:, :], a["L2_gnn_W_src"][:, :])
                load(wdst, a["L2_gnn_W_dst"][:, :])
                load(w3[:, :].rearrange("p (r d) -> p r d", d=D), a["L3_gnn_weight"].rearrange("r p d -> p r d"))
                for name in VECS:
                    load(vec[name][:, :], a[name].rearrange("(o d) -> o d", o=1).broadcast_to([P, D]))
                for k, (name, n) in enumerate((("L1_gnn_att_src", H1 * D), ("L1_gnn_att_dst", H1 * D),
                                               ("L2_gnn_att_src", D), ("L2_gnn_att_dst", D))):
                    load(att[:, k, 0:n], a[name].rearrange("(o h) c -> o (h c)", o=1).broadcast_to([P, n]))
                load(scan_rows[EP:EP + P, :], out_rows[:, 0, 0:D])
                load(scan1_rows[EP:EP + P, 0:D], out_rows[:, 0, 0:D])
                load(scan1_rows[EP:EP + P, D:D + H1], ones[:, 0:H1])
                sp.wait_ge(loaded.sem, 16 * loads)
                loaded.base = 16 * loads
        cleared.base += 1

        def turn_edges(row, tiles):
            with nc.Block() as block:
                @block.tensor
                def _(pe):
                    for f in range(TQ):
                        ins = nc.tensor.transpose(pa[:, f * P:f * P + ER], row[:, f * P:(f + 1) * P], ident[0:ER, 0:ER])
                    ins.then_inc(turned.sem, 1)

                @block.vector
                def _(dve):
                    dve.wait_ge(turned.sem, turned.past(1))
                    nc.vector.tensor_copy(tiles.rearrange("p (q f) -> p f q", f=TQ),
                                          pa[:, 0:TQ * P].rearrange("p (f q) -> p f q", q=P)[:, :, 0:ER])
            turned.base += 1

        with nc.Block() as block:
            @block.vector
            def _(dve):
                v = nc.vector
                v.tensor_copy(dst_f, dst_i)
                v.tensor_copy(src_f, src_i)
                v.tensor_copy(pd[:, 0:P], iota_i)
                v.tensor_copy(his[:, :], iota_i[:, 0:HI])
                step(dve, v.tensor_copy(number[:, 0:1], number_i))
                v.tensor_scalar(number[:, 1:2], number[:, 0:1], float(P), None, ALU.add)
                v.tensor_scalar(number[:, 2:3], number[:, 0:1], -1.0, None, ALU.mult)
                v.memset(parts[:, :, :, :], 0.0)
                v.memset(bias_sum[:, :], 0.0)
                v.memset(one_rows[:, :], 1.0)
                step(dve, v.tensor_single_scalar(tmp_i, src_i, 2 * P - 1, ALU.bitwise_and))
                v.tensor_copy(lo16[0:ER, :], tmp_i)
                v.tensor_copy(prev_f, prev_i)
                step(dve, v.tensor_copy(next_f, next_i))
                v.tensor_tensor(keep[:, 1:EC], dst_f[:, 1:EC], dst_f[:, 0:EC - 1], ALU.is_equal)
                v.tensor_tensor(keep[:, 0:1], dst_f[:, 0:1], prev_f, ALU.is_equal)
                v.tensor_tensor(notlast[:, 0:EC - 1], dst_f[:, 0:EC - 1], dst_f[:, 1:EC], ALU.is_equal)
                step(dve, v.tensor_tensor(notlast[:, EC - 1:EC], dst_f[:, EC - 1:EC], next_f, ALU.is_equal))
                v.tensor_scalar(cut[:, :], keep[:, :], -1.0, BIG, ALU.add, ALU.mult)
                v.tensor_scalar(last[:, :], notlast[:, :], -1.0, 1.0, ALU.mult, ALU.add)
                v.tensor_copy(keep16[0:ER, :], keep[:, :])
                v.tensor_scalar(cut16[0:ER, :], keep[:, :], -1.0, BIG, ALU.add, ALU.mult)
                v.scalar_tensor_tensor(out=tmp_f, in0=rel_i, scalar=float(NP), in1=src_f, op0=ALU.mult, op1=ALU.add)
                v.tensor_reduce(carry[:, 0:1], keep[:, :], AX.X, ALU.min)
                step(dve, v.tensor_reduce(carry[:, 1:2], notlast[:, :], AX.X, ALU.min))
                for k in range(2):
                    v.tensor_copy(ends[:, k, 0:2 * H1], carry[:, k:k + 1].broadcast_to([ER, 2 * H1]))
                part16 = prod16[0:65, :]
                for k in range(3):
                    step(dve, v.tensor_copy(part16, raw_b))
                    v.tensor_copy(bias_sum[32 * k:32 * k + 1, :], part16[32 * k:32 * k + 1, :])
                    step(dve, v.tensor_tensor(raw_b, raw_b, part16, ALU.subtract))
                for k, (w, to, heads, c) in enumerate(((w1[:, :], sc1[:, 0:H1], H1, D), (w1[:, :], sc1[:, H1:2 * H1], H1, D),
                                                       (w2[:, :], sc2[:, 0:H2], H2, D // H2),
                                                       (wdst, sc2[:, H2:2 * H2], H2, D // H2))):
                    step(dve, v.tensor_tensor(prod[:, 0:heads * c], w[:, 0:heads * c], att[:, k, 0:heads * c], ALU.mult))
                    step(dve, v.tensor_reduce(to, prod[:, 0:heads * c].rearrange("p (h c) -> p h c", c=c), AX.X, ALU.add))

            @block.tensor
            def _(pe):
                for k in range(4):
                    ins = nc.tensor.transpose(pb[:, k * D:(k + 1) * D], raw_w[:, k, :], ident[:, :])
                ins.then_inc(turned.sem, 1)

            @block.scalar
            def _(act):
                act.wait_ge(turned.sem, turned.past(1))
                nc.scalar.copy(w0[:, :, :], pb[:, 0:4 * D].rearrange("p (k d) -> p k d", d=D))
        turned.base += 1

        with nc.Block() as block:
            @block.tensor
            def _(pe):
                nc.tensor.transpose(pa[:, 0:ER], ends[:, 0, :], ident[0:ER, 0:ER])
                nc.tensor.transpose(pa[:, P:P + ER], ends[:, 1, :], ident[0:ER, 0:ER]).then_inc(turned.sem, 1)

            @block.vector
            def _(dve):
                dve.wait_ge(turned.sem, turned.past(1))
                nc.vector.tensor_copy(whole[:, 0, 0:ER], pa[:, 0:ER])
                nc.vector.tensor_scalar(whole[:, 1, 0:ER], pa[:, 0:ER], -1.0, BIG, ALU.add, ALU.mult)
                nc.vector.tensor_copy(whole[:, 2, 0:ER], pa[:, P:P + ER])

            @block.sync
            def _(sp):
                sp.dma_start(keep_row.rearrange("o (q f) -> (o q) f", f=EC), keep16[0:ER, :]).then_inc(stored.sem, 16)
                sp.dma_start(cut_row.rearrange("o (q f) -> (o q) f", f=EC), cut16[0:ER, :]).then_inc(stored.sem, 16)
                sp.dma_start(lo_row.rearrange("o (q f) -> (o q) f", f=EC), lo16[0:ER, :]).then_inc(stored.sem, 16)
                sp.wait_ge(stored.sem, stored.past(48))
        turned.base += 1
        stored.base += 48
        turn_edges(src_f, src_idx[:, 0:ET])
        turn_edges(tmp_f, y_idx[:, 0:ET])
        for op, by, tiles in ((ALU.arith_shift_right, 7, hi_t), (ALU.bitwise_and, P - 1, lo_t)):
            with nc.Block() as block:
                @block.vector
                def _(dve):
                    step(dve, nc.vector.tensor_single_scalar(tmp_i, dst_i, by, op))
                    nc.vector.tensor_copy(tmp_f, tmp_i)
            turn_edges(tmp_f, tiles)

        def laps(engine, first, body):
            first()
            with engine.Fori(0, ITERS - 1) as i:
                for c in range(NB):
                    body(i, c, True)
            for c in range(NB):
                body(ITERS - 1, c, c < NB - 1)

        def edge_pass(table, width, idx, mask_row, op0, op1, mode="plain"):
            beside = H1 if mode == "heads" else 0
            target = scan1_rows if beside else scan_rows

            def written_rows(b):
                return out_rows[:, b, 0:CT * (D + beside)].rearrange("p (t d) -> p t d", d=D + beside)

            def rows(c, t):
                n = (c * CT + t) * width
                return arena[:, n:n + width]

            def hot(b):
                both = weighted_flat[:, b * CT * H1 * P:b * CT * H1 * P + CT * (64 + P) // 2].bitcast(BF16)
                return (both[:, 0:CT * 64].rearrange("p (t k) -> p t k", k=64),
                        both[:, CT * 64:CT * (64 + P)].rearrange("p (t k) -> p t k", k=P))

            with nc.Block() as block:
                @block.gpsimd
                def _(pool):
                    with pool.Fori(0, ITERS) as i:
                        for c in range(NB):
                            wait_apart(pool, idx_staged.sem, idx_staged.past(i * NB + c + 1))
                            for t in range(CT):
                                nc.gpsimd.indirect_dma_start(
                                    out=rows(c, t), out_offset=None, in_=table[:, :],
                                    in_offset=bass.IndirectOffsetOnAxis(ap=slot[:, c, t:t + 1], axis=0)
                                ).then_inc(gathered[c].sem, 16)

                @block.sync
                def _(sp):
                    if mode == "count":
                        for rows_, width_ in ((start1_rows, 2 * H1), (start2_rows, H2)):
                            n = EP * width_ // P // ER
                            sp.dma_start(rows_.rearrange("(p e) w -> p (e w)", p=P).rearrange("p (k f) -> p k f", f=ER),
                                         ends_row[:, 0:ER].unsqueeze(1).broadcast_to([P, n, ER])).then_inc(stored.sem, 16)
                    with sp.Fori(0, ITERS) as i:
                        for c in range(NB):
                            k = i * NB + c
                            sp.wait_ge(chunk_scanned.sem, chunk_scanned.by_last_lap(k + 1))
                            sp.dma_start(mask[:, c, :], mask_row[0:1, bass.ds(k * CE, CE)].broadcast_to([P, CE])
                                         ).then_inc(mask_loaded[c].sem, 16)
                    if mode == "count":
                        sp.wait_ge(stored.sem, stored.past(32))

                @block.vector
                def _(dve):
                    v = nc.vector

                    def weigh(i, c):
                        k, b = i * NB + c, c % 2
                        if mode == "plain":
                            return
                        dve.wait_ge(chunk_turned.sem, chunk_turned.by_last_lap(k + NB - 1))
                        if mode == "count":
                            hot_hi, hot_lo = hot(b)
                            v.tensor_tensor(hot_hi, pd[:, 0:64].unsqueeze(1).broadcast_to([P, CT, 64]),
                                            hi_t[:, bass.ds(k * CT, CT)].unsqueeze(2).broadcast_to([P, CT, 64]), ALU.is_equal)
                            v.tensor_tensor(hot_lo, pd[:, 0:P].unsqueeze(1).broadcast_to([P, CT, P]),
                                            lo_t[:, bass.ds(k * CT, CT)].unsqueeze(2).broadcast_to([P, CT, P]), ALU.is_equal
                                            ).then_inc(chunk_weighted.sem, 1)
                        elif mode == "heads":
                            for t in range(CT):
                                ins = v.tensor_tensor(
                                    weighted[:, b, t, :].rearrange("p (h n) -> p h n", n=P),
                                    pd[:, 0:P].unsqueeze(1).broadcast_to([P, H1, P]),
                                    alpha_flat[:, bass.ds((k * CT + t) * H1, H1)].unsqueeze(2).broadcast_to([P, H1, P]), ALU.mult)
                            ins.then_inc(chunk_weighted.sem, 1)
                        else:
                            dve.wait_ge(gathered[c % NB].sem, gathered[c % NB].past((i + c // NB + 1) * 16 * CT))
                            half = D // H2
                            n = (c % NB) * CT * width
                            v.tensor_tensor(
                                weighted[:, b, :, 0:D].rearrange("p t (h n) -> p t h n", n=half),
                                arena[:, n:n + CT * width].rearrange("p (t h n) -> p t h n", h=H2, n=half),
                                alpha[:, bass.ds(k * CT, CT), 0:H2].unsqueeze(3).broadcast_to([P, CT, H2, half]), ALU.mult
                            ).then_inc(chunk_weighted.sem, 1)

                    def scan(i, c, more):
                        if more:
                            weigh(i, c + 1)
                        k, b = i * NB + c, c % 2
                        dve.wait_ge(chunk_turned.sem, chunk_turned.past(k + 1))
                        if mode == "count":
                            dve.wait_ge(counted.sem, counted.past(k))
                            v.tensor_tensor(counts[:, :], counts[:, :], pc[0:64, b * CE:b * CE + P], ALU.add
                                            ).then_inc(counted.sem, 1)
                        dve.wait_ge(mask_loaded[c].sem, mask_loaded[c].past((i + 1) * 16))
                        dve.wait_ge(chunk_back.sem, chunk_back.by_last_lap(k + 1))
                        dve.wait_ge(chunk_scanned.sem, chunk_scanned.past(k))
                        v.tensor_tensor_scan(scan_t[:, b, :], mask[:, c, :], pa[:, b * CE:(b + 1) * CE],
                                             scan_t[:, 1 - b, CE - 1:CE], op0, op1).then_inc(chunk_scanned.sem, 1)

                    laps(dve, lambda: weigh(0, 0), scan)

                @block.tensor
                def _(pe):
                    def turn(i, c):
                        k, b, s = i * NB + c, c % 2, c % NB
                        if mode != "plain":
                            pe.wait_ge(chunk_weighted.sem, chunk_weighted.past(k + 1))
                        if mode != "halves":
                            pe.wait_ge(gathered[s].sem, gathered[s].past((i + c // NB + 1) * 16 * CT))
                        pe.wait_ge(chunk_scanned.sem, chunk_scanned.past(k - 1))
                        if mode == "count":
                            hot_hi, hot_lo = hot(b)
                            for t in range(CT):
                                nc.tensor.matmul(pc[0:64, b * CE:b * CE + P], hot_hi[:, t, :], hot_lo[:, t, :],
                                                 start=(t == 0), stop=(t == CT - 1))
                        for t in range(CT):
                            to = pa[:, b * CE + t * P:b * CE + (t + 1) * P]
                            if mode == "heads":
                                for hd in range(H1):
                                    ins = nc.tensor.matmul(to, rows(s, t)[:, hd * D:(hd + 1) * D],
                                                           weighted[:, b, t, hd * P:(hd + 1) * P],
                                                           start=(hd == 0), stop=(hd == H1 - 1))
                            elif mode == "halves":
                                ins = nc.tensor.transpose(to, weighted[:, b, t, 0:D], ident[:, :])
                            else:
                                ins = nc.tensor.transpose(to, rows(s, t), ident[:, :])
                        ins.then_inc(chunk_turned.sem, 1)

                    def back(i, c, more):
                        if more:
                            turn(i, c + 1)
                        k, b = i * NB + c, c % 2
                        pe.wait_ge(chunk_scanned.sem, chunk_scanned.past(k + 1))
                        pe.wait_ge(chunk_copied.sem, chunk_copied.by_last_lap(k + 1))
                        for t in range(CT):
                            ins = nc.tensor.transpose(pb[:, b * CE + t * P:b * CE + (t + 1) * P],
                                                      scan_t[:, b, t * P:(t + 1) * P], ident[:, :])
                        ins.then_inc(chunk_back.sem, 1)

                    laps(pe, lambda: turn(0, 0), back)

                @block.scalar
                def _(act):
                    def stage_numbers(k, c):
                        nc.scalar.copy(slot[:, c, :], idx[:, bass.ds(k * CT, CT)]).then_inc(idx_staged.sem, 1)

                    for c in range(NB):
                        stage_numbers(c, c)
                    wait_apart(act, chunk_turned.sem, chunk_turned.past(1))
                    stage_numbers(NB, 0)
                    with act.Fori(0, ITERS) as i:
                        for c in range(NB):
                            k, b = i * NB + c, c % 2
                            act.wait_ge(chunk_back.sem, chunk_back.past(k + 1))
                            act.wait_ge(written[b].sem, written[b].by_last_lap((i * 2 + c // 2 + 1) * 16))
                            ins = nc.scalar.copy(written_rows(b)[:, :, 0:D],
                                                 pb[:, b * CE:(b + 1) * CE].rearrange("p (t d) -> p t d", d=D))
                            if beside:
                                ins = nc.scalar.copy(written_rows(b)[:, :, D:D + beside], own_t[:, bass.ds(k * CT, CT), :])
                            ins.then_inc(chunk_copied.sem, 1)
                            act.wait_ge(chunk_copied.sem, chunk_copied.past(k + 1))
                            act.dma_start(target[bass.ds(k * CE, CE), :].rearrange("(t p) d -> p t d", p=P), written_rows(b)
                                          ).then_inc(written[b].sem, 16)
                            stage_numbers(k + 1 + NB, (c + 1) % NB)
                    for b in range(2):
                        act.wait_ge(written[b].sem, written[b].past(16 * CHUNKS // 2))
            idx_staged.base += CHUNKS + NB + 1
            if mode == "count":
                stored.base += 32
            for c in gathered:
                c.base += 16 * CT * ITERS
            for c in (chunk_turned, chunk_scanned, chunk_back, chunk_copied):
                c.base += CHUNKS
            if mode != "plain":
                chunk_weighted.base += CHUNKS
            for w in written:
                w.base += 16 * CHUNKS // 2
            for m in mask_loaded:
                m.base += 16 * ITERS

        def gather_results(pool, to, table, width):
            def arrived(i):
                pool.wait_ge(group_rows[i % 2].sem, group_rows[i % 2].past((i // 2 + 1) * 16 * NG))
                pool.sem_inc(group_here.sem, 1)

            for i in range(groups):
                for j in range(i * NG, (i + 1) * NG):
                    nc.gpsimd.indirect_dma_start(out=to[:, j, 0:width], out_offset=None, in_=table[:, :],
                                                 in_offset=bass.IndirectOffsetOnAxis(ap=last_idx[:, j:j + 1], axis=0)
                                                 ).then_inc(group_rows[i % 2].sem, 16)
                if i > 0:
                    arrived(i - 1)
            arrived(groups - 1)

        def results_gathered():
            for b in range(2):
                group_rows[b].base += 16 * NG * ((groups + 1 - b) // 2)
            group_here.base += groups

        def wide(t):
            return t.unsqueeze(2).broadcast_to([P, NT, D])

        def across(t):
            return t.unsqueeze(1).broadcast_to([P, NT, D])

        def layernorm_relu(tmp):
            with nc.Block() as block:
                @block.vector
                def _(dve):
                    v = nc.vector
                    step(dve, v.tensor_reduce(stat[:, 0, :], x[:, :, :], AX.X, ALU.add))
                    step(dve, v.tensor_scalar(stat[:, 0, :], stat[:, 0, :], 1.0 / D, None, ALU.mult))
                    step(dve, v.tensor_tensor(h[:, :, :], x[:, :, :], wide(stat[:, 0, :]), ALU.subtract))
                    step(dve, v.tensor_tensor(tmp, h[:, :, :], h[:, :, :], ALU.mult))
                    step(dve, v.tensor_reduce(stat[:, 1, :], tmp, AX.X, ALU.add))
                    v.tensor_scalar(stat[:, 1, :], stat[:, 1, :], 1.0 / D, LN_EPS, ALU.mult, ALU.add).then_inc(sums_ready.sem, 1)
                    dve.wait_ge(sums_ready.sem, sums_ready.past(2))
                    step(dve, v.reciprocal(stat[:, 0, :], stat[:, 1, :]))
                    v.scalar_tensor_tensor(out=h[:, :, :], in0=h[:, :, :], scalar=0.0, in1=wide(stat[:, 0, :]),
                                           op0=ALU.max, op1=ALU.mult)

                @block.scalar
                def _(act):
                    act.wait_ge(sums_ready.sem, sums_ready.past(1))
                    nc.scalar.activation(stat[:, 1, :], stat[:, 1, :], ACT.Sqrt).then_inc(sums_ready.sem, 1)
            sums_ready.base += 2

        def store_rows(table, rows):
            with nc.Block() as block:
                @block.sync
                def _(sp):
                    sp.dma_start(table.rearrange("(j p) d -> p j d", p=P), rows).then_inc(stored.sem, 16)
                    sp.wait_ge(stored.sem, stored.past(16))
            stored.base += 16

        def stage(s):
            return weighted_flat[:, s * NG * P:(s + 1) * NG * P]

        def lhs(s):
            return weighted_flat[:, (2 + s) * NG * P:(3 + s) * NG * P]

        def group_steps(engine, begin, step):
            begin()
            with engine.Fori(0, (groups - 2) // 2) as pair:
                for b in range(2):
                    step(pair * 2 + b, b, 2)
            for i in range((groups - 2) // 2 * 2, groups):
                step(i, i % 2, min(groups - 1 - i, 2))

        def project(ns, front, by_tile, by_group, post, begin=None, scalar_front=None, scalar_post=None, gathers=None, store=None,
                    buffers=None):
            turns = (pa, pd)

            def uses(buf):
                return (NG - buf + NS - 1) // NS

            def turned_input(s, b):
                if ns == 1:
                    return weighted_flat[:, (1 + b) * NG * P:(2 + b) * NG * P]
                return weighted_flat[:, (2 + s) * NG * P:(3 + s) * NG * P] if b == 0 else more_lhs[s]

            with nc.Block() as block:
                if gathers is not None:
                    @block.gpsimd
                    def _(pool):
                        gathers(pool)

                @block.vector
                def _(dve):
                    def begin_fronts():
                        front(dve, 0)
                        front(dve, 1)

                    def step(i, b, left):
                        if left > 1:
                            front(dve, i + 2)
                        dve.wait_ge(group_product.sem, group_product.past(i + 1))
                        post(dve, i, b)

                    group_steps(dve, begin_fronts, step)

                @block.tensor
                def _(pe):
                    def turn(i, first=False):
                        pe.wait_ge(group_staged.sem, group_staged.past((i + 1) * ns))
                        if not first:
                            pe.wait_ge(group_lhs.sem, group_lhs.past(i))
                        for s in range(ns):
                            for t in range(NG):
                                ins = nc.tensor.transpose(turns[s][:, t * P:(t + 1) * P], stage(s)[:, t * P:(t + 1) * P], ident[:, :])
                        ins.then_inc(group_turned.sem, 1)

                    def multiply(i, b):
                        pe.wait_ge(group_lhs.sem, group_lhs.past(i + 1))
                        pe.wait_ge(group_kept.sem, group_kept.past(i if by_tile is not None else i - 1))
                        for t in range(NG):
                            if by_tile is not None:
                                ws, bias, n, _ = by_tile
                                pe.wait_ge(tile_out.sem, tile_out.by_last_lap(i * NG + (t + 1 if t > 1 else 2 - t)))
                                to = pb[:, t % 2 * CE:t % 2 * CE + n]
                                ins = nc.tensor.matmul(to, turned_input(0, b)[:, t * P:(t + 1) * P], ws, start=True, stop=(bias is None))
                                if bias is not None:
                                    ins = nc.tensor.matmul(to, one_rows[:, :], bias, start=False, stop=True)
                                ins.then_inc(tile_product.sem, 1)
                            ws, bias, n = by_group
                            to = products(b if by_tile is None else 0)[:, t * n:(t + 1) * n]
                            for s in range(ns):
                                ins = nc.tensor.matmul(to, turned_input(s, b)[:, t * P:(t + 1) * P], ws[s],
                                                       start=(s == 0), stop=(bias is None and s == ns - 1))
                            if bias is not None:
                                ins = nc.tensor.matmul(to, one_rows[:, :], bias, start=False, stop=True)
                        ins.then_inc(group_product.sem, 1)

                    def step(i, b, left):
                        if left > 0:
                            turn(i + 1)
                        multiply(i, b)

                    group_steps(pe, lambda: turn(0, True), step)

                @block.scalar
                def _(act):
                    def keep(i, b):
                        act.wait_ge(group_turned.sem, group_turned.past(i + 1))
                        act.wait_ge(group_product.sem, group_product.past(i - 1))
                        for s in range(ns):
                            ins = nc.scalar.copy(turned_input(s, b), turns[s][:, 0:NG * P])
                        ins.then_inc(group_lhs.sem, 1)

                    def copy_product(i, t):
                        n, b, buf = by_tile[2], t % 2, t % NS
                        act.wait_ge(tile_product.sem, tile_product.past(i * NG + t + 1))
                        use = i * uses(buf) + t // NS
                        act.wait_ge(tile_stored[buf].sem, tile_stored[buf].by_last_lap(use * 16 + 16))
                        nc.scalar.copy(buffers[:, buf * CE:buf * CE + n], pb[:, b * CE:b * CE + n]).then_inc(tile_out.sem, 1)

                    def begin_groups():
                        if begin is not None:
                            begin(act)
                        scalar_front(act, 0)
                        keep(0, 0)
                        scalar_front(act, 1)

                    def step(i, b, left):
                        if left > 0:
                            keep(i + 1, 1 - b)
                        if by_tile is not None:
                            for t in range(NG):
                                if t == NG // 2 and left > 1:
                                    scalar_front(act, i + 2)
                                copy_product(i, t)
                        else:
                            if left > 1:
                                scalar_front(act, i + 2)
                            act.wait_ge(group_product.sem, group_product.past(i + 1))
                            scalar_post(act, i, b)

                    group_steps(act, begin_groups, step)

                @block.sync
                def _(sp):
                    if by_tile is not None:
                        n, rows = by_tile[2:]
                        with sp.Fori(0, groups) as i:
                            for t in range(NG):
                                buf = t % NS
                                sp.wait_ge(tile_out.sem, tile_out.past(i * NG + t + 1))
                                to, kept = rows(i * NG + t), buffers[:, buf * CE:buf * CE + n]
                                sp.dma_start(to, kept if len(to.shape) == 2 else kept.rearrange("p (r d) -> p r d", d=D)
                                             ).then_inc(tile_stored[buf].sem, 16)
                        for buf in range(NS):
                            sp.wait_ge(tile_stored[buf].sem, tile_stored[buf].past(16 * uses(buf) * groups))
                    if store is not None:
                        store(sp)
            group_staged.base += ns * groups
            for c in (group_turned, group_lhs, group_product, group_kept):
                c.base += groups
            if by_tile is not None:
                tile_product.base += NT
                tile_out.base += NT
                for buf in range(NS):
                    tile_stored[buf].base += 16 * uses(buf) * groups
            if gathers is not None:
                results_gathered()

        def products(b):
            return (pc, pb)[b]

        def middle(t, i):
            return t[:, bass.ds(i * NG, NG), :]

        def group_wide(t):
            return t.unsqueeze(2).broadcast_to([P, NG, D])

        def group_across(t):
            return t.unsqueeze(1).broadcast_to([P, NG, D])

        def as_tiles(t):
            return t.rearrange("p (t d) -> p t d", d=D)

        LN_STEPS = 6

        def layernorm_group(dve, step, i, x_i, outs):
            v = nc.vector
            mu, var = ln_stat[:, 0, :], ln_stat[:, 1, :]
            step(v.tensor_reduce(mu, x_i, AX.X, ALU.add))
            step(v.tensor_scalar(mu, mu, 1.0 / D, None, ALU.mult))
            if not (isinstance(i, int) and i == 0):
                dve.wait_ge(group_staged.sem, group_staged.past(i))
            step(v.tensor_tensor(as_tiles(T1), x_i, group_wide(mu), ALU.subtract))
            step(v.tensor_tensor(T2, T1, T1, ALU.mult))
            step(v.tensor_reduce(var, as_tiles(T2), AX.X, ALU.add))
            v.tensor_scalar(var, var, 1.0 / D, LN_EPS, ALU.mult, ALU.add).then_inc(to_scalar.sem, 1)
            dve.wait_ge(to_vector.sem, to_vector.past(i + 1))
            step(v.reciprocal(mu, var))
            dve.wait_ge(group_turned.sem, group_turned.by_last_lap(i + 1))
            for to in outs:
                ins = v.scalar_tensor_tensor(out=to, in0=as_tiles(T1), scalar=0.0, in1=group_wide(mu), op0=ALU.max, op1=ALU.mult)
            ins.then_inc(group_staged.sem, 1)

        def deviations(act, i):
            act.wait_ge(to_scalar.sem, to_scalar.past(i + 1))
            nc.scalar.activation(ln_stat[:, 1, :], ln_stat[:, 1, :], ACT.Sqrt).then_inc(to_vector.sem, 1)

        def feed_forward():
            hidden = [arena[:, NT * D + k * NG * P:NT * D + (k + 1) * NG * P] for k in range(FF // P)]
            nk = FF // P
            ups = (pb, pd)

            with nc.Block() as block:
                @block.gpsimd
                def _(pool):
                    with pool.Fori(0, groups) as i:
                        wait_apart(pool, group_turned.sem, group_turned.by_last_lap(i + 1))
                        nc.gpsimd.tensor_copy(stage(0).rearrange("p (t d) -> p t d", d=D), h[:, bass.ds(i * NG, NG), :]
                                              ).then_inc(group_staged.sem, 1)

                @block.tensor
                def _(pe):
                    with pe.Fori(0, groups) as i:
                        pe.wait_ge(group_staged.sem, group_staged.past(i + 1))
                        for t in range(NG):
                            ins = nc.tensor.transpose(pa[:, t * P:(t + 1) * P], stage(0)[:, t * P:(t + 1) * P], ident[:, :])
                        ins.then_inc(group_turned.sem, 1)
                        pe.wait_ge(group_lhs.sem, group_lhs.past(i + 1))
                        for k in range(nk):
                            pe.wait_ge(ff_hidden.sem, ff_hidden.by_last_lap(i * nk + k + 1))
                            for lo, hi in ((0, CE), (CE, NG * P)):
                                ins = nc.tensor.matmul(ups[k % 2][:, lo:hi], ff1[:, k * P:(k + 1) * P], lhs(0)[:, lo:hi],
                                                       start=True, stop=True)
                            ins.then_inc(ff_up.sem, 1)
                        pe.wait_ge(ff_hidden.sem, ff_hidden.past((i + 1) * nk))
                        pe.wait_ge(ff_kept.sem, ff_kept.by_last_lap(i + 1))
                        for t in range(NG):
                            for k in range(nk):
                                ins = nc.tensor.matmul(pc[:, t * P:(t + 1) * P], hidden[k][:, t * P:(t + 1) * P], ff2[:, k, :],
                                                       start=(k == 0), stop=(k == nk - 1))
                        ins.then_inc(ff_down.sem, 1)

                @block.scalar
                def _(act):
                    with act.Fori(0, groups) as i:
                        for k in range(nk):
                            act.wait_ge(ff_down.sem, ff_down.by_last_lap(i + 1))
                            act.wait_ge(ff_up.sem, ff_up.past(i * nk + k + 1))
                            nc.scalar.activation(hidden[k], ups[k % 2][:, 0:NG * P], ACT.Relu, bias=ff1_b[:, k:k + 1]
                                                 ).then_inc(ff_hidden.sem, 1)

                @block.vector
                def _(dve):
                    with dve.Fori(0, groups) as i:
                        dve.wait_ge(ff_up.sem, ff_up.past(i * nk))
                        dve.wait_ge(group_turned.sem, group_turned.past(i + 1))
                        nc.vector.tensor_copy(lhs(0), pa[:, 0:NG * P]).then_inc(group_lhs.sem, 1)
                        dve.wait_ge(ff_down.sem, ff_down.past(i + 1))
                        nc.vector.tensor_copy(g[:, bass.ds(i * NG, NG), :], pc[:, 0:NG * P].rearrange("p (t d) -> p t d", d=D)
                                              ).then_inc(ff_kept.sem, 1)
            group_staged.base += groups
            group_turned.base += groups
            group_lhs.base += groups
            ff_up.base += nk * groups
            ff_hidden.base += nk * groups
            ff_down.base += groups
            ff_kept.base += groups

        def column_sums(rows):
            four = NT - 1 - (NT - 1) % 4
            assert four == NT - 1
            with nc.Block() as block:
                @block.tensor
                def _(pe):
                    nc.tensor.matmul(pa[:, 0:4 * D], ones[:, :], rows[:, 0:4, :].rearrange("p j d -> p (j d)"), start=True, stop=False)
                    with pe.Fori(1, NT // 4) as j:
                        nc.tensor.matmul(pa[:, 0:4 * D], ones[:, :], rows[:, bass.ds(j * 4, 4), :].rearrange("p j d -> p (j d)"),
                                         start=False, stop=False)
                    nc.tensor.matmul(pa[:, 0:D], ones_tail[:, :], rows[:, NT - 1, :], start=False, stop=True)

        def summed_columns():
            return pa[:, 0:4 * D].rearrange("p (k d) -> p d k", d=D)

        def batchnorm(rows, w):
            column_sums(rows)
            with nc.Block() as block:
                @block.vector
                def _(dve):
                    v = nc.vector
                    step(dve, v.tensor_reduce(mean[:, :], summed_columns(), AX.X, ALU.add))
                    step(dve, v.tensor_scalar(mean[:, :], mean[:, :], 1.0 / N, None, ALU.mult))
                    step(dve, v.tensor_tensor(g2, rows, across(mean[:, :]), ALU.subtract))
                    v.tensor_tensor(rows, g2, g2, ALU.mult)
            column_sums(rows)
            with nc.Block() as block:
                @block.vector
                def _(dve):
                    v = nc.vector
                    step(dve, v.tensor_reduce(gain[:, :], summed_columns(), AX.X, ALU.add))
                    v.tensor_scalar(gain[:, :], gain[:, :], 1.0 / N, LN_EPS, ALU.mult, ALU.add).then_inc(sums_ready.sem, 1)
                    dve.wait_ge(sums_ready.sem, sums_ready.past(2))
                    step(dve, v.reciprocal(mean[:, :], gain[:, :]))
                    v.tensor_tensor(mean[:, :], mean[:, :], w, ALU.mult)

                @block.scalar
                def _(act):
                    act.wait_ge(sums_ready.sem, sums_ready.past(1))
                    nc.scalar.activation(gain[:, :], gain[:, :], ACT.Sqrt).then_inc(sums_ready.sem, 1)
            sums_ready.base += 2

        EA = weighted_flat[0:ER, 0:H1 * EC].rearrange("q (h f) -> q h f", f=EC)
        FROM_DST = arena[0:ER, 0:2 * H1 * EC].rearrange("q (h f) -> q h f", f=EC)
        START = arena[0:ER, 2 * H1 * EC:4 * H1 * EC]
        M = arena[0:ER, 2 * H1 * EC:3 * H1 * EC].rearrange("q (h f) -> q h f", f=EC)
        own_t = arena[:, 8192:8192 + ET * H1].rearrange("p (t h) -> p t h", h=H1)
        DEN = arena[0:ER, 3 * H1 * EC:4 * H1 * EC].rearrange("q (h f) -> q h f", f=EC)

        def segment_scan(n, to, of, kind):
            with_, flag, op0, op1, start = {"sum": (keep, 0, ALU.mult, ALU.add, 0.0),
                                            "max": (cut, 1, ALU.add, ALU.max, -BIG),
                                            "spread": (notlast, 2, ALU.mult, ALU.add, 0.0)}[kind]
            way = slice(None, None, -1) if kind == "spread" else slice(None)
            end = 0 if kind == "spread" else EC - 1
            into = (0, ER) if kind == "spread" else (1, ER + 1)
            out_of = (1, ER + 1) if kind == "spread" else (0, ER)

            with nc.Block() as block:
                @block.vector
                def _(dve):
                    v = nc.vector
                    for k in range(n):
                        step(dve, v.tensor_tensor_scan(to(k)[:, way], with_[:, way], of(k)[:, way], start, op0, op1))
                        v.tensor_copy(ends[:, 0, k:k + 1], to(k)[:, end:end + 1])
                    v.memset(ends_row[:, 0:1], start)
                    v.memset(ends_row[:, ER:ER + 1], start).then_inc(ends_ready.sem, 1)
                    dve.wait_ge(turned.sem, turned.past(1))
                    v.tensor_tensor_scan(ends_row[0:n, into[0]:into[1]][:, way], whole[0:n, flag, 0:ER][:, way],
                                         pa[0:n, 0:ER][:, way], start, op0, op1).then_inc(ends_ready.sem, 1)
                    dve.wait_ge(turned.sem, turned.past(2))
                    step(dve, v.tensor_copy(carry[:, 0:n], pb[0:ER, 0:n]))
                    for k in range(n):
                        v.tensor_tensor_scan(to(k)[:, way], with_[:, way], of(k)[:, way], carry[:, k:k + 1], op0, op1)

                @block.tensor
                def _(pe):
                    pe.wait_ge(ends_ready.sem, ends_ready.past(1))
                    nc.tensor.transpose(pa[:, 0:ER], ends[:, 0, :], ident[0:ER, 0:ER]).then_inc(turned.sem, 1)
                    pe.wait_ge(ends_ready.sem, ends_ready.past(2))
                    nc.tensor.transpose(pb[0:ER, 0:P], ends_row[:, out_of[0]:out_of[1]], ident[:, :]).then_inc(turned.sem, 1)
            ends_ready.base += 2
            turned.base += 2

        def look_up_scores(heads, start_rows, width):
            hots = weighted_flat[:, 0:2 * CE].bitcast(BF16).rearrange("p (b a n) -> p b a n", b=2, a=2)
            hot_hi = weighted_flat[:, 2 * CE:2 * CE + 2 * CT * HI].rearrange("p (b t j) -> p b t j", b=2, t=CT)
            left = weighted_flat[:, 3 * CE:5 * CE].rearrange("p (b n) -> p b n", b=2)
            apart = weighted_flat[:, 7 * CE:8 * CE].bitcast(BF16).rearrange("p (b n) -> p b n", b=2)
            value_slot = startval_slot[:, 0:width]
            hi_i = weighted_flat[:, 5 * CE:5 * CE + ET].bitcast(I32)
            hi = out_rows[:, :, :].rearrange("p b n -> p (b n)")[:, 0:ET]
            ways = heads * HI
            picks = [(pa, pb)[c // 2][:, c % 2 * CE:c % 2 * CE + CT * ways] for c in range(NB)]

            with nc.Block() as block:
                @block.vector
                def _(dve):
                    v = nc.vector
                    v.tensor_copy(pd[:, 0:HI], his[:, :])
                    rest = nodeval[:, :, 0:heads].rearrange("p j h -> p h j")
                    for k in range(3):
                        part = parts[:, k, 0:heads, 0:NT]
                        step(dve, v.tensor_copy(part, rest))
                        if k < 2:
                            step(dve, v.tensor_tensor(rest, rest, part, ALU.subtract))
                    step(dve, v.tensor_single_scalar(hi_i, src_idx[:, 0:ET], 8, ALU.arith_shift_right))
                    step(dve, v.tensor_copy(hi, hi_i))
                    v.memset(ln_stat[:, 0, 0:1], 0.0).then_inc(sums_ready.sem, 1)

                    def make_hot(i, c):
                        k, b, s = i * NB + c, c % 2, c % NB
                        dve.wait_ge(mask_loaded[s].sem, mask_loaded[s].past((i + c // NB + 1) * 16))
                        dve.wait_ge(picked.sem, picked.by_last_lap(k + 1))
                        v.tensor_scalar(hots[:, b, 1, :], mask[:, s, :], number[:, 1:2], None, ALU.is_equal
                                        ).then_inc(hot_made[1].sem, 1)

                    def make_mask(i, c):
                        k, b = i * NB + c, c % 2
                        dve.wait_ge(masked.sem, masked.past(k - 1))
                        v.tensor_tensor(hot_hi[:, b, :, :], pd[:, 0:HI].unsqueeze(1).broadcast_to([P, CT, HI]),
                                        hi[:, bass.ds(k * CT, CT)].unsqueeze(2).broadcast_to([P, CT, HI]), ALU.is_equal
                                        ).then_inc(hi_made.sem, 1)

                    def begin():
                        make_hot(0, 0)
                        make_mask(0, 0)

                    def leave_one(i, c, more):
                        if more:
                            make_hot(i, c + 1)
                        k, b, s = i * NB + c, c % 2, c % NB
                        dve.wait_ge(hi_made.sem, hi_made.past(k + 1))
                        dve.wait_ge(summed.sem, summed.by_last_lap(k + 1))
                        dve.wait_ge(picked.sem, picked.past(k + 1))
                        kept = left[:, b, 0:CT * ways]
                        v.tensor_tensor(kept.rearrange("p (t h j) -> p t h j", h=heads, j=HI),
                                        picks[s].rearrange("p (t h j) -> p t h j", h=heads, j=HI),
                                        hot_hi[:, b, :, :].unsqueeze(2).broadcast_to([P, CT, heads, HI]), ALU.mult
                                        ).then_inc(masked.sem, 1)
                        if more:
                            make_mask(i, c + 1)
                        dve.wait_ge(masked.sem, masked.past(k + 1))
                        v.tensor_reduce(alpha[:, bass.ds(k * CT, CT), 0:heads],
                                        kept.rearrange("p (t h j) -> p t h j", h=heads, j=HI), AX.X, ALU.add
                                        ).then_inc(summed.sem, 1)

                    laps(dve, begin, leave_one)

                @block.tensor
                def _(pe):
                    pe.wait_ge(sums_ready.sem, sums_ready.past(1))
                    with pe.Fori(0, ITERS) as i:
                        for c in range(NB):
                            k, b = i * NB + c, c % 2
                            for a in range(2):
                                pe.wait_ge(hot_made[a].sem, hot_made[a].past(k + 1))
                            pe.wait_ge(masked.sem, masked.by_last_lap(k + 1))
                            for t in range(CT):
                                for a in range(2):
                                    for n in range(3):
                                        ins = nc.tensor.matmul(
                                            picks[c][:, t * ways:(t + 1) * ways].rearrange("p (h j) -> p h j", j=HI),
                                            hots[:, b, a, t * P:(t + 1) * P], parts[:, n, 0:heads, a:a + 2 * HI - 1:2],
                                            start=(a == 0 and n == 0), stop=(a == 1 and n == 2))
                            ins.then_inc(picked.sem, 1)

                @block.scalar
                def _(act):
                    def distances(i, c):
                        k, b, s = i * NB + c, c % 2, c % NB
                        act.wait_ge(mask_loaded[s].sem, mask_loaded[s].past((i + c // NB + 1) * 16))
                        act.wait_ge(hot_made[0].sem, hot_made[0].past(k - 1))
                        nc.scalar.activation(apart[:, b, :], mask[:, s, :], ACT.Abs, bias=number[:, 2:3]).then_inc(lo_apart.sem, 1)

                    def make_hot(i, c, more):
                        if more:
                            distances(i, c + 1)
                        k, b = i * NB + c, c % 2
                        act.wait_ge(picked.sem, picked.by_last_lap(k + 1))
                        act.wait_ge(lo_apart.sem, lo_apart.past(k + 1))
                        nc.scalar.activation(hots[:, b, 0, :], apart[:, b, :], ACT.Relu, bias=ones[:, 0:1], scale=-1.0
                                             ).then_inc(hot_made[0].sem, 1)

                    laps(act, lambda: distances(0, 0), make_hot)

                @block.gpsimd
                def _(pool):
                    with pool.Fori(0, ITERS) as i:
                        wait_apart(pool, rows_moved.sem, rows_moved.past(16 * i))
                        nc.gpsimd.tensor_copy(slot[:, 0, 0:1], start_idx[:, bass.ds(i, 1)]).then_inc(idx_staged.sem, 1)
                        nc.gpsimd.tensor_copy(value_slot, startval[:, bass.ds(i, 1), 0:width].rearrange("p j w -> p (j w)")
                                              ).then_inc(idx_staged.sem, 1)
                        wait_apart(pool, idx_staged.sem, idx_staged.past(2 * i + 2))
                        nc.gpsimd.indirect_dma_start(out=start_rows[:, :],
                                                     out_offset=bass.IndirectOffsetOnAxis(ap=slot[:, 0, 0:1], axis=0),
                                                     in_=value_slot, in_offset=None, bounds_check=EP - 1,
                                                     oob_is_err=False).then_inc(rows_moved.sem, 16)
                    pool.wait_ge(rows_moved.sem, rows_moved.past(16 * NT))

                @block.sync
                def _(sp):
                    with sp.Fori(0, ITERS) as i:
                        for c in range(NB):
                            k = i * NB + c
                            for a in range(2):
                                sp.wait_ge(hot_made[a].sem, hot_made[a].by_last_lap(k + 1))
                            sp.dma_start(mask[:, c, :], lo_row[0:1, bass.ds(k * CE, CE)].broadcast_to([P, CE])
                                         ).then_inc(mask_loaded[c].sem, 16)
                    sp.wait_ge(rows_moved.sem, rows_moved.past(16 * NT))
                    sp.dma_start(START[:, 0:width * EC], start_rows.rearrange("(q f) w -> q (f w)", f=EC)).then_inc(loaded.sem, 16)
                    sp.wait_ge(loaded.sem, loaded.past(16))
            loaded.base += 16
            sums_ready.base += 1
            idx_staged.base += 2 * NT
            rows_moved.base += 16 * NT
            for c in (*hot_made, lo_apart, hi_made, picked, masked, summed):
                c.base += CHUNKS
            for m in mask_loaded:
                m.base += 16 * ITERS

        def attention(heads, start_rows, with_self):
            width = 2 * heads if with_self else heads
            look_up_scores(heads, start_rows, width)
            start = START[:, 0:width * EC].rearrange("q (f w) -> q w f", w=width)
            segment_scan(width, lambda k: FROM_DST[:, k, :], lambda k: start[:, k, :], "sum")
            scores_to_rows(heads)
            e, den, m = EA[:, 0:heads, :], DEN[:, 0:heads, :], M[:, 0:heads, :]
            with nc.Block() as block:
                @block.vector
                def _(dve):
                    v = nc.vector
                    step(dve, v.tensor_tensor(e, e, FROM_DST[:, 0:heads, :], ALU.add))
                    v.scalar_tensor_tensor(out=e, in0=e, scalar=0.2, in1=e, op0=ALU.mult, op1=ALU.max)
            segment_scan(heads, lambda k: M[:, k, :], lambda k: EA[:, k, :], "max")

            def by_last(t):
                return last[:, :].unsqueeze(1).broadcast_to([ER, heads, EC])

            with nc.Block() as block:
                @block.vector
                def _(dve):
                    nc.vector.tensor_tensor(den, m, by_last(m), ALU.mult)
            segment_scan(heads, lambda k: M[:, k, :], lambda k: DEN[:, k, :], "spread")
            with nc.Block() as block:
                @block.vector
                def _(dve):
                    v = nc.vector
                    if with_self:
                        own = FROM_DST[:, heads:2 * heads, :]
                        step(dve, v.tensor_tensor(m, m, own, ALU.max))
                        v.tensor_tensor(own, own, m, ALU.subtract)
                    v.tensor_tensor(e, e, m, ALU.subtract).then_inc(sums_ready.sem, 1)

                @block.scalar
                def _(act):
                    act.wait_ge(sums_ready.sem, sums_ready.past(1))
                    nc.scalar.activation(e, e, ACT.Exp)
                    if with_self:
                        nc.scalar.activation(FROM_DST[:, heads:2 * heads, :], FROM_DST[:, heads:2 * heads, :], ACT.Exp)
            sums_ready.base += 1
            segment_scan(heads, lambda k: M[:, k, :], lambda k: EA[:, k, :], "sum")
            with nc.Block() as block:
                @block.vector
                def _(dve):
                    step(dve, nc.vector.tensor_tensor(den, m, by_last(m), ALU.mult))
            segment_scan(heads, lambda k: M[:, k, :], lambda k: DEN[:, k, :], "spread")
            with nc.Block() as block:
                @block.vector
                def _(dve):
                    v = nc.vector
                    if with_self:
                        own = FROM_DST[:, heads:2 * heads, :]
                        step(dve, v.tensor_tensor(m, m, own, ALU.add))
                    else:
                        step(dve, v.tensor_scalar(m, m, 1e-16, None, ALU.add))
                    step(dve, v.reciprocal(m, m))
                    if with_self:
                        v.tensor_tensor(own, own, m, ALU.mult)
                    v.tensor_tensor(e, e, m, ALU.mult)
            turns = [(EA[:, hd, :], alpha[:, :, hd]) for hd in range(heads)]
            if with_self:
                turns += [(FROM_DST[:, heads + hd, :], own_t[:, :, hd]) for hd in range(heads)]
            with nc.Block() as block:
                @block.tensor
                def _(pe):
                    for k, (row, _) in enumerate(turns):
                        if k >= 2:
                            pe.wait_ge(ends_ready.sem, ends_ready.past(k - 1))
                        for f in range(TQ):
                            ins = nc.tensor.transpose((pa, pb)[k % 2][:, f * P:f * P + ER], row[:, f * P:(f + 1) * P],
                                                      ident[0:ER, 0:ER])
                        ins.then_inc(turned.sem, 1)

                @block.vector
                def _(dve):
                    for k, (_, tiles) in enumerate(turns):
                        dve.wait_ge(turned.sem, turned.past(k + 1))
                        nc.vector.tensor_copy(tiles.rearrange("p (q f) -> p f q", f=TQ),
                                              (pa, pb)[k % 2][:, 0:TQ * P].rearrange("p (f q) -> p f q", q=P)[:, :, 0:ER]
                                              ).then_inc(ends_ready.sem, 1)
            turned.base += len(turns)
            ends_ready.base += len(turns)

        def scores_to_rows(heads):
            with nc.Block() as block:
                @block.tensor
                def _(pe):
                    for hd in range(heads):
                        if hd >= 2:
                            pe.wait_ge(ends_ready.sem, ends_ready.past(hd - 1))
                        tiles = alpha[:, :, hd].rearrange("p (q f) -> p f q", f=TQ)
                        for f in range(TQ):
                            ins = nc.tensor.transpose((pa, pb)[hd % 2][0:ER, f * P:(f + 1) * P], tiles[:, f, :], ident[:, :])
                        ins.then_inc(turned.sem, 1)

                @block.vector
                def _(dve):
                    for hd in range(heads):
                        dve.wait_ge(turned.sem, turned.past(hd + 1))
                        nc.vector.tensor_copy(EA[:, hd, :], (pa, pb)[hd % 2][0:ER, 0:EC]).then_inc(ends_ready.sem, 1)
            turned.base += heads
            ends_ready.base += heads

        T1, T2 = arena[:, 2 * NT * D:2 * NT * D + NG * D], arena[:, 2 * NT * D + NG * D:2 * NT * D + 2 * NG * D]
        T3 = arena[:, NT * D:NT * D + NG * D]
        more_lhs = [arena[:, NT * D + k * NG * D:NT * D + (k + 1) * NG * D] for k in (1, 2)]

        layernorm_relu(g)
        store_rows(h_tab, h[:, :, :])
        edge_pass(h_tab, D, src_idx, keep_row, ALU.mult, ALU.add, "count")

        cum = arena[0:NT, 0:P]
        firsts = arena[0:NT, 2 * P:3 * P]
        has = arena[0:NT, 3 * P:4 * P]
        total = arena[0:NT, 4 * P:4 * P + 1]
        offset = arena[0:NT, 4 * P + 1:4 * P + 2]
        with nc.Block() as block:
            @block.vector
            def _(dve):
                v = nc.vector
                cnt = counts[0:NT, :]
                v.tensor_scalar(has, cnt, 1.0, None, ALU.min)
                step(dve, v.tensor_reduce(total, cnt, AX.X, ALU.add))
                v.tensor_tensor_scan(cum, ones[0:NT, :], cnt, 0.0, ALU.mult, ALU.add).then_inc(ends_ready.sem, 1)
                dve.wait_ge(turned.sem, turned.past(1))
                step(dve, v.tensor_copy(offset, pa[0:NT, 0:1]))
                step(dve, v.tensor_scalar(cum, cum, offset, None, ALU.add))
                step(dve, v.tensor_tensor(firsts, cum, cnt, ALU.subtract))
                v.tensor_scalar(cum, cum, -1.0 - EP, None, ALU.add)
                step(dve, v.tensor_scalar(firsts, firsts, -float(SKIP), None, ALU.add))
                v.tensor_tensor(cum, cum, has, ALU.mult)
                step(dve, v.tensor_tensor(firsts, firsts, has, ALU.mult))
                v.tensor_scalar(cum, cum, float(EP), None, ALU.add)
                step(dve, v.tensor_scalar(firsts, firsts, float(SKIP), None, ALU.add))
                v.tensor_scalar(has, cnt, 1.0, None, ALU.max).then_inc(ends_ready.sem, 1)
                dve.wait_ge(turned.sem, turned.past(2))
                v.tensor_copy(last_idx[:, :], pb[:, 0:NT])
                v.tensor_copy(start_idx[:, :], pb[:, P:P + NT])
                v.reciprocal(rcount[:, :], pb[:, 2 * P:2 * P + NT])

            @block.tensor
            def _(pe):
                pe.wait_ge(ends_ready.sem, ends_ready.past(1))
                nc.tensor.matmul(pa[0:NT, 0:1], before[:, :], total, start=True, stop=True).then_inc(turned.sem, 1)
                pe.wait_ge(ends_ready.sem, ends_ready.past(2))
                for k, t in enumerate((cum, firsts, has)):
                    ins = nc.tensor.transpose(pb[:, k * P:k * P + NT], t, ident[0:NT, 0:NT])
                ins.then_inc(turned.sem, 1)
        turned.base += 2
        ends_ready.base += 2

        def sage(layer):
            final = layer == 1

            def front(dve, i):
                dve.wait_ge(group_here.sem, group_here.past(i + 1))
                dve.wait_ge(group_turned.sem, group_turned.by_last_lap(i + 1))
                nc.vector.tensor_tensor(as_tiles(stage(0)), middle(g, i), group_wide(rcount[:, bass.ds(i * NG, NG)]), ALU.mult
                                        ).then_inc(group_staged.sem, 1)

            def scalar_front(act, i):
                wait_apart(act, group_turned.sem, group_turned.by_last_lap(i + 1))
                nc.scalar.copy(as_tiles(stage(1)), middle(h, i)).then_inc(group_staged.sem, 1)

            n_s, n_v = (2, 2) if final else (1, 1)

            def post(dve, i, b):
                v = nc.vector
                h_i, x_i = middle(h, i), middle(x, i)
                step = post_step.of(dve, i, 2 if final else 0)
                dve.wait_ge(group_kept.sem, group_kept.past(i))
                v.tensor_scalar(T1, products(b)[:, 0:NG * D], 0.0, None, ALU.min).then_inc(to_scalar.sem, 1)
                dve.wait_ge(to_vector.sem, to_vector.past(i * n_v + 1))
                ins = v.scalar_tensor_tensor(out=as_tiles(T3) if final else h_i, in0=as_tiles(T1), scalar=-1.0, in1=as_tiles(T2),
                                             op0=ALU.add, op1=ALU.add)
                if not final:
                    ins.then_inc(group_kept.sem, 1)
                    return
                step(ins)
                top = ln_stat[:, 0, :]
                step(v.tensor_reduce(top, as_tiles(T3), AX.X, ALU.max))
                v.tensor_tensor(as_tiles(T3), as_tiles(T3), group_wide(top), ALU.subtract).then_inc(to_scalar.sem, 1)
                dve.wait_ge(to_scalar.sem, to_scalar.past(i * n_s + 2))
                v.tensor_tensor(x_i, x_i, as_tiles(T3), ALU.add)
                wait_apart(dve, to_vector.sem, to_vector.past(i * n_v + 2))
                v.tensor_reduce(stat[:, 1, bass.ds(i * NG, NG)], as_tiles(T1), AX.X, ALU.add).then_inc(group_kept.sem, 1)

            def scalar_post(act, i, b):
                act.wait_ge(to_scalar.sem, to_scalar.past(i * n_s + 1))
                nc.scalar.activation(T1, T1, ACT.Exp)
                nc.scalar.activation(T2, products(b)[:, 0:NG * D], ACT.Relu).then_inc(to_vector.sem, 1)
                if final:
                    act.wait_ge(to_scalar.sem, to_scalar.past(i * n_s + 2))
                    nc.scalar.activation(T1, T3, ACT.Exp).then_inc(to_vector.sem, 1)

            def store(sp):
                with sp.Fori(0, groups) as i:
                    sp.wait_ge(group_kept.sem, group_kept.past(i + 1))
                    sp.dma_start(h_tab[bass.ds(i * NG * P, NG * P), :].rearrange("(j p) d -> p j d", p=P), middle(h, i)
                                 ).then_inc(stored.sem, 16)
                sp.wait_ge(stored.sem, stored.past(16 * groups))

            project(2, front, None, ([w0[:, 2 * layer, :], w0[:, 2 * layer + 1, :]], bias_sum[:, layer * D:(layer + 1) * D], D),
                    post, scalar_front=scalar_front, scalar_post=scalar_post,
                    gathers=lambda pool: gather_results(pool, g, scan_rows, D), store=None if final else store)
            post_step.done(groups)
            to_scalar.base += n_s * groups
            to_vector.base += n_v * groups
            if not final:
                stored.base += 16 * groups

        sage(0)
        edge_pass(h_tab, D, src_idx, keep_row, ALU.mult, ALU.add)
        sage(1)

        def front(dve, i):
            step = front_step.of(dve, i, 1 + LN_STEPS)
            x_i = middle(x, i)
            dve.wait_ge(sums_ready.sem, sums_ready.past(1))
            step(nc.vector.tensor_tensor(x_i, x_i, group_wide(stat[:, 0, bass.ds(i * NG, NG)]), ALU.subtract), apart=True)
            layernorm_group(dve, step, i, x_i, (middle(h, i), as_tiles(stage(0))))

        def logarithms(act):
            nc.scalar.activation(stat[:, 0, :], stat[:, 1, :], ACT.Ln).then_inc(sums_ready.sem, 1)

        def post(dve, i, b):
            nc.vector.tensor_copy(nodeval[:, bass.ds(i * NG, NG), :], products(0)[:, 0:NG * 2 * H1].rearrange("p (t k) -> p t k", k=2 * H1)
                                  ).then_inc(group_kept.sem, 1)

        project(1, front, (w1[:, :], None, H1 * D, lambda j: x1_tab[bass.ds(j * P, P), :]), ([sc1[:, :]], None, 2 * H1), post,
                begin=logarithms, scalar_front=deviations, buffers=arena[:, 0:NS * CE])
        sums_ready.base += 1
        front_step.done(groups)
        to_scalar.base += groups
        to_vector.base += groups
        with nc.Block() as block:
            @block.vector
            def _(dve):
                v = nc.vector
                s_src, s_dst = nodeval[:, :, 0:H1], nodeval[:, :, H1:2 * H1]
                v.tensor_copy(startval[:, :, 0:H1], s_dst)
                step(dve, v.tensor_tensor(startval[:, :, H1:2 * H1], s_src, s_dst, ALU.add))
                own = startval[:, :, H1:2 * H1]
                v.scalar_tensor_tensor(out=own, in0=own, scalar=0.2, in1=own, op0=ALU.mult, op1=ALU.max)
        attention(H1, start1_rows, True)
        with nc.Block() as block:
            @block.vector
            def _(dve):
                nc.vector.tensor_copy(pd[:, 0:P], ident[:, :])
        edge_pass(x1_tab, H1 * D, src_idx, keep_row, ALU.mult, ALU.add, "heads")

        DH = D + H1
        sums = arena[:, 0:NT * DH].rearrange("p (j d) -> p j d", d=DH)
        own_rows = [arena[:, NT * DH + b * NG * H1 * D:NT * DH + (b + 1) * NG * H1 * D].rearrange("p (t n) -> p t n", t=NG)
                    for b in range(2)]
        with nc.Block() as block:
            @block.gpsimd
            def _(pool):
                gather_results(pool, sums, scan1_rows, DH)

            @block.sync
            def _(sp):
                for i in range(groups):
                    b = i % 2
                    if i >= 2:
                        sp.wait_ge(group_kept.sem, group_kept.past(i - 1))
                    sp.dma_start(own_rows[b], x1_tab[i * NG * P:(i + 1) * NG * P, :].rearrange("(t p) n -> p t n", p=P)
                                 ).then_inc(own_loaded[b].sem, 16)

            @block.vector
            def _(dve):
                v = nc.vector

                def add_own(i, b, lap):
                    dve.wait_ge(own_loaded[b].sem, own_loaded[b].past(lap * 16 + 16))
                    dve.wait_ge(group_here.sem, group_here.past(i + 1))
                    step = front_step.of(dve, i, H1 + 1)
                    for hd in range(H1):
                        for t in range(NG):
                            j = bass.ds(i * NG + t, 1)
                            row = sums[:, j, 0:D].rearrange("p j d -> p (j d)")
                            ins = v.scalar_tensor_tensor(out=row, in0=own_rows[b][:, t, hd * D:(hd + 1) * D],
                                                         scalar=sums[:, j, D + hd:D + hd + 1].rearrange("p j d -> p (j d)"),
                                                         in1=row, op0=ALU.mult, op1=ALU.add)
                        step(ins)
                    h_i = middle(h, i)
                    step(v.scalar_tensor_tensor(out=h_i, in0=sums[:, bass.ds(i * NG, NG), 0:D], scalar=1.0 / H1, in1=h_i,
                                                     op0=ALU.mult, op1=ALU.add))
                    v.tensor_tensor(h_i, h_i, group_across(vec["L1_gnn_bias"][:, :]), ALU.add).then_inc(group_kept.sem, 1)

                with dve.Fori(0, groups // 2) as lap:
                    for b in range(2):
                        add_own(lap * 2 + b, b, lap)
                if groups % 2:
                    add_own(groups - 1, 0, groups // 2)
        results_gathered()
        front_step.done(groups)
        for b in range(2):
            own_loaded[b].base += 16 * ((groups + 1 - b) // 2)
        group_kept.base += groups
        batchnorm(h[:, :, :], vec["L1_gnn_bn1_w"][:, :])
        with nc.Block() as block:
            @block.vector
            def _(dve):
                step(dve, nc.vector.tensor_tensor(g2, g2, across(mean[:, :]), ALU.mult))
                nc.vector.tensor_tensor(h[:, :, :], g2, across(vec["L1_gnn_bn1_b"][:, :]), ALU.add)
        feed_forward()
        with nc.Block() as block:
            @block.vector
            def _(dve):
                step(dve, nc.vector.tensor_tensor(g, g, across(vec["L1_gnn_b2"][:, :]), ALU.add))
                nc.vector.tensor_tensor(g, g, h[:, :, :], ALU.add)
        batchnorm(g, vec["L1_gnn_bn2_w"][:, :])

        def front(dve, i):
            step = front_step.of(dve, i, 3 + LN_STEPS)
            v = nc.vector
            g_i, x_i = middle(g2, i), middle(x, i)
            step(v.tensor_tensor(g_i, g_i, group_across(mean[:, :]), ALU.mult))
            step(v.tensor_tensor(g_i, g_i, group_across(vec["L1_gnn_bn2_b"][:, :]), ALU.add))
            step(v.tensor_tensor(x_i, x_i, g_i, ALU.add), apart=True)
            layernorm_group(dve, step, i, x_i, (as_tiles(stage(0)),))

        def post(dve, i, b):
            nc.vector.tensor_copy(nodeval[:, bass.ds(i * NG, NG), 0:2 * H2], products(0)[:, 0:NG * 2 * H2].rearrange("p (t k) -> p t k", k=2 * H2)
                                  ).then_inc(group_kept.sem, 1)

        project(1, front, (w2[:, :], None, D, lambda j: h_tab[bass.ds(j * P, P), :]), ([sc2[:, :]], None, 2 * H2), post,
                scalar_front=deviations, buffers=arena[:, 0:NS * CE])
        front_step.done(groups)
        to_scalar.base += groups
        to_vector.base += groups
        with nc.Block() as block:
            @block.vector
            def _(dve):
                nc.vector.tensor_copy(startval[:, :, 0:H2], nodeval[:, :, H2:2 * H2])
        attention(H2, start2_rows, False)
        edge_pass(h_tab, D, src_idx, keep_row, ALU.mult, ALU.add, "halves")

        def front(dve, i):
            step = front_step.of(dve, i, 4 + LN_STEPS)
            v = nc.vector
            g_i, x_i = middle(g, i), middle(x, i)
            dve.wait_ge(group_here.sem, group_here.past(i + 1))
            step(v.tensor_tensor(g_i, g_i, group_across(vec["L2_gnn_bias"][:, :]), ALU.add))
            step(v.scalar_tensor_tensor(out=as_tiles(T1), in0=g_i, scalar=0.0, in1=group_across(vec["L2_gnn_prelu_w"][:, :]),
                                             op0=ALU.min, op1=ALU.mult))
            step(v.scalar_tensor_tensor(out=g_i, in0=g_i, scalar=0.0, in1=as_tiles(T1), op0=ALU.max, op1=ALU.add))
            step(v.tensor_tensor(x_i, x_i, g_i, ALU.add), apart=True)
            layernorm_group(dve, step, i, x_i, (as_tiles(stage(0)),))

        def post(dve, i, b):
            nc.vector.tensor_tensor(middle(x, i), middle(x, i), as_tiles(products(0)[:, 0:NG * D]), ALU.add).then_inc(group_kept.sem, 1)

        y_rows = y_tab.rearrange("(r n) d -> n r d", r=R)
        project(1, front, (w3[:, 0:R * D], bias_sum[:, 2 * D:(2 + R) * D], R * D, lambda j: y_rows[bass.ds(j * P, P), :, :]),
                ([w3[:, R * D:(R + 1) * D]], bias_sum[:, (2 + R) * D:(3 + R) * D], D), post, scalar_front=deviations,
                gathers=lambda pool: gather_results(pool, g, scan_rows, D), buffers=arena[:, NT * D:NT * D + NS * CE])
        front_step.done(groups)
        to_scalar.base += groups
        to_vector.base += groups
        edge_pass(y_tab, D, y_idx, cut_row, ALU.add, ALU.max)
        with nc.Block() as block:
            @block.gpsimd
            def _(pool):
                gather_results(pool, g, scan_rows, D)

            @block.vector
            def _(dve):
                with dve.Fori(0, groups) as i:
                    dve.wait_ge(group_here.sem, group_here.past(i + 1))
                    nc.vector.tensor_tensor(middle(x, i), middle(x, i), middle(g, i), ALU.add).then_inc(group_kept.sem, 1)

            @block.sync
            def _(sp):
                for i in range(groups):
                    sp.wait_ge(group_kept.sem, group_kept.past(i + 1))
                    j, full = i * NG, NG if i < groups - 1 else NG - 1
                    sp.dma_start(out[j * P:(j + full) * P, :].rearrange("(j p) d -> p j d", p=P), x[:, j:j + full, :]
                                 ).then_inc(stored.sem, 16)
                sp.dma_start(out[(NT - 1) * P:N, :], x[0:NL, NT - 1, :]).then_inc(stored.sem, 16)
                sp.wait_ge(stored.sem, stored.past(16 * (groups + 1)))


INPUTS = ["x", "src", "dst", "edge_type_4", "L0_gnn_W1l", "L0_gnn_b1", "L0_gnn_W1r", "L0_gnn_W2l", "L0_gnn_b2", "L0_gnn_W2r",
          "L1_gnn_W", "L1_gnn_att_src", "L1_gnn_att_dst", "L1_gnn_bias", "L1_gnn_bn1_w", "L1_gnn_bn1_b", "L1_gnn_W1",
          "L1_gnn_b1", "L1_gnn_W2", "L1_gnn_b2", "L1_gnn_bn2_w", "L1_gnn_bn2_b", "L2_gnn_W_src", "L2_gnn_W_dst",
          "L2_gnn_att_src", "L2_gnn_att_dst", "L2_gnn_bias", "L2_gnn_prelu_w", "L3_gnn_weight", "L3_gnn_bias"]


def kernel(**inputs):
    import concourse.bacc as bacc
    from concourse.bass_utils import run_bass_kernel_spmd

    nc = bacc.Bacc("TRN2", target_bir_lowering=False, num_devices=1)
    arrays, aps = {}, {}
    for name in INPUTS:
        arrays[f"in_{name}"] = np.ascontiguousarray(inputs[name])
        aps[name] = nc.dram_tensor(f"in_{name}", arrays[f"in_{name}"].shape, mybir.dt.from_np(arrays[f"in_{name}"].dtype),
                                   kind="ExternalInput").ap()
    out = nc.dram_tensor("out", [N, D], F32, kind="ExternalOutput").ap()
    build(nc, aps, out)
    return run_bass_kernel_spmd(nc, [arrays], core_ids=[0]).results[0]["out"]
```

```python
import numpy as np
import concourse.bass as bass
from concourse import mybir
from contextlib import ExitStack

F32 = mybir.dt.float32
BF16 = mybir.dt.bfloat16
I32 = mybir.dt.int32
ALU = mybir.AluOpType
ACT = mybir.ActivationFunctionType
AX = mybir.AxisListType

P = 128
N, D, E = 6250, 128, 100000
NT = -(-N // P)
NP = NT * P
NG = 7
NS = 4
NL = N - (NT - 1) * P
TQ = 7
EC = TQ * P
ER = -(-E // EC)
EP = ER * EC
ET = EP // P
CT = 4
CE = CT * P
NB = 4
CHUNKS = ET // CT
ITERS = CHUNKS // NB
H1, H2, R = 4, 2, 4
FF = 512
LQ = 7
LB = 4 * LQ
HI = -(-NT // 2)
BIG = 3.0e38
LN_EPS = 1e-5
SKIP = EP + 1024


class Chain:

    def __init__(self, sem):
        self.sem, self.n = sem, 0

    def __call__(self, engine, ins):
        self.n += 1
        ins.then_inc(self.sem, 1)
        engine.wait_ge(self.sem, self.n)


class Count:

    def __init__(self, sem, ahead=0):
        self.sem, self.base, self.ahead = sem, 0, ahead

    def past(self, n):
        return n + (self.base + self.ahead)

    def by_last_lap(self, n):
        return n + self.base


class GroupChain:

    def __init__(self, count, wait_apart):
        self.count, self.wait_apart, self.per = count, wait_apart, 0

    def of(self, engine, i, per):
        self.per, at = per, 0

        def step(ins, apart=False):
            nonlocal at
            at += 1
            assert at <= per
            ins.then_inc(self.count.sem, 1)
            if apart:
                self.wait_apart(engine, self.count.sem, self.count.past(i * per + at))
            else:
                engine.wait_ge(self.count.sem, self.count.past(i * per + at))

        return step

    def done(self, laps):
        self.count.base += laps * self.per


def build(nc, a, out):
    assert NT % NG == 0 and ET % CT == 0 and CHUNKS % NB == 0
    groups = NT // NG
    with ExitStack() as ctx:
        def sb(name, shape, dt=F32):
            return ctx.enter_context(nc.sbuf_tensor(name, shape, dt))

        def count(name, ahead=0):
            return Count(ctx.enter_context(nc.semaphore(name)), ahead)

        def dram(name, shape, dt=F32):
            return nc.dram_tensor(name, shape, dt).ap()

        h_tab = dram("h_tab", [NP, D])
        x1_tab = dram("x1_tab", [NP, H1 * D])
        y_tab = dram("y_tab", [R * NP, D])
        scan_rows = dram("scan_rows", [EP + P, D])
        start1_rows = dram("start1_rows", [EP, 2 * H1])
        start2_rows = dram("start2_rows", [EP, H2])
        scan1_rows = dram("scan1_rows", [EP + P, D + H1])
        keep_row = dram("keep_row", [1, EP], BF16)
        cut_row = dram("cut_row", [1, EP], BF16)
        lo_row = dram("lo_row", [1, EP], BF16)
        hi_row = dram("hi_row", [1, EP], BF16)

        x = sb("x", [P, NT, D])
        h = sb("h", [P, NT, D])
        arena = sb("arena", [P, 14336])
        g = arena[:, 0:NT * D].rearrange("p (j d) -> p j d", d=D)
        g2 = arena[:, NT * D:2 * NT * D].rearrange("p (j d) -> p j d", d=D)
        weighted = sb("weighted", [P, 2, CT, H1 * P])
        weighted_flat = weighted[:, :, :, :].rearrange("p b t n -> p (b t n)")
        alpha = sb("alpha", [P, ET, H1])
        alpha_flat = alpha[:, :, :].rearrange("p t h -> p (t h)")
        hi_t = alpha_flat[:, 0:ET]
        lo_t = alpha_flat[:, ET:2 * ET]
        src_idx = sb("src_idx", [P, ET + (NB + 1) * CT], I32)
        y_idx = sb("y_idx", [P, ET + (NB + 1) * CT], I32)
        last_idx = sb("last_idx", [P, NT], I32)
        start_idx = sb("start_idx", [P, NT], I32)
        rcount = sb("rcount", [P, NT])
        slot = sb("slot", [P, NB, CT], I32)
        keep = sb("keep", [ER, EC])
        cut = sb("cut", [ER, EC])
        last = sb("last", [ER, EC])
        notlast = sb("notlast", [ER, EC])
        whole = sb("whole", [P, 3, P])
        ends = sb("ends", [ER, 2, P])
        ends_row = sb("ends_row", [P, P])
        carry = sb("carry", [ER, P])
        mask = sb("mask", [P, NB, CE], BF16)
        scan_t = sb("scan_t", [P, 2, CE])
        out_rows = sb("out_rows", [P, 2, CE + CT * H1])
        nodeval = sb("nodeval", [P, NT, 2 * H1])
        startval = sb("startval", [P, NT, 2 * H1])
        stat = sb("stat", [P, 2, NT])
        ln_stat = sb("ln_stat", [P, 2, NG])
        row_stats = sb("row_stats", [P, NG, 6])
        moments = sb("moments", [P, NG, 2])
        ident = sb("ident", [P, P])
        ones = sb("ones", [P, P])
        ones_tail = sb("ones_tail", [P, P])
        before = sb("before", [NT, NT])
        counts = sb("counts", [64, P])
        startval_slot = sb("startval_slot", [P, 2 * H1])
        number = sb("number", [P, 3])
        other_hi = sb("other_hi", [HI, H1, HI], BF16)
        parts = sb("parts", [P, 3, H1, 64], BF16)
        w0 = sb("w0", [P, 4, D])
        w1 = sb("w1", [P, H1 * D])
        sc1 = sb("sc1", [P, 2 * H1])
        ff1 = sb("ff1", [P, FF])
        ff2 = sb("ff2", [P, FF // P, D])
        ff1_b = sb("ff1_b", [P, FF // P])
        w2 = sb("w2", [P, D])
        sc2 = sb("sc2", [P, 2 * H2])
        w3 = sb("w3", [P, (R + 1) * D])
        bias_sum = sb("bias_sum", [65, (2 + R + 1) * D], BF16)
        one_rows = sb("one_rows", [65, P], BF16)
        VECS = ["L1_gnn_bias", "L1_gnn_bn1_w", "L1_gnn_bn1_b", "L1_gnn_b2", "L1_gnn_bn2_w", "L1_gnn_bn2_b",
                "L2_gnn_bias", "L2_gnn_prelu_w"]
        vec = {n: sb(n + "_all", [P, D]) for n in VECS}
        mean = sb("mean", [P, D])
        gain = sb("gain", [P, D])

        pa, pb, pc, pd = [ctx.enter_context(nc.psum_tensor(n, [P, 2 * CE], F32)) for n in ("pa", "pb", "pc", "pd")]

        step = Chain(ctx.enter_context(nc.semaphore("vector_step")))
        pool_step = Chain(ctx.enter_context(nc.semaphore("pool_step")))
        passed = ctx.enter_context(nc.semaphore("passed"))
        cleared = count("cleared")
        loaded = count("loaded")
        stored = count("stored")
        rows_moved = count("rows_moved")
        group_rows = [count(f"group_rows{b}") for b in range(2)]
        group_here = count("group_here")
        own_loaded = [count(f"own_loaded{b}") for b in range(2)]
        turned = count("turned")
        ends_ready = count("ends_ready")
        sums_ready = count("sums_ready")
        gathered = [count(f"gathered{c}") for c in range(NB)]
        idx_staged = count("idx_staged")
        hot_made = [count(f"hot_made{a}", 2 * LQ) for a in range(2)]
        lo_apart = count("lo_apart")
        numbers_loaded = [count(f"numbers_loaded{b}") for b in range(2)]
        picked = count("picked", NB)
        summed = count("summed", NB)
        chunk_weighted = count("chunk_weighted")
        counted = count("counted", 1)
        chunk_turned = count("chunk_turned", NB)
        chunk_scanned = count("chunk_scanned", NB)
        chunk_back = count("chunk_back", 2)
        chunk_copied = count("chunk_copied", 2)
        written = [count(f"written{b}", 16) for b in range(2)]
        mask_loaded = [count(f"mask_loaded{c}") for c in range(NB)]
        group_staged = count("group_staged")
        group_turned = count("group_turned", 1)
        group_lhs = count("group_lhs")
        group_product = count("group_product", 2)
        group_kept = count("group_kept", 2)
        to_scalar = count("to_scalar")
        to_vector = count("to_vector")
        tile_product = count("tile_product")
        tile_out = count("tile_out", 2)
        tile_stored = [count(f"tile_stored{b}", 16) for b in range(NS)]
        ff_up = count("ff_up", 1)
        ff_hidden = count("ff_hidden", 2)
        ff_down = count("ff_down", 1)
        ff_kept = count("ff_kept", 1)

        def wait_apart(engine, sem, value):
            engine.wait_ge(sem, value)
            engine.sem_inc(passed, 1)

        front_step = GroupChain(count("front_step"), wait_apart)
        post_step = GroupChain(count("post_step"), wait_apart)

        dst_i = arena[0:ER, 0:EC].bitcast(I32)
        src_i = arena[0:ER, EC:2 * EC].bitcast(I32)
        rel_i = arena[0:ER, 2 * EC:3 * EC].bitcast(I32)
        dst_f = arena[0:ER, 3 * EC:4 * EC]
        src_f = arena[0:ER, 4 * EC:5 * EC]
        tmp_f = arena[0:ER, 5 * EC:6 * EC]
        tmp_i = arena[0:ER, 6 * EC:7 * EC].bitcast(I32)
        prev_i = arena[0:ER, 7 * EC:7 * EC + 1].bitcast(I32)
        next_i = arena[0:ER, 7 * EC + 1:7 * EC + 2].bitcast(I32)
        prev_f = arena[0:ER, 7 * EC + 2:7 * EC + 3]
        next_f = arena[0:ER, 7 * EC + 3:7 * EC + 4]
        at = 7 * EC + 8

        def take(n):
            nonlocal at
            at += n
            return arena[:, at - n:at]

        raw_b = take((2 + R + 1) * D)[0:65, :]
        raw_w = take(4 * D).rearrange("p (k d) -> p k d", d=D)
        att = take(4 * H1 * D).rearrange("p (k d) -> p k d", d=H1 * D)
        wdst = take(D)
        prod = take(H1 * D)
        prod16 = take((2 + R + 1) * D // 2).bitcast(BF16)
        iota_i = take(P).bitcast(I32)
        number_i = take(1).bitcast(I32)
        lo16 = take(EC // 2).bitcast(BF16)
        hi16 = take(EC // 2).bitcast(BF16)
        other_f = take(H1 * HI)[0:HI, :].rearrange("p (h j) -> p h j", j=HI)
        keep16 = take(EC // 2).bitcast(BF16)
        cut16 = take(EC // 2).bitcast(BF16)

        ERF, TAIL = E // EC, E % EC
        with nc.Block() as block:
            @block.vector
            def _(dve):
                v = nc.vector
                v.memset(dst_i, N)
                v.memset(src_i, 0)
                v.memset(rel_i, 0)
                v.memset(prev_i, -1)
                v.memset(next_i, -1)
                v.memset(x[:, NT - 1, :], 0.0)
                v.memset(ends[:, :, :], 0.0)
                v.memset(ends_row[:, :], 0.0)
                v.memset(counts[:, :], 0.0)
                v.memset(src_idx[:, ET:], 0)
                v.memset(y_idx[:, ET:], 0)
                v.memset(scan_t[:, 1, :], 0.0)
                v.memset(ones[:, :], 1.0)
                v.memset(out_rows[:, 0, :], 0.0).then_inc(cleared.sem, 1)

            @block.gpsimd
            def _(pool):
                p = nc.gpsimd
                pool_step(pool, p.memset(ident[:, :], 0.0))
                p.affine_select(out=ident[:, :], in_=ident[:, :], compare_op=ALU.not_equal, fill=1.0,
                                base=0, pattern=[[-1, P]], channel_multiplier=1)
                pool_step(pool, p.memset(ones_tail[:, :], 1.0))
                p.affine_select(out=ones_tail[:, :], in_=ones_tail[:, :], compare_op=ALU.is_ge, fill=0.0,
                                base=NL - 1, pattern=[[0, P]], channel_multiplier=-1)
                pool_step(pool, p.memset(before[:, :], 1.0))
                p.affine_select(out=before[:, :], in_=before[:, :], compare_op=ALU.is_gt, fill=0.0,
                                base=0, pattern=[[1, NT]], channel_multiplier=-1)
                pool_step(pool, p.memset(other_f, -BIG))
                for hd in range(H1):
                    p.affine_select(out=other_f[:, hd, :], in_=other_f[:, hd, :], compare_op=ALU.not_equal, fill=0.0,
                                    base=0, pattern=[[-1, HI]], channel_multiplier=1)
                p.iota(iota_i, [[1, P]], base=0, channel_multiplier=0)
                p.iota(number_i, [[0, 1]], base=0, channel_multiplier=1)

            @block.tensor
            def _(pe):
                for c in (counted, ff_up, picked, summed, chunk_turned, chunk_back, group_turned, group_product, ff_down):
                    pe.sem_inc(c.sem, c.ahead)

            @block.scalar
            def _(act):
                for c in (*hot_made, chunk_scanned, chunk_copied, *written, tile_out, group_kept, *tile_stored, ff_hidden, ff_kept):
                    act.sem_inc(c.sem, c.ahead)

            @block.sync
            def _(sp):
                loads = 0

                def load(to, of, **single):
                    nonlocal loads
                    loads += 1
                    sp.dma_start(to, of, **single).then_inc(loaded.sem, 16)

                few = {"allow_slow_non_contiguous": True}
                sp.wait_ge(cleared.sem, 1)
                for to, name in ((dst_i, "dst"), (src_i, "src"), (rel_i, "edge_type_4")):
                    load(to[0:ERF, :], a[name][0:ERF * EC].rearrange("(q f) -> q f", f=EC))
                    load(to[ERF:ERF + 1, 0:TAIL], a[name][ERF * EC:E].rearrange("(q f) -> q f", q=1))
                load(prev_i[1:ER, :], a["dst"][0:ERF * EC].rearrange("(q f) -> q f", f=EC)[:, EC - 1:EC], **few)
                load(next_i[0:ER - 2, :], a["dst"][EC:ERF * EC].rearrange("(q f) -> q f", f=EC)[:, 0:1], **few)
                load(next_i[ER - 2:ER - 1, :], a["dst"][ERF * EC:ERF * EC + 1].rearrange("(q f) -> q f", q=1), **few)
                load(x[:, 0:NT - 1, :], a["x"][0:(NT - 1) * P, :].rearrange("(j p) d -> p j d", p=P))
                load(x[0:NL, NT - 1, :], a["x"][(NT - 1) * P:N, :])
                for k, name in enumerate(("L0_gnn_W1l", "L0_gnn_W1r", "L0_gnn_W2l", "L0_gnn_W2r")):
                    load(raw_w[:, k, :], a[name][:, :])
                for k, name in enumerate(("L0_gnn_b1", "L0_gnn_b2")):
                    load(raw_b[:, k * D:(k + 1) * D], a[name].rearrange("(o d) -> o d", o=1).broadcast_to([65, D]))
                load(raw_b[:, 2 * D:], a["L3_gnn_bias"].rearrange("(o r) d -> o (r d)", o=1).broadcast_to([65, (R + 1) * D]))
                load(w1[:, :], a["L1_gnn_W"][:, :])
                load(ff1[:, :], a["L1_gnn_W1"][:, :])
                load(ff2[:, :, :], a["L1_gnn_W2"].rearrange("(k p) d -> p k d", p=P))
                load(ff1_b[:, :], a["L1_gnn_b1"].rearrange("(k p) -> p k", p=P), **few)
                load(w2[:, :], a["L2_gnn_W_src"][:, :])
                load(wdst, a["L2_gnn_W_dst"][:, :])
                load(w3[:, :].rearrange("p (r d) -> p r d", d=D), a["L3_gnn_weight"].rearrange("r p d -> p r d"))
                for name in VECS:
                    load(vec[name][:, :], a[name].rearrange("(o d) -> o d", o=1).broadcast_to([P, D]))
                for k, (name, n) in enumerate((("L1_gnn_att_src", H1 * D), ("L1_gnn_att_dst", H1 * D),
                                               ("L2_gnn_att_src", D), ("L2_gnn_att_dst", D))):
                    load(att[:, k, 0:n], a[name].rearrange("(o h) c -> o (h c)", o=1).broadcast_to([P, n]))
                load(scan_rows[EP:EP + P, :], out_rows[:, 0, 0:D])
                load(scan1_rows[EP:EP + P, 0:D], out_rows[:, 0, 0:D])
                load(scan1_rows[EP:EP + P, D:D + H1], ones[:, 0:H1])
                sp.wait_ge(loaded.sem, 16 * loads)
                loaded.base = 16 * loads
        cleared.base += 1

        def turn_edges(row, tiles):
            with nc.Block() as block:
                @block.tensor
                def _(pe):
                    for f in range(TQ):
                        ins = nc.tensor.transpose(pa[:, f * P:f * P + ER], row[:, f * P:(f + 1) * P], ident[0:ER, 0:ER])
                    ins.then_inc(turned.sem, 1)

                @block.vector
                def _(dve):
                    dve.wait_ge(turned.sem, turned.past(1))
                    nc.vector.tensor_copy(tiles.rearrange("p (q f) -> p f q", f=TQ),
                                          pa[:, 0:TQ * P].rearrange("p (f q) -> p f q", q=P)[:, :, 0:ER])
            turned.base += 1

        with nc.Block() as block:
            @block.vector
            def _(dve):
                v = nc.vector
                v.tensor_copy(dst_f, dst_i)
                v.tensor_copy(src_f, src_i)
                v.tensor_copy(pd[:, 0:P], iota_i)
                v.tensor_copy(other_hi[:, :, :], other_f)
                step(dve, v.tensor_copy(number[:, 0:1], number_i))
                v.tensor_scalar(number[:, 1:2], number[:, 0:1], float(P), None, ALU.add)
                v.tensor_scalar(number[:, 2:3], number[:, 0:1], -1.0, None, ALU.mult)
                v.memset(parts[:, :, :, :], 0.0)
                v.memset(bias_sum[:, :], 0.0)
                v.memset(one_rows[:, :], 1.0)
                step(dve, v.tensor_single_scalar(tmp_i, src_i, 8, ALU.arith_shift_right))
                step(dve, v.tensor_copy(hi16[0:ER, :], tmp_i))
                step(dve, v.tensor_single_scalar(tmp_i, src_i, 2 * P - 1, ALU.bitwise_and))
                v.tensor_copy(lo16[0:ER, :], tmp_i)
                v.tensor_copy(prev_f, prev_i)
                step(dve, v.tensor_copy(next_f, next_i))
                v.tensor_tensor(keep[:, 1:EC], dst_f[:, 1:EC], dst_f[:, 0:EC - 1], ALU.is_equal)
                v.tensor_tensor(keep[:, 0:1], dst_f[:, 0:1], prev_f, ALU.is_equal)
                v.tensor_tensor(notlast[:, 0:EC - 1], dst_f[:, 0:EC - 1], dst_f[:, 1:EC], ALU.is_equal)
                step(dve, v.tensor_tensor(notlast[:, EC - 1:EC], dst_f[:, EC - 1:EC], next_f, ALU.is_equal))
                v.tensor_scalar(cut[:, :], keep[:, :], -1.0, BIG, ALU.add, ALU.mult)
                v.tensor_scalar(last[:, :], notlast[:, :], -1.0, 1.0, ALU.mult, ALU.add)
                v.tensor_copy(keep16[0:ER, :], keep[:, :])
                v.tensor_scalar(cut16[0:ER, :], keep[:, :], -1.0, BIG, ALU.add, ALU.mult)
                v.scalar_tensor_tensor(out=tmp_f, in0=rel_i, scalar=float(NP), in1=src_f, op0=ALU.mult, op1=ALU.add)
                v.tensor_reduce(carry[:, 0:1], keep[:, :], AX.X, ALU.min)
                step(dve, v.tensor_reduce(carry[:, 1:2], notlast[:, :], AX.X, ALU.min))
                for k in range(2):
                    v.tensor_copy(ends[:, k, 0:2 * H1], carry[:, k:k + 1].broadcast_to([ER, 2 * H1]))
                part16 = prod16[0:65, :]
                for k in range(3):
                    step(dve, v.tensor_copy(part16, raw_b))
                    v.tensor_copy(bias_sum[32 * k:32 * k + 1, :], part16[32 * k:32 * k + 1, :])
                    step(dve, v.tensor_tensor(raw_b, raw_b, part16, ALU.subtract))
                for k, (w, to, heads, c) in enumerate(((w1[:, :], sc1[:, 0:H1], H1, D), (w1[:, :], sc1[:, H1:2 * H1], H1, D),
                                                       (w2[:, :], sc2[:, 0:H2], H2, D // H2),
                                                       (wdst, sc2[:, H2:2 * H2], H2, D // H2))):
                    step(dve, v.tensor_tensor(prod[:, 0:heads * c], w[:, 0:heads * c], att[:, k, 0:heads * c], ALU.mult))
                    step(dve, v.tensor_reduce(to, prod[:, 0:heads * c].rearrange("p (h c) -> p h c", c=c), AX.X, ALU.add))

            @block.tensor
            def _(pe):
                for k in range(4):
                    ins = nc.tensor.transpose(pb[:, k * D:(k + 1) * D], raw_w[:, k, :], ident[:, :])
                ins.then_inc(turned.sem, 1)

            @block.scalar
            def _(act):
                act.wait_ge(turned.sem, turned.past(1))
                nc.scalar.copy(w0[:, :, :], pb[:, 0:4 * D].rearrange("p (k d) -> p k d", d=D))
        turned.base += 1

        with nc.Block() as block:
            @block.tensor
            def _(pe):
                nc.tensor.transpose(pa[:, 0:ER], ends[:, 0, :], ident[0:ER, 0:ER])
                nc.tensor.transpose(pa[:, P:P + ER], ends[:, 1, :], ident[0:ER, 0:ER]).then_inc(turned.sem, 1)

            @block.vector
            def _(dve):
                dve.wait_ge(turned.sem, turned.past(1))
                nc.vector.tensor_copy(whole[:, 0, 0:ER], pa[:, 0:ER])
                nc.vector.tensor_scalar(whole[:, 1, 0:ER], pa[:, 0:ER], -1.0, BIG, ALU.add, ALU.mult)
                nc.vector.tensor_copy(whole[:, 2, 0:ER], pa[:, P:P + ER])

            @block.sync
            def _(sp):
                sp.dma_start(keep_row.rearrange("o (q f) -> (o q) f", f=EC), keep16[0:ER, :]).then_inc(stored.sem, 16)
                sp.dma_start(cut_row.rearrange("o (q f) -> (o q) f", f=EC), cut16[0:ER, :]).then_inc(stored.sem, 16)
                sp.dma_start(lo_row.rearrange("o (q f) -> (o q) f", f=EC), lo16[0:ER, :]).then_inc(stored.sem, 16)
                sp.dma_start(hi_row.rearrange("o (q f) -> (o q) f", f=EC), hi16[0:ER, :]).then_inc(stored.sem, 16)
                sp.wait_ge(stored.sem, stored.past(64))
        turned.base += 1
        stored.base += 64
        turn_edges(src_f, src_idx[:, 0:ET])
        turn_edges(tmp_f, y_idx[:, 0:ET])
        for op, by, tiles in ((ALU.arith_shift_right, 7, hi_t), (ALU.bitwise_and, P - 1, lo_t)):
            with nc.Block() as block:
                @block.vector
                def _(dve):
                    step(dve, nc.vector.tensor_single_scalar(tmp_i, dst_i, by, op))
                    nc.vector.tensor_copy(tmp_f, tmp_i)
            turn_edges(tmp_f, tiles)

        def laps(engine, first, body, n=NB, times=ITERS):
            first()
            with engine.Fori(0, times - 1) as i:
                for c in range(n):
                    body(i, c, True)
            for c in range(n):
                body(times - 1, c, c < n - 1)

        def edge_pass(table, width, idx, mask_row, op0, op1, mode="plain"):
            beside = H1 if mode == "heads" else 0
            target = scan1_rows if beside else scan_rows

            def written_rows(b):
                return out_rows[:, b, 0:CT * (D + beside)].rearrange("p (t d) -> p t d", d=D + beside)

            def rows(c, t):
                n = (c * CT + t) * width
                return arena[:, n:n + width]

            def hot(b):
                both = weighted_flat[:, b * CT * H1 * P:b * CT * H1 * P + CT * (64 + P) // 2].bitcast(BF16)
                return (both[:, 0:CT * 64].rearrange("p (t k) -> p t k", k=64),
                        both[:, CT * 64:CT * (64 + P)].rearrange("p (t k) -> p t k", k=P))

            with nc.Block() as block:
                @block.gpsimd
                def _(pool):
                    with pool.Fori(0, ITERS) as i:
                        for c in range(NB):
                            wait_apart(pool, idx_staged.sem, idx_staged.past(i * NB + c + 1))
                            for t in range(CT):
                                nc.gpsimd.indirect_dma_start(
                                    out=rows(c, t), out_offset=None, in_=table[:, :],
                                    in_offset=bass.IndirectOffsetOnAxis(ap=slot[:, c, t:t + 1], axis=0)
                                ).then_inc(gathered[c].sem, 16)

                @block.sync
                def _(sp):
                    with sp.Fori(0, ITERS) as i:
                        for c in range(NB):
                            k = i * NB + c
                            sp.wait_ge(chunk_scanned.sem, chunk_scanned.by_last_lap(k + 1))
                            sp.dma_start(mask[:, c, :], mask_row[0:1, bass.ds(k * CE, CE)].broadcast_to([P, CE])
                                         ).then_inc(mask_loaded[c].sem, 16)

                @block.vector
                def _(dve):
                    v = nc.vector

                    def weigh(i, c):
                        k, b = i * NB + c, c % 2
                        if mode == "plain":
                            return
                        dve.wait_ge(chunk_turned.sem, chunk_turned.by_last_lap(k + NB - 1))
                        if mode == "count":
                            hot_hi, hot_lo = hot(b)
                            v.tensor_tensor(hot_hi, pd[:, 0:64].unsqueeze(1).broadcast_to([P, CT, 64]),
                                            hi_t[:, bass.ds(k * CT, CT)].unsqueeze(2).broadcast_to([P, CT, 64]), ALU.is_equal)
                            v.tensor_tensor(hot_lo, pd[:, 0:P].unsqueeze(1).broadcast_to([P, CT, P]),
                                            lo_t[:, bass.ds(k * CT, CT)].unsqueeze(2).broadcast_to([P, CT, P]), ALU.is_equal
                                            ).then_inc(chunk_weighted.sem, 1)
                        elif mode == "heads":
                            for t in range(CT):
                                ins = v.tensor_tensor(
                                    weighted[:, b, t, :].rearrange("p (h n) -> p h n", n=P),
                                    pd[:, 0:P].unsqueeze(1).broadcast_to([P, H1, P]),
                                    alpha_flat[:, bass.ds((k * CT + t) * H1, H1)].unsqueeze(2).broadcast_to([P, H1, P]), ALU.mult)
                            ins.then_inc(chunk_weighted.sem, 1)
                        else:
                            dve.wait_ge(gathered[c % NB].sem, gathered[c % NB].past((i + c // NB + 1) * 16 * CT))
                            half = D // H2
                            n = (c % NB) * CT * width
                            v.tensor_tensor(
                                weighted[:, b, :, 0:D].rearrange("p t (h n) -> p t h n", n=half),
                                arena[:, n:n + CT * width].rearrange("p (t h n) -> p t h n", h=H2, n=half),
                                alpha[:, bass.ds(k * CT, CT), 0:H2].unsqueeze(3).broadcast_to([P, CT, H2, half]), ALU.mult
                            ).then_inc(chunk_weighted.sem, 1)

                    def scan(i, c, more):
                        if more:
                            weigh(i, c + 1)
                        k, b = i * NB + c, c % 2
                        dve.wait_ge(chunk_turned.sem, chunk_turned.past(k + 1))
                        if mode == "count":
                            dve.wait_ge(counted.sem, counted.past(k))
                            v.tensor_tensor(counts[:, :], counts[:, :], pc[0:64, b * CE:b * CE + P], ALU.add
                                            ).then_inc(counted.sem, 1)
                        dve.wait_ge(mask_loaded[c].sem, mask_loaded[c].past((i + 1) * 16))
                        dve.wait_ge(chunk_back.sem, chunk_back.by_last_lap(k + 1))
                        dve.wait_ge(chunk_scanned.sem, chunk_scanned.past(k))
                        v.tensor_tensor_scan(scan_t[:, b, :], mask[:, c, :], pa[:, b * CE:(b + 1) * CE],
                                             scan_t[:, 1 - b, CE - 1:CE], op0, op1).then_inc(chunk_scanned.sem, 1)

                    laps(dve, lambda: weigh(0, 0), scan)

                @block.tensor
                def _(pe):
                    def turn(i, c):
                        k, b, s = i * NB + c, c % 2, c % NB
                        if mode != "plain":
                            pe.wait_ge(chunk_weighted.sem, chunk_weighted.past(k + 1))
                        if mode != "halves":
                            pe.wait_ge(gathered[s].sem, gathered[s].past((i + c // NB + 1) * 16 * CT))
                        pe.wait_ge(chunk_scanned.sem, chunk_scanned.past(k - 1))
                        if mode == "count":
                            hot_hi, hot_lo = hot(b)
                            for t in range(CT):
                                nc.tensor.matmul(pc[0:64, b * CE:b * CE + P], hot_hi[:, t, :], hot_lo[:, t, :],
                                                 start=(t == 0), stop=(t == CT - 1))
                        for t in range(CT):
                            to = pa[:, b * CE + t * P:b * CE + (t + 1) * P]
                            if mode == "heads":
                                for hd in range(H1):
                                    ins = nc.tensor.matmul(to, rows(s, t)[:, hd * D:(hd + 1) * D],
                                                           weighted[:, b, t, hd * P:(hd + 1) * P],
                                                           start=(hd == 0), stop=(hd == H1 - 1))
                            elif mode == "halves":
                                ins = nc.tensor.transpose(to, weighted[:, b, t, 0:D], ident[:, :])
                            else:
                                ins = nc.tensor.transpose(to, rows(s, t), ident[:, :])
                        ins.then_inc(chunk_turned.sem, 1)

                    def back(i, c, more):
                        if more:
                            turn(i, c + 1)
                        k, b = i * NB + c, c % 2
                        pe.wait_ge(chunk_scanned.sem, chunk_scanned.past(k + 1))
                        pe.wait_ge(chunk_copied.sem, chunk_copied.by_last_lap(k + 1))
                        for t in range(CT):
                            ins = nc.tensor.transpose(pb[:, b * CE + t * P:b * CE + (t + 1) * P],
                                                      scan_t[:, b, t * P:(t + 1) * P], ident[:, :])
                        ins.then_inc(chunk_back.sem, 1)

                    laps(pe, lambda: turn(0, 0), back)

                @block.scalar
                def _(act):
                    def stage_numbers(k, c):
                        nc.scalar.copy(slot[:, c, :], idx[:, bass.ds(k * CT, CT)]).then_inc(idx_staged.sem, 1)

                    for c in range(NB):
                        stage_numbers(c, c)
                    wait_apart(act, chunk_turned.sem, chunk_turned.past(1))
                    stage_numbers(NB, 0)
                    with act.Fori(0, ITERS) as i:
                        for c in range(NB):
                            k, b = i * NB + c, c % 2
                            act.wait_ge(chunk_back.sem, chunk_back.past(k + 1))
                            act.wait_ge(written[b].sem, written[b].by_last_lap((i * 2 + c // 2 + 1) * 16))
                            ins = nc.scalar.copy(written_rows(b)[:, :, 0:D],
                                                 pb[:, b * CE:(b + 1) * CE].rearrange("p (t d) -> p t d", d=D))
                            if beside:
                                ins = nc.scalar.copy(written_rows(b)[:, :, D:D + beside], own_t[:, bass.ds(k * CT, CT), :])
                            ins.then_inc(chunk_copied.sem, 1)
                            act.wait_ge(chunk_copied.sem, chunk_copied.past(k + 1))
                            act.dma_start(target[bass.ds(k * CE, CE), :].rearrange("(t p) d -> p t d", p=P), written_rows(b)
                                          ).then_inc(written[b].sem, 16)
                            stage_numbers(k + 1 + NB, (c + 1) % NB)
                    for b in range(2):
                        act.wait_ge(written[b].sem, written[b].past(16 * CHUNKS // 2))
            idx_staged.base += CHUNKS + NB + 1
            for c in gathered:
                c.base += 16 * CT * ITERS
            for c in (chunk_turned, chunk_scanned, chunk_back, chunk_copied):
                c.base += CHUNKS
            if mode != "plain":
                chunk_weighted.base += CHUNKS
            for w in written:
                w.base += 16 * CHUNKS // 2
            for m in mask_loaded:
                m.base += 16 * ITERS

        def gather_results(pool, to, table, width):
            def arrived(i):
                pool.wait_ge(group_rows[i % 2].sem, group_rows[i % 2].past((i // 2 + 1) * 16 * NG))
                pool.sem_inc(group_here.sem, 1)

            for i in range(groups):
                for j in range(i * NG, (i + 1) * NG):
                    nc.gpsimd.indirect_dma_start(out=to[:, j, 0:width], out_offset=None, in_=table[:, :],
                                                 in_offset=bass.IndirectOffsetOnAxis(ap=last_idx[:, j:j + 1], axis=0)
                                                 ).then_inc(group_rows[i % 2].sem, 16)
                if i > 0:
                    arrived(i - 1)
            arrived(groups - 1)

        def results_gathered():
            for b in range(2):
                group_rows[b].base += 16 * NG * ((groups + 1 - b) // 2)
            group_here.base += groups

        def stage(s):
            return weighted_flat[:, s * NG * P:(s + 1) * NG * P]

        def lhs(s):
            return weighted_flat[:, (2 + s) * NG * P:(3 + s) * NG * P]

        def group_steps(engine, begin, step):
            begin()
            with engine.Fori(0, (groups - 2) // 2) as pair:
                for b in range(2):
                    step(pair * 2 + b, b, 2)
            for i in range((groups - 2) // 2 * 2, groups):
                step(i, i % 2, min(groups - 1 - i, 2))

        def project(ns, front, by_tile, by_group, post, begin=None, scalar_front=None, scalar_post=None, gathers=None, store=None,
                    buffers=None):
            turns = (pa, pd)

            def uses(buf):
                return (NG - buf + NS - 1) // NS

            def turned_input(s, b):
                if ns == 1:
                    return weighted_flat[:, (1 + b) * NG * P:(2 + b) * NG * P]
                return weighted_flat[:, (2 + s) * NG * P:(3 + s) * NG * P] if b == 0 else more_lhs[s]

            with nc.Block() as block:
                if gathers is not None:
                    @block.gpsimd
                    def _(pool):
                        gathers(pool)

                @block.vector
                def _(dve):
                    def begin_fronts():
                        front(dve, 0)
                        front(dve, 1)

                    def step(i, b, left):
                        if left > 1:
                            front(dve, i + 2)
                        dve.wait_ge(group_product.sem, group_product.past(i + 1))
                        post(dve, i, b)

                    group_steps(dve, begin_fronts, step)

                @block.tensor
                def _(pe):
                    def turn(i, first=False):
                        pe.wait_ge(group_staged.sem, group_staged.past((i + 1) * ns))
                        if not first:
                            pe.wait_ge(group_lhs.sem, group_lhs.past(i))
                        for s in range(ns):
                            for t in range(NG):
                                ins = nc.tensor.transpose(turns[s][:, t * P:(t + 1) * P], stage(s)[:, t * P:(t + 1) * P], ident[:, :])
                        ins.then_inc(group_turned.sem, 1)

                    def multiply(i, b):
                        pe.wait_ge(group_lhs.sem, group_lhs.past(i + 1))
                        pe.wait_ge(group_kept.sem, group_kept.past(i if by_tile is not None else i - 1))
                        for t in range(NG):
                            if by_tile is not None:
                                ws, bias, n, _ = by_tile
                                pe.wait_ge(tile_out.sem, tile_out.by_last_lap(i * NG + (t + 1 if t > 1 else 2 - t)))
                                to = pb[:, t % 2 * CE:t % 2 * CE + n]
                                ins = nc.tensor.matmul(to, turned_input(0, b)[:, t * P:(t + 1) * P], ws, start=True, stop=(bias is None))
                                if bias is not None:
                                    ins = nc.tensor.matmul(to, one_rows[:, :], bias, start=False, stop=True)
                                ins.then_inc(tile_product.sem, 1)
                            ws, bias, n = by_group
                            to = products(b if by_tile is None else 0)[:, t * n:(t + 1) * n]
                            for s in range(ns):
                                ins = nc.tensor.matmul(to, turned_input(s, b)[:, t * P:(t + 1) * P], ws[s],
                                                       start=(s == 0), stop=(bias is None and s == ns - 1))
                            if bias is not None:
                                ins = nc.tensor.matmul(to, one_rows[:, :], bias, start=False, stop=True)
                        ins.then_inc(group_product.sem, 1)

                    def step(i, b, left):
                        if left > 0:
                            turn(i + 1)
                        multiply(i, b)

                    group_steps(pe, lambda: turn(0, True), step)

                @block.scalar
                def _(act):
                    def keep(i, b):
                        act.wait_ge(group_turned.sem, group_turned.past(i + 1))
                        act.wait_ge(group_product.sem, group_product.past(i - 1))
                        for s in range(ns):
                            ins = nc.scalar.copy(turned_input(s, b), turns[s][:, 0:NG * P])
                        ins.then_inc(group_lhs.sem, 1)

                    def copy_product(i, t):
                        n, b, buf = by_tile[2], t % 2, t % NS
                        act.wait_ge(tile_product.sem, tile_product.past(i * NG + t + 1))
                        use = i * uses(buf) + t // NS
                        act.wait_ge(tile_stored[buf].sem, tile_stored[buf].by_last_lap(use * 16 + 16))
                        nc.scalar.copy(buffers[:, buf * CE:buf * CE + n], pb[:, b * CE:b * CE + n]).then_inc(tile_out.sem, 1)

                    def begin_groups():
                        if begin is not None:
                            begin(act)
                        scalar_front(act, 0)
                        keep(0, 0)
                        scalar_front(act, 1)

                    def step(i, b, left):
                        if left > 0:
                            keep(i + 1, 1 - b)
                        if by_tile is not None:
                            for t in range(NG):
                                if t == NG - 2 and left > 1:
                                    scalar_front(act, i + 2)
                                copy_product(i, t)
                        else:
                            if left > 1:
                                scalar_front(act, i + 2)
                            act.wait_ge(group_product.sem, group_product.past(i + 1))
                            scalar_post(act, i, b)

                    group_steps(act, begin_groups, step)

                @block.sync
                def _(sp):
                    if by_tile is not None:
                        n, rows = by_tile[2:]
                        with sp.Fori(0, groups) as i:
                            for t in range(NG):
                                buf = t % NS
                                sp.wait_ge(tile_out.sem, tile_out.past(i * NG + t + 1))
                                to, kept = rows(i * NG + t), buffers[:, buf * CE:buf * CE + n]
                                sp.dma_start(to, kept if len(to.shape) == 2 else kept.rearrange("p (r d) -> p r d", d=D)
                                             ).then_inc(tile_stored[buf].sem, 16)
                        for buf in range(NS):
                            sp.wait_ge(tile_stored[buf].sem, tile_stored[buf].past(16 * uses(buf) * groups))
                    if store is not None:
                        store(sp)
            group_staged.base += ns * groups
            for c in (group_turned, group_lhs, group_product, group_kept):
                c.base += groups
            if by_tile is not None:
                tile_product.base += NT
                tile_out.base += NT
                for buf in range(NS):
                    tile_stored[buf].base += 16 * uses(buf) * groups
            if gathers is not None:
                results_gathered()

        def products(b):
            return (pc, pb)[b]

        def middle(t, i):
            return t[:, bass.ds(i * NG, NG), :]

        def group_wide(t):
            return t.unsqueeze(2).broadcast_to([P, NG, D])

        def group_across(t):
            return t.unsqueeze(1).broadcast_to([P, NG, D])

        def as_tiles(t):
            return t.rearrange("p (t d) -> p t d", d=D)

        LN_STEPS = 4

        def layernorm_group(dve, step, i, x_i, outs, done=None):
            v = nc.vector
            mu, var = moments[:, :, 0], ln_stat[:, 1, :]
            for t in range(NG):
                ins = v.bn_stats(out=row_stats[:, t, :], in_=x_i[:, t, :])
            step(ins, apart=True)
            for t in range(NG):
                ins = v.bn_aggr(out=moments[:, t, :], in_=row_stats[:, t, :])
            step(ins)
            if not (isinstance(i, int) and i == 0):
                c = done or group_staged
                dve.wait_ge(c.sem, c.past(i))
            v.tensor_scalar(var, moments[:, :, 1], LN_EPS, None, ALU.add).then_inc(to_scalar.sem, 1)
            step(v.tensor_tensor(as_tiles(T1), x_i, group_wide(mu), ALU.subtract))
            dve.wait_ge(to_vector.sem, to_vector.past(i + 1))
            step(v.reciprocal(mu, var))
            if done is None:
                dve.wait_ge(group_turned.sem, group_turned.by_last_lap(i + 1))
            for to in outs:
                ins = v.scalar_tensor_tensor(out=to, in0=as_tiles(T1), scalar=0.0, in1=group_wide(mu), op0=ALU.max, op1=ALU.mult)
            ins.then_inc((done or group_staged).sem, 1)

        def deviations(act, i):
            act.wait_ge(to_scalar.sem, to_scalar.past(i + 1))
            nc.scalar.activation(ln_stat[:, 1, :], ln_stat[:, 1, :], ACT.Sqrt).then_inc(to_vector.sem, 1)

        def feed_forward():
            hidden = [weighted_flat[:, NG * P:2 * NG * P], weighted_flat[:, 3 * NG * P:4 * NG * P], T1, T2]
            nk = FF // P
            ups = (pb, pd)

            with nc.Block() as block:
                @block.tensor
                def _(pe):
                    def turn(i):
                        pe.wait_ge(group_staged.sem, group_staged.past(i + 1))
                        for t in range(NG):
                            ins = nc.tensor.transpose(pa[:, t * P:(t + 1) * P], stage(0)[:, t * P:(t + 1) * P], ident[:, :])
                        ins.then_inc(group_turned.sem, 1)

                    def multiply(i, more):
                        pe.wait_ge(group_lhs.sem, group_lhs.past(i + 1))
                        for k in range(nk):
                            pe.wait_ge(ff_hidden.sem, ff_hidden.by_last_lap(i * nk + k + 1))
                            for lo, hi in ((0, CE), (CE, NG * P)):
                                ins = nc.tensor.matmul(ups[k % 2][:, lo:hi], ff1[:, k * P:(k + 1) * P], lhs(0)[:, lo:hi],
                                                       start=True, stop=True)
                            ins.then_inc(ff_up.sem, 1)
                        if more:
                            turn(i + 1)
                        pe.wait_ge(ff_hidden.sem, ff_hidden.past((i + 1) * nk))
                        pe.wait_ge(ff_kept.sem, ff_kept.by_last_lap(i + 1))
                        for t in range(NG):
                            for k in range(nk):
                                ins = nc.tensor.matmul(pc[:, t * P:(t + 1) * P], hidden[k][:, t * P:(t + 1) * P], ff2[:, k, :],
                                                       start=(k == 0), stop=(k == nk - 1))
                        ins.then_inc(ff_down.sem, 1)

                    turn(0)
                    with pe.Fori(0, groups - 1) as i:
                        multiply(i, True)
                    multiply(groups - 1, False)

                @block.scalar
                def _(act):
                    def keep(i):
                        act.wait_ge(ff_up.sem, ff_up.past(i * nk))
                        act.wait_ge(group_turned.sem, group_turned.past(i + 1))
                        nc.scalar.copy(lhs(0), pa[:, 0:NG * P]).then_inc(group_lhs.sem, 1)

                    def activate(i, more):
                        for k in range(nk):
                            act.wait_ge(ff_down.sem, ff_down.by_last_lap(i + 1))
                            act.wait_ge(ff_up.sem, ff_up.past(i * nk + k + 1))
                            nc.scalar.activation(hidden[k], ups[k % 2][:, 0:NG * P], ACT.Relu, bias=ff1_b[:, k:k + 1]
                                                 ).then_inc(ff_hidden.sem, 1)
                        if more:
                            keep(i + 1)

                    keep(0)
                    with act.Fori(0, groups - 1) as i:
                        activate(i, True)
                    activate(groups - 1, False)

                @block.vector
                def _(dve):
                    v = nc.vector

                    def normalise(i):
                        step = front_step.of(dve, i, 2)
                        g_i = middle(g2, i)
                        step(v.tensor_tensor(g_i, g_i, group_across(mean[:, :]), ALU.mult))
                        b1 = group_across(vec["L1_gnn_bn1_b"][:, :])
                        step(v.tensor_tensor(middle(h, i), g_i, b1, ALU.add))
                        dve.wait_ge(group_turned.sem, group_turned.by_last_lap(i + 1))
                        v.tensor_tensor(as_tiles(stage(0)), g_i, b1, ALU.add).then_inc(group_staged.sem, 1)

                    def finish(i, more):
                        if more:
                            normalise(i + 1)
                        step = post_step.of(dve, i, 1)
                        g_i = middle(g, i)
                        dve.wait_ge(ff_down.sem, ff_down.past(i + 1))
                        step(v.tensor_tensor(g_i, pc[:, 0:NG * P].rearrange("p (t d) -> p t d", d=D),
                                             group_across(vec["L1_gnn_b2"][:, :]), ALU.add))
                        v.tensor_tensor(g_i, g_i, middle(h, i), ALU.add).then_inc(ff_kept.sem, 1)

                    normalise(0)
                    with dve.Fori(0, groups - 1) as i:
                        finish(i, True)
                    finish(groups - 1, False)
            front_step.done(groups)
            post_step.done(groups)
            group_staged.base += groups
            group_turned.base += groups
            group_lhs.base += groups
            ff_up.base += nk * groups
            ff_hidden.base += nk * groups
            ff_down.base += groups
            ff_kept.base += groups

        def add_columns(pe, rows, i, first=False, last=False):
            for lo, hi in ((0, 4), (4, NG - 1 if last else NG)):
                ins = nc.tensor.matmul(pa[:, lo * D:hi * D], ones[:, :],
                                       rows[:, bass.ds(i * NG + lo, hi - lo), :].rearrange("p j d -> p (j d)"),
                                       start=first, stop=(last and lo == 0))
            if last:
                ins = nc.tensor.matmul(pa[:, (NG - 1) * D:NG * D], ones_tail[:, :], rows[:, NT - 1, :], start=False, stop=True)
            return ins

        def sum_columns(pe, rows, ready):
            def add(i, **ends):
                if ready is not None:
                    pe.wait_ge(ready.sem, ready.past(i + 1))
                return add_columns(pe, rows, i, **ends)

            add(0, first=True)
            with pe.Fori(1, groups - 1) as i:
                add(i)
            return add(groups - 1, last=True)

        def summed_columns():
            return pa[:, 0:NG * D].rearrange("p (k d) -> p d k", d=D)

        def batchnorm(rows, w):
            with nc.Block() as block:
                @block.vector
                def _(dve):
                    v = nc.vector
                    step(dve, v.tensor_reduce(mean[:, :], summed_columns(), AX.X, ALU.add))
                    step(dve, v.tensor_scalar(mean[:, :], mean[:, :], 1.0 / N, None, ALU.mult))
                    with dve.Fori(0, groups) as i:
                        v.tensor_tensor(middle(g2, i), middle(rows, i), group_across(mean[:, :]), ALU.subtract).then_inc(to_scalar.sem, 1)
                    dve.wait_ge(sums_ready.sem, sums_ready.past(1))
                    step(dve, v.tensor_reduce(gain[:, :], summed_columns(), AX.X, ALU.add))
                    v.tensor_scalar(gain[:, :], gain[:, :], 1.0 / N, LN_EPS, ALU.mult, ALU.add).then_inc(sums_ready.sem, 1)
                    dve.wait_ge(sums_ready.sem, sums_ready.past(3))
                    step(dve, v.reciprocal(mean[:, :], gain[:, :]))
                    v.tensor_tensor(mean[:, :], mean[:, :], w, ALU.mult)

                @block.scalar
                def _(act):
                    with act.Fori(0, groups) as i:
                        wait_apart(act, to_scalar.sem, to_scalar.past(i + 1))
                        nc.scalar.activation(middle(rows, i), middle(g2, i), ACT.Square).then_inc(to_vector.sem, 1)
                    act.wait_ge(sums_ready.sem, sums_ready.past(2))
                    nc.scalar.activation(gain[:, :], gain[:, :], ACT.Sqrt).then_inc(sums_ready.sem, 1)

                @block.tensor
                def _(pe):
                    sum_columns(pe, rows, to_vector).then_inc(sums_ready.sem, 1)
            sums_ready.base += 3
            to_scalar.base += groups
            to_vector.base += groups

        EA = weighted_flat[0:ER, 0:H1 * EC].rearrange("q (h f) -> q h f", f=EC)
        FROM_DST = arena[0:ER, 0:2 * H1 * EC].rearrange("q (h f) -> q h f", f=EC)
        START = arena[0:ER, 2 * H1 * EC:4 * H1 * EC]
        M = arena[0:ER, 2 * H1 * EC:3 * H1 * EC].rearrange("q (h f) -> q h f", f=EC)
        own_t = arena[:, 8192:8192 + ET * H1].rearrange("p (t h) -> p t h", h=H1)
        DEN = arena[0:ER, 3 * H1 * EC:4 * H1 * EC].rearrange("q (h f) -> q h f", f=EC)

        def segment_scan(n, to, of, kind):
            with_, flag, op0, op1, start = {"sum": (keep, 0, ALU.mult, ALU.add, 0.0),
                                            "max": (cut, 1, ALU.add, ALU.max, -BIG),
                                            "spread": (notlast, 2, ALU.mult, ALU.add, 0.0)}[kind]
            way = slice(None, None, -1) if kind == "spread" else slice(None)
            end = 0 if kind == "spread" else EC - 1
            into = (0, ER) if kind == "spread" else (1, ER + 1)
            out_of = (1, ER + 1) if kind == "spread" else (0, ER)

            with nc.Block() as block:
                @block.vector
                def _(dve):
                    v = nc.vector
                    for k in range(n):
                        step(dve, v.tensor_tensor_scan(to(k)[:, way], with_[:, way], of(k)[:, way], start, op0, op1))
                        v.tensor_copy(ends[:, 0, k:k + 1], to(k)[:, end:end + 1])
                    v.memset(ends_row[:, 0:1], start)
                    v.memset(ends_row[:, ER:ER + 1], start).then_inc(ends_ready.sem, 1)
                    dve.wait_ge(turned.sem, turned.past(1))
                    v.tensor_tensor_scan(ends_row[0:n, into[0]:into[1]][:, way], whole[0:n, flag, 0:ER][:, way],
                                         pa[0:n, 0:ER][:, way], start, op0, op1).then_inc(ends_ready.sem, 1)
                    dve.wait_ge(turned.sem, turned.past(2))
                    step(dve, v.tensor_copy(carry[:, 0:n], pb[0:ER, 0:n]))
                    for k in range(n):
                        v.tensor_tensor_scan(to(k)[:, way], with_[:, way], of(k)[:, way], carry[:, k:k + 1], op0, op1)

                @block.tensor
                def _(pe):
                    pe.wait_ge(ends_ready.sem, ends_ready.past(1))
                    nc.tensor.transpose(pa[:, 0:ER], ends[:, 0, :], ident[0:ER, 0:ER]).then_inc(turned.sem, 1)
                    pe.wait_ge(ends_ready.sem, ends_ready.past(2))
                    nc.tensor.transpose(pb[0:ER, 0:P], ends_row[:, out_of[0]:out_of[1]], ident[:, :]).then_inc(turned.sem, 1)
            ends_ready.base += 2
            turned.base += 2

        def look_up_scores(heads, start_rows, width):
            hots = weighted_flat[:, 0:NB * CE].bitcast(BF16).rearrange("p (b a n) -> p b a n", b=NB, a=2)
            hot_hi = weighted_flat[0:HI, NB * CE:NB * CE * 3 // 2].bitcast(BF16).rearrange("p (b n) -> p b n", b=NB)
            lo_b = arena[:, 0:LQ * CE].bitcast(BF16).rearrange("p (c n) -> p c n", n=CE)
            hi_b = arena[0:HI, LQ * CE:2 * LQ * CE].bitcast(BF16).rearrange("p (c n) -> p c n", n=CE)
            apart = weighted_flat[:, 7 * CE:8 * CE].bitcast(BF16).rearrange("p (b n) -> p b n", b=2)
            value_slot = startval_slot[:, 0:width]
            ways = heads * HI
            picks = [(pa, pb)[c // 2][:, c % 2 * CE:c % 2 * CE + CT * ways] for c in range(NB)]

            by_vector = (6,) if heads == H1 else (1, 3, 5)
            by_scalar = [c for c in range(LB) if c % 7 not in by_vector]
            LS = len(by_scalar)
            assert LS % 2 == 0

            def scalars(i, c):
                return i * LS + sum(b % LB in by_scalar for b in range(c)) - sum(b % LB in by_scalar for b in range(c, 0))

            def numbers_here(engine, i, c, always=False):
                if always or c % LQ == 0:
                    half, use = c // LQ % 2, i * 2 + c // (2 * LQ)
                    engine.wait_ge(numbers_loaded[half].sem, numbers_loaded[half].past((use + 1) * 32))

            with nc.Block() as block:
                @block.vector
                def _(dve):
                    v = nc.vector
                    rest = nodeval[:, :, 0:heads].rearrange("p j h -> p h j")
                    for k in range(3):
                        part = parts[:, k, 0:heads, 0:NT]
                        ins = v.tensor_copy(part, rest)
                        if k < 2:
                            step(dve, ins)
                            step(dve, v.tensor_tensor(rest, rest, part, ALU.subtract))
                    ins.then_inc(sums_ready.sem, 1)

                    def make_hot(i, c):
                        k, b, s = i * LB + c, c % NB, c % (2 * LQ)
                        numbers_here(dve, i, c)
                        dve.wait_ge(picked.sem, picked.by_last_lap(k + 1))
                        for a in range(2):
                            if a == 1 or c % LB not in by_scalar:
                                v.tensor_scalar(hots[:, b, a, :], lo_b[:, s, :], number[:, a:a + 1], None, ALU.is_equal)
                        v.tensor_scalar(hot_hi[:, b, :], hi_b[:, s, :], number[0:HI, 0:1], None, ALU.is_equal
                                        ).then_inc(hot_made[1].sem, 1)

                    def take_one(i, c, more):
                        if not isinstance(i, int) or c + 2 < LB:
                            make_hot(i, c + 2)
                        k = i * LB + c
                        wait_apart(dve, picked.sem, picked.past(k + 1))
                        v.tensor_reduce(alpha[:, bass.ds(k * CT, CT), 0:heads],
                                        picks[c % NB].rearrange("p (t h j) -> p t h j", h=heads, j=HI), AX.X, ALU.max
                                        ).then_inc(summed.sem, 1)

                    def begin():
                        make_hot(0, 0)
                        make_hot(0, 1)

                    laps(dve, begin, take_one, LB, CHUNKS // LB)

                @block.tensor
                def _(pe):
                    pe.wait_ge(sums_ready.sem, sums_ready.past(1))
                    with pe.Fori(0, CHUNKS // LB) as i:
                        for c in range(LB):
                            k, b = i * LB + c, c % NB
                            pe.wait_ge(hot_made[1].sem, hot_made[1].past(k + 1))
                            if c in by_scalar:
                                pe.wait_ge(hot_made[0].sem, hot_made[0].past(scalars(i, c + 1)))
                            pe.wait_ge(summed.sem, summed.by_last_lap(k + 1))
                            for t in range(CT):
                                to = picks[c % NB][:, t * ways:(t + 1) * ways].rearrange("p (h j) -> p h j", j=HI)
                                nc.tensor.matmul(to, hot_hi[:, b, t * P:(t + 1) * P], other_hi[:, 0:heads, :], start=True, stop=False)
                                for a in range(2):
                                    for n in range(3):
                                        ins = nc.tensor.matmul(to, hots[:, b, a, t * P:(t + 1) * P],
                                                               parts[:, n, 0:heads, a:a + 2 * HI - 1:2],
                                                               start=False, stop=(a == 1 and n == 2))
                            ins.then_inc(picked.sem, 1)

                @block.scalar
                def _(act):
                    def distances(i, m):
                        c = by_scalar[m % LS] + m // LS * LB
                        numbers_here(act, i, c, always=True)
                        act.wait_ge(hot_made[0].sem, hot_made[0].past(i * LS + m - 1))
                        nc.scalar.activation(apart[:, m % 2, :], lo_b[:, c % (2 * LQ), :], ACT.Abs, bias=number[:, 2:3]
                                             ).then_inc(lo_apart.sem, 1)

                    def make_hot(i, m, more):
                        if more:
                            distances(i, m + 1)
                        c = by_scalar[m]
                        act.wait_ge(picked.sem, picked.by_last_lap(i * LB + c + 1))
                        act.wait_ge(lo_apart.sem, lo_apart.past(i * LS + m + 1))
                        nc.scalar.activation(hots[:, c % NB, 0, :], apart[:, m % 2, :], ACT.Relu, bias=ones[:, 0:1], scale=-1.0
                                             ).then_inc(hot_made[0].sem, 1)

                    laps(act, lambda: distances(0, 0), make_hot, LS, CHUNKS // LB)

                @block.gpsimd
                def _(pool):
                    with pool.Fori(0, ITERS) as i:
                        wait_apart(pool, rows_moved.sem, rows_moved.past(16 * i))
                        nc.gpsimd.tensor_copy(slot[:, 0, 0:1], start_idx[:, bass.ds(i, 1)]).then_inc(idx_staged.sem, 1)
                        nc.gpsimd.tensor_copy(value_slot, startval[:, bass.ds(i, 1), 0:width].rearrange("p j w -> p (j w)")
                                              ).then_inc(idx_staged.sem, 1)
                        wait_apart(pool, idx_staged.sem, idx_staged.past(2 * i + 2))
                        nc.gpsimd.indirect_dma_start(out=start_rows[:, :],
                                                     out_offset=bass.IndirectOffsetOnAxis(ap=slot[:, 0, 0:1], axis=0),
                                                     in_=value_slot, in_offset=None, bounds_check=EP - 1,
                                                     oob_is_err=False).then_inc(rows_moved.sem, 16)
                    pool.wait_ge(rows_moved.sem, rows_moved.past(16 * NT))

                @block.sync
                def _(sp):
                    with sp.Fori(0, CHUNKS // LB) as i:
                        for q in range(LB // LQ):
                            k, half = i * LB + q * LQ, q % 2
                            wait_apart(sp, hot_made[1].sem, hot_made[1].past(k - LQ))
                            sp.wait_ge(hot_made[0].sem, hot_made[0].past(scalars(i, (q - 1) * LQ)))
                            for to, row, n in ((lo_b, lo_row, P), (hi_b, hi_row, HI)):
                                sp.dma_start(to[:, half * LQ:(half + 1) * LQ, :].rearrange("p c n -> p (c n)"),
                                             row[0:1, bass.ds(k * CE, LQ * CE)].broadcast_to([n, LQ * CE])
                                             ).then_inc(numbers_loaded[half].sem, 16)
                    sp.wait_ge(rows_moved.sem, rows_moved.past(16 * NT))
                    sp.dma_start(START[:, 0:width * EC], start_rows.rearrange("(q f) w -> q (f w)", f=EC)).then_inc(loaded.sem, 16)
                    sp.wait_ge(loaded.sem, loaded.past(16))
            loaded.base += 16
            sums_ready.base += 1
            idx_staged.base += 2 * NT
            rows_moved.base += 16 * NT
            for c in (hot_made[1], picked, summed):
                c.base += CHUNKS
            for c in (hot_made[0], lo_apart):
                c.base += scalars(CHUNKS // LB, 0)
            for m in numbers_loaded:
                m.base += 32 * (CHUNKS // (2 * LQ))

        def attention(heads, start_rows, with_self):
            width = 2 * heads if with_self else heads
            look_up_scores(heads, start_rows, width)
            start = START[:, 0:width * EC].rearrange("q (f w) -> q w f", w=width)
            segment_scan(width, lambda k: FROM_DST[:, k, :], lambda k: start[:, k, :], "sum")
            scores_to_rows(heads)
            e, den, m = EA[:, 0:heads, :], DEN[:, 0:heads, :], M[:, 0:heads, :]
            with nc.Block() as block:
                @block.vector
                def _(dve):
                    v = nc.vector
                    step(dve, v.tensor_tensor(e, e, FROM_DST[:, 0:heads, :], ALU.add))
                    v.scalar_tensor_tensor(out=e, in0=e, scalar=0.2, in1=e, op0=ALU.mult, op1=ALU.max)
            segment_scan(heads, lambda k: M[:, k, :], lambda k: EA[:, k, :], "max")

            def by_last(t):
                return last[:, :].unsqueeze(1).broadcast_to([ER, heads, EC])

            with nc.Block() as block:
                @block.vector
                def _(dve):
                    nc.vector.tensor_tensor(den, m, by_last(m), ALU.mult)
            segment_scan(heads, lambda k: M[:, k, :], lambda k: DEN[:, k, :], "spread")
            with nc.Block() as block:
                @block.vector
                def _(dve):
                    v = nc.vector
                    if with_self:
                        own = FROM_DST[:, heads:2 * heads, :]
                        step(dve, v.tensor_tensor(m, m, own, ALU.max))
                        v.tensor_tensor(own, own, m, ALU.subtract)
                    v.tensor_tensor(e, e, m, ALU.subtract).then_inc(sums_ready.sem, 1)

                @block.scalar
                def _(act):
                    act.wait_ge(sums_ready.sem, sums_ready.past(1))
                    nc.scalar.activation(e, e, ACT.Exp)
                    if with_self:
                        nc.scalar.activation(FROM_DST[:, heads:2 * heads, :], FROM_DST[:, heads:2 * heads, :], ACT.Exp)
            sums_ready.base += 1
            segment_scan(heads, lambda k: M[:, k, :], lambda k: EA[:, k, :], "sum")
            with nc.Block() as block:
                @block.vector
                def _(dve):
                    step(dve, nc.vector.tensor_tensor(den, m, by_last(m), ALU.mult))
            segment_scan(heads, lambda k: M[:, k, :], lambda k: DEN[:, k, :], "spread")
            with nc.Block() as block:
                @block.vector
                def _(dve):
                    v = nc.vector
                    if with_self:
                        own = FROM_DST[:, heads:2 * heads, :]
                        step(dve, v.tensor_tensor(m, m, own, ALU.add))
                    else:
                        step(dve, v.tensor_scalar(m, m, 1e-16, None, ALU.add))
                    step(dve, v.reciprocal(m, m))
                    if with_self:
                        v.tensor_tensor(own, own, m, ALU.mult)
                    v.tensor_tensor(e, e, m, ALU.mult)
            turns = [(EA[:, hd, :], alpha[:, :, hd]) for hd in range(heads)]
            if with_self:
                turns += [(FROM_DST[:, heads + hd, :], own_t[:, :, hd]) for hd in range(heads)]
            with nc.Block() as block:
                @block.tensor
                def _(pe):
                    for k, (row, _) in enumerate(turns):
                        if k >= 2:
                            pe.wait_ge(ends_ready.sem, ends_ready.past(k - 1))
                        for f in range(TQ):
                            ins = nc.tensor.transpose((pa, pb)[k % 2][:, f * P:f * P + ER], row[:, f * P:(f + 1) * P],
                                                      ident[0:ER, 0:ER])
                        ins.then_inc(turned.sem, 1)

                @block.vector
                def _(dve):
                    for k, (_, tiles) in enumerate(turns):
                        dve.wait_ge(turned.sem, turned.past(k + 1))
                        nc.vector.tensor_copy(tiles.rearrange("p (q f) -> p f q", f=TQ),
                                              (pa, pb)[k % 2][:, 0:TQ * P].rearrange("p (f q) -> p f q", q=P)[:, :, 0:ER]
                                              ).then_inc(ends_ready.sem, 1)
            turned.base += len(turns)
            ends_ready.base += len(turns)

        def scores_to_rows(heads):
            with nc.Block() as block:
                @block.tensor
                def _(pe):
                    for hd in range(heads):
                        if hd >= 2:
                            pe.wait_ge(ends_ready.sem, ends_ready.past(hd - 1))
                        tiles = alpha[:, :, hd].rearrange("p (q f) -> p f q", f=TQ)
                        for f in range(TQ):
                            ins = nc.tensor.transpose((pa, pb)[hd % 2][0:ER, f * P:(f + 1) * P], tiles[:, f, :], ident[:, :])
                        ins.then_inc(turned.sem, 1)

                @block.vector
                def _(dve):
                    for hd in range(heads):
                        dve.wait_ge(turned.sem, turned.past(hd + 1))
                        nc.vector.tensor_copy(EA[:, hd, :], (pa, pb)[hd % 2][0:ER, 0:EC]).then_inc(ends_ready.sem, 1)
            turned.base += heads
            ends_ready.base += heads

        T1, T2 = arena[:, 2 * NT * D:2 * NT * D + NG * D], arena[:, 2 * NT * D + NG * D:2 * NT * D + 2 * NG * D]
        T3 = arena[:, NT * D:NT * D + NG * D]
        more_lhs = [arena[:, NT * D + k * NG * D:NT * D + (k + 1) * NG * D] for k in (1, 2)]

        with nc.Block() as block:
            @block.vector
            def _(dve):
                with dve.Fori(0, groups) as i:
                    layernorm_group(dve, front_step.of(dve, i, LN_STEPS), i, middle(x, i), (middle(h, i),), group_kept)

            @block.scalar
            def _(act):
                with act.Fori(0, groups) as i:
                    deviations(act, i)

            @block.sync
            def _(sp):
                with sp.Fori(0, groups) as i:
                    sp.wait_ge(group_kept.sem, group_kept.past(i + 1))
                    sp.dma_start(h_tab[bass.ds(i * NG * P, NG * P), :].rearrange("(j p) d -> p j d", p=P), middle(h, i)
                                 ).then_inc(stored.sem, 16)
                sp.wait_ge(stored.sem, stored.past(16 * groups))
        front_step.done(groups)
        stored.base += 16 * groups
        for c in (group_kept, to_scalar, to_vector):
            c.base += groups
        edge_pass(h_tab, D, src_idx, keep_row, ALU.mult, ALU.add, "count")

        cum = arena[0:NT, 0:P]
        firsts = arena[0:NT, 2 * P:3 * P]
        has = arena[0:NT, 3 * P:4 * P]
        total = arena[0:NT, 4 * P:4 * P + 1]
        offset = arena[0:NT, 4 * P + 1:4 * P + 2]
        with nc.Block() as block:
            @block.vector
            def _(dve):
                v = nc.vector
                cnt = counts[0:NT, :]
                v.tensor_scalar(has, cnt, 1.0, None, ALU.min)
                step(dve, v.tensor_reduce(total, cnt, AX.X, ALU.add))
                v.tensor_tensor_scan(cum, ones[0:NT, :], cnt, 0.0, ALU.mult, ALU.add).then_inc(ends_ready.sem, 1)
                dve.wait_ge(turned.sem, turned.past(1))
                step(dve, v.tensor_copy(offset, pa[0:NT, 0:1]))
                step(dve, v.tensor_scalar(cum, cum, offset, None, ALU.add))
                step(dve, v.tensor_tensor(firsts, cum, cnt, ALU.subtract))
                v.tensor_scalar(cum, cum, -1.0 - EP, None, ALU.add)
                step(dve, v.tensor_scalar(firsts, firsts, -float(SKIP), None, ALU.add))
                v.tensor_tensor(cum, cum, has, ALU.mult)
                step(dve, v.tensor_tensor(firsts, firsts, has, ALU.mult))
                v.tensor_scalar(cum, cum, float(EP), None, ALU.add)
                step(dve, v.tensor_scalar(firsts, firsts, float(SKIP), None, ALU.add))
                v.tensor_scalar(has, cnt, 1.0, None, ALU.max).then_inc(ends_ready.sem, 1)
                dve.wait_ge(turned.sem, turned.past(2))
                v.tensor_copy(last_idx[:, :], pb[:, 0:NT])
                v.tensor_copy(start_idx[:, :], pb[:, P:P + NT])
                v.reciprocal(rcount[:, :], pb[:, 2 * P:2 * P + NT])

            @block.tensor
            def _(pe):
                pe.wait_ge(ends_ready.sem, ends_ready.past(1))
                nc.tensor.matmul(pa[0:NT, 0:1], before[:, :], total, start=True, stop=True).then_inc(turned.sem, 1)
                pe.wait_ge(ends_ready.sem, ends_ready.past(2))
                for k, t in enumerate((cum, firsts, has)):
                    ins = nc.tensor.transpose(pb[:, k * P:k * P + NT], t, ident[0:NT, 0:NT])
                ins.then_inc(turned.sem, 1)
        turned.base += 2
        ends_ready.base += 2

        def sage(layer):
            final = layer == 1

            def front(dve, i):
                dve.wait_ge(group_here.sem, group_here.past(i + 1))
                dve.wait_ge(group_turned.sem, group_turned.by_last_lap(i + 1))
                nc.vector.tensor_tensor(as_tiles(stage(0)), middle(g, i), group_wide(rcount[:, bass.ds(i * NG, NG)]), ALU.mult
                                        ).then_inc(group_staged.sem, 1)

            def scalar_front(act, i):
                wait_apart(act, group_turned.sem, group_turned.by_last_lap(i + 1))
                nc.scalar.copy(as_tiles(stage(1)), middle(h, i)).then_inc(group_staged.sem, 1)

            n_s, n_v = (2, 2) if final else (1, 1)

            def post(dve, i, b):
                v = nc.vector
                h_i, x_i = middle(h, i), middle(x, i)
                step = post_step.of(dve, i, 2 if final else 0)
                dve.wait_ge(group_kept.sem, group_kept.past(i))
                v.tensor_scalar(T1, products(b)[:, 0:NG * D], 0.0, None, ALU.min).then_inc(to_scalar.sem, 1)
                dve.wait_ge(to_vector.sem, to_vector.past(i * n_v + 1))
                ins = v.scalar_tensor_tensor(out=as_tiles(T3) if final else h_i, in0=as_tiles(T1), scalar=-1.0, in1=as_tiles(T2),
                                             op0=ALU.add, op1=ALU.add)
                if not final:
                    ins.then_inc(group_kept.sem, 1)
                    return
                step(ins)
                top = ln_stat[:, 0, :]
                step(v.tensor_reduce(top, as_tiles(T3), AX.X, ALU.max))
                v.tensor_tensor(as_tiles(T3), as_tiles(T3), group_wide(top), ALU.subtract).then_inc(to_scalar.sem, 1)
                dve.wait_ge(to_scalar.sem, to_scalar.past(i * n_s + 2))
                v.tensor_tensor(x_i, x_i, as_tiles(T3), ALU.add)
                wait_apart(dve, to_vector.sem, to_vector.past(i * n_v + 2))
                v.tensor_reduce(stat[:, 1, bass.ds(i * NG, NG)], as_tiles(T1), AX.X, ALU.add).then_inc(group_kept.sem, 1)

            def scalar_post(act, i, b):
                act.wait_ge(to_scalar.sem, to_scalar.past(i * n_s + 1))
                nc.scalar.activation(T1, T1, ACT.Exp)
                nc.scalar.activation(T2, products(b)[:, 0:NG * D], ACT.Relu).then_inc(to_vector.sem, 1)
                if final:
                    act.wait_ge(to_scalar.sem, to_scalar.past(i * n_s + 2))
                    nc.scalar.activation(T1, T3, ACT.Exp).then_inc(to_vector.sem, 1)

            def store(sp):
                for rows, width in ((start1_rows, 2 * H1), (start2_rows, H2)):
                    sp.dma_start(rows.rearrange("(p e) w -> p (e w)", p=P).rearrange("p (k f) -> p k f", f=ER),
                                 ends_row[:, 0:ER].unsqueeze(1).broadcast_to([P, EP * width // P // ER, ER])).then_inc(stored.sem, 16)
                with sp.Fori(0, groups) as i:
                    sp.wait_ge(group_kept.sem, group_kept.past(i + 1))
                    sp.dma_start(h_tab[bass.ds(i * NG * P, NG * P), :].rearrange("(j p) d -> p j d", p=P), middle(h, i)
                                 ).then_inc(stored.sem, 16)
                sp.wait_ge(stored.sem, stored.past(16 * (groups + 2)))

            project(2, front, None, ([w0[:, 2 * layer, :], w0[:, 2 * layer + 1, :]], bias_sum[:, layer * D:(layer + 1) * D], D),
                    post, scalar_front=scalar_front, scalar_post=scalar_post,
                    gathers=lambda pool: gather_results(pool, g, scan_rows, D), store=None if final else store)
            post_step.done(groups)
            to_scalar.base += n_s * groups
            to_vector.base += n_v * groups
            if not final:
                stored.base += 16 * (groups + 2)

        sage(0)
        edge_pass(h_tab, D, src_idx, keep_row, ALU.mult, ALU.add)
        sage(1)

        def front(dve, i):
            step = front_step.of(dve, i, 1 + LN_STEPS)
            x_i = middle(x, i)
            dve.wait_ge(sums_ready.sem, sums_ready.past(1))
            step(nc.vector.tensor_tensor(x_i, x_i, group_wide(stat[:, 0, bass.ds(i * NG, NG)]), ALU.subtract), apart=True)
            layernorm_group(dve, step, i, x_i, (middle(h, i), as_tiles(stage(0))))

        def logarithms(act):
            nc.scalar.activation(stat[:, 0, :], stat[:, 1, :], ACT.Ln).then_inc(sums_ready.sem, 1)

        def post(dve, i, b):
            nc.vector.tensor_copy(nodeval[:, bass.ds(i * NG, NG), :], products(0)[:, 0:NG * 2 * H1].rearrange("p (t k) -> p t k", k=2 * H1)
                                  ).then_inc(group_kept.sem, 1)

        project(1, front, (w1[:, :], None, H1 * D, lambda j: x1_tab[bass.ds(j * P, P), :]), ([sc1[:, :]], None, 2 * H1), post,
                begin=logarithms, scalar_front=deviations, buffers=arena[:, 0:NS * CE])
        sums_ready.base += 1
        front_step.done(groups)
        to_scalar.base += groups
        to_vector.base += groups
        with nc.Block() as block:
            @block.vector
            def _(dve):
                v = nc.vector
                s_src, s_dst = nodeval[:, :, 0:H1], nodeval[:, :, H1:2 * H1]
                v.tensor_copy(startval[:, :, 0:H1], s_dst)
                step(dve, v.tensor_tensor(startval[:, :, H1:2 * H1], s_src, s_dst, ALU.add))
                own = startval[:, :, H1:2 * H1]
                v.scalar_tensor_tensor(out=own, in0=own, scalar=0.2, in1=own, op0=ALU.mult, op1=ALU.max)
        attention(H1, start1_rows, True)
        with nc.Block() as block:
            @block.vector
            def _(dve):
                nc.vector.tensor_copy(pd[:, 0:P], ident[:, :])
        edge_pass(x1_tab, H1 * D, src_idx, keep_row, ALU.mult, ALU.add, "heads")

        DH = D + H1
        sums = arena[:, 0:NT * DH].rearrange("p (j d) -> p j d", d=DH)
        own_rows = [arena[:, NT * DH + b * NG * H1 * D:NT * DH + (b + 1) * NG * H1 * D].rearrange("p (t n) -> p t n", t=NG)
                    for b in range(2)]
        with nc.Block() as block:
            @block.gpsimd
            def _(pool):
                gather_results(pool, sums, scan1_rows, DH)

            @block.sync
            def _(sp):
                for i in range(groups):
                    b = i % 2
                    if i >= 2:
                        sp.wait_ge(group_kept.sem, group_kept.past(i - 1))
                    sp.dma_start(own_rows[b], x1_tab[i * NG * P:(i + 1) * NG * P, :].rearrange("(t p) n -> p t n", p=P)
                                 ).then_inc(own_loaded[b].sem, 16)

            @block.vector
            def _(dve):
                v = nc.vector

                def add_own(i, b, lap):
                    dve.wait_ge(own_loaded[b].sem, own_loaded[b].past(lap * 16 + 16))
                    dve.wait_ge(group_here.sem, group_here.past(i + 1))
                    step = front_step.of(dve, i, H1 + 1)
                    for hd in range(H1):
                        for t in range(NG):
                            j = bass.ds(i * NG + t, 1)
                            row = sums[:, j, 0:D].rearrange("p j d -> p (j d)")
                            ins = v.scalar_tensor_tensor(out=row, in0=own_rows[b][:, t, hd * D:(hd + 1) * D],
                                                         scalar=sums[:, j, D + hd:D + hd + 1].rearrange("p j d -> p (j d)"),
                                                         in1=row, op0=ALU.mult, op1=ALU.add)
                        step(ins)
                    h_i = middle(h, i)
                    step(v.scalar_tensor_tensor(out=h_i, in0=sums[:, bass.ds(i * NG, NG), 0:D], scalar=1.0 / H1, in1=h_i,
                                                     op0=ALU.mult, op1=ALU.add))
                    v.tensor_tensor(h_i, h_i, group_across(vec["L1_gnn_bias"][:, :]), ALU.add).then_inc(group_kept.sem, 1)

                with dve.Fori(0, groups // 2) as lap:
                    for b in range(2):
                        add_own(lap * 2 + b, b, lap)
                if groups % 2:
                    add_own(groups - 1, 0, groups // 2)

            @block.tensor
            def _(pe):
                sum_columns(pe, h, group_kept)
        results_gathered()
        front_step.done(groups)
        for b in range(2):
            own_loaded[b].base += 16 * ((groups + 1 - b) // 2)
        group_kept.base += groups
        batchnorm(h[:, :, :], vec["L1_gnn_bn1_w"][:, :])
        feed_forward()
        with nc.Block() as block:
            @block.tensor
            def _(pe):
                sum_columns(pe, g, None)
        batchnorm(g, vec["L1_gnn_bn2_w"][:, :])

        def front(dve, i):
            step = front_step.of(dve, i, 3 + LN_STEPS)
            v = nc.vector
            g_i, x_i = middle(g2, i), middle(x, i)
            step(v.tensor_tensor(g_i, g_i, group_across(mean[:, :]), ALU.mult))
            step(v.tensor_tensor(g_i, g_i, group_across(vec["L1_gnn_bn2_b"][:, :]), ALU.add))
            step(v.tensor_tensor(x_i, x_i, g_i, ALU.add), apart=True)
            layernorm_group(dve, step, i, x_i, (as_tiles(stage(0)),))

        def post(dve, i, b):
            nc.vector.tensor_copy(nodeval[:, bass.ds(i * NG, NG), 0:2 * H2], products(0)[:, 0:NG * 2 * H2].rearrange("p (t k) -> p t k", k=2 * H2)
                                  ).then_inc(group_kept.sem, 1)

        project(1, front, (w2[:, :], None, D, lambda j: h_tab[bass.ds(j * P, P), :]), ([sc2[:, :]], None, 2 * H2), post,
                scalar_front=deviations, buffers=arena[:, 0:NS * CE])
        front_step.done(groups)
        to_scalar.base += groups
        to_vector.base += groups
        with nc.Block() as block:
            @block.vector
            def _(dve):
                nc.vector.tensor_copy(startval[:, :, 0:H2], nodeval[:, :, H2:2 * H2])
        attention(H2, start2_rows, False)
        edge_pass(h_tab, D, src_idx, keep_row, ALU.mult, ALU.add, "halves")

        def front(dve, i):
            step = front_step.of(dve, i, 4 + LN_STEPS)
            v = nc.vector
            g_i, x_i = middle(g, i), middle(x, i)
            dve.wait_ge(group_here.sem, group_here.past(i + 1))
            step(v.tensor_tensor(g_i, g_i, group_across(vec["L2_gnn_bias"][:, :]), ALU.add))
            step(v.scalar_tensor_tensor(out=as_tiles(T1), in0=g_i, scalar=0.0, in1=group_across(vec["L2_gnn_prelu_w"][:, :]),
                                             op0=ALU.min, op1=ALU.mult))
            step(v.scalar_tensor_tensor(out=g_i, in0=g_i, scalar=0.0, in1=as_tiles(T1), op0=ALU.max, op1=ALU.add))
            step(v.tensor_tensor(x_i, x_i, g_i, ALU.add), apart=True)
            layernorm_group(dve, step, i, x_i, (as_tiles(stage(0)),))

        def post(dve, i, b):
            nc.vector.tensor_tensor(middle(x, i), middle(x, i), as_tiles(products(0)[:, 0:NG * D]), ALU.add).then_inc(group_kept.sem, 1)

        y_rows = y_tab.rearrange("(r n) d -> n r d", r=R)
        project(1, front, (w3[:, 0:R * D], bias_sum[:, 2 * D:(2 + R) * D], R * D, lambda j: y_rows[bass.ds(j * P, P), :, :]),
                ([w3[:, R * D:(R + 1) * D]], bias_sum[:, (2 + R) * D:(3 + R) * D], D), post, scalar_front=deviations,
                gathers=lambda pool: gather_results(pool, g, scan_rows, D), buffers=arena[:, NT * D:NT * D + NS * CE])
        front_step.done(groups)
        to_scalar.base += groups
        to_vector.base += groups
        edge_pass(y_tab, D, y_idx, cut_row, ALU.add, ALU.max)
        with nc.Block() as block:
            @block.gpsimd
            def _(pool):
                gather_results(pool, g, scan_rows, D)

            @block.vector
            def _(dve):
                with dve.Fori(0, groups) as i:
                    dve.wait_ge(group_here.sem, group_here.past(i + 1))
                    nc.vector.tensor_tensor(middle(x, i), middle(x, i), middle(g, i), ALU.add).then_inc(group_kept.sem, 1)

            @block.sync
            def _(sp):
                for i in range(groups):
                    sp.wait_ge(group_kept.sem, group_kept.past(i + 1))
                    j, full = i * NG, NG if i < groups - 1 else NG - 1
                    sp.dma_start(out[j * P:(j + full) * P, :].rearrange("(j p) d -> p j d", p=P), x[:, j:j + full, :]
                                 ).then_inc(stored.sem, 16)
                sp.dma_start(out[(NT - 1) * P:N, :], x[0:NL, NT - 1, :]).then_inc(stored.sem, 16)
                sp.wait_ge(stored.sem, stored.past(16 * (groups + 1)))


INPUTS = ["x", "src", "dst", "edge_type_4", "L0_gnn_W1l", "L0_gnn_b1", "L0_gnn_W1r", "L0_gnn_W2l", "L0_gnn_b2", "L0_gnn_W2r",
          "L1_gnn_W", "L1_gnn_att_src", "L1_gnn_att_dst", "L1_gnn_bias", "L1_gnn_bn1_w", "L1_gnn_bn1_b", "L1_gnn_W1",
          "L1_gnn_b1", "L1_gnn_W2", "L1_gnn_b2", "L1_gnn_bn2_w", "L1_gnn_bn2_b", "L2_gnn_W_src", "L2_gnn_W_dst",
          "L2_gnn_att_src", "L2_gnn_att_dst", "L2_gnn_bias", "L2_gnn_prelu_w", "L3_gnn_weight", "L3_gnn_bias"]


def kernel(**inputs):
    import concourse.bacc as bacc
    from concourse.bass_utils import run_bass_kernel_spmd

    nc = bacc.Bacc("TRN2", target_bir_lowering=False, num_devices=1)
    arrays, aps = {}, {}
    for name in INPUTS:
        arrays[f"in_{name}"] = np.ascontiguousarray(inputs[name])
        aps[name] = nc.dram_tensor(f"in_{name}", arrays[f"in_{name}"].shape, mybir.dt.from_np(arrays[f"in_{name}"].dtype),
                                   kind="ExternalInput").ap()
    out = nc.dram_tensor("out", [N, D], F32, kind="ExternalOutput").ap()
    build(nc, aps, out)
    return run_bass_kernel_spmd(nc, [arrays], core_ids=[0]).results[0]["out"]
```
